# Optimizing a Trainium2 kernel written in Bass

```python
import numpy as np
import jax
import jax.numpy as jnp

def _softmax(x, axis=-1):
    return jax.nn.softmax(x, axis=axis)

def _gelu(x):
    return jax.nn.gelu(x, approximate=True)

def _silu(x):
    return jax.nn.silu(x)

def _sigmoid(x):
    return jax.nn.sigmoid(x)

def _layernorm(x, axis=-1, eps=1e-05):
    m = jnp.mean(x, axis=axis, keepdims=True)
    v = jnp.var(x, axis=axis, keepdims=True)
    return (x - m) / jnp.sqrt(v + eps)

def _scatter_add(tgt, idx, src, axis=0):
    return tgt.at[idx].add(src)

def _segment_sum(src, seg, n):
    return jax.ops.segment_sum(src, seg, n)
kernel_name = 'mk_perceiver_d4_seqx_r4_455345'

def setup_inputs(seed: int=0):
    np.random.seed(seed)
    _w = jnp.asarray

    def _rec_inputs():
        import jax
        import jax.numpy as jnp
        _rk = jax.random.key(seed)
        x = 7.22e-05 + 1 * jax.random.normal(jax.random.fold_in(_rk, 1), (32, 32, 256), jnp.float32)
        _lenS = 32 - jax.random.randint(jax.random.fold_in(_rk, 7), (32,), 0, max(1, 32 // 4) + 1, jnp.int32)
        _lenS2 = 257 - jax.random.randint(jax.random.fold_in(_rk, 8), (32,), 0, max(1, 257 // 4) + 1, jnp.int32)
        _ctx_1024P = jax.random.normal(jax.random.fold_in(_rk, 11), (32, 16, 256), jnp.float32)
        _ctx_1024c = jax.random.dirichlet(jax.random.fold_in(_rk, 511), 0.3 * jnp.ones((16,), jnp.float32), (32, 257))
        _ctx_1024t = jnp.einsum('bsk,bkd->bsd', _ctx_1024c, _ctx_1024P)
        _ctx_1024t = _ctx_1024t * jax.lax.rsqrt(jnp.mean(jnp.square(_ctx_1024t)) + 1e-12) * 0.953939
        ctx_1024 = 4.13588e-05 + 0.999923 * (_ctx_1024t + 0.3 * jax.random.normal(jax.random.fold_in(_rk, 611), (32, 257, 256), jnp.float32))
        _validS = jnp.arange(32)[None, :] < _lenS[:, None]
        _validS2 = jnp.arange(257)[None, :] < _lenS2[:, None]
        _causal = jnp.tril(jnp.ones((32, 32), dtype=bool))
        mask_BxSxS_ik0 = jnp.where(jnp.broadcast_to(_validS[:, None, :], (32, 32, 32)), 0, 1).astype(jnp.int32)
        mask_BxS2_if0 = jnp.where(jnp.ones((32, 257), dtype=bool), 0, 1).astype(jnp.int32)
        return (x, ctx_1024, mask_BxSxS_ik0, mask_BxS2_if0)
    x, ctx_1024, mask_BxSxS_ik0, mask_BxS2_if0 = _rec_inputs()

    def _L0_xattn_setup():
        import jax, jax.numpy as jnp
        import numpy as np
        HEADS = 8
        DIM_HEAD = 64
        key = jax.random.key(seed)
        ks = jax.random.split(key, 9)
        B, N1, N2, D = (4, 512, 512, 256)
        inner = HEADS * DIM_HEAD
        s_in = 1.0 / np.sqrt(D)
        s_inner = 1.0 / np.sqrt(inner)
        return {'x1': jax.random.normal(ks[0], (B, N1, D), jnp.float32), 'x2': jax.random.normal(ks[1], (B, N2, D), jnp.float32), 'Wq1': jax.random.normal(ks[2], (D, inner), jnp.float32) * s_in, 'Wk1': jax.random.normal(ks[3], (D, inner), jnp.float32) * s_in, 'Wv1': jax.random.normal(ks[4], (D, inner), jnp.float32) * s_in, 'Wk2': jax.random.normal(ks[5], (D, inner), jnp.float32) * s_in, 'Wv2': jax.random.normal(ks[6], (D, inner), jnp.float32) * s_in, 'Wo': jax.random.normal(ks[7], (inner, D), jnp.float32) * s_inner, 'bo': jnp.zeros((D,), jnp.float32)}
    _L0_xattn_all = _L0_xattn_setup()
    _L0_xattn_in = {k: v for k, v in _L0_xattn_all.items() if k in ('Wq1', 'Wk1', 'Wv1', 'Wk2', 'Wv2', 'Wo', 'bo')}
    del _L0_xattn_all

    def _L0_attn_setup():
        import jax, jax.numpy as jnp
        import numpy as np
        import math
        E = 256
        H = 16
        B = 2
        T = 512

        def _rotary(x):
            D = x.shape[-1]
            inv_freq = 1.0 / 10000.0 ** (jnp.arange(0, D, 2, dtype=jnp.float32) / D)
            t = jnp.arange(x.shape[-2], dtype=jnp.float32)
            freqs = t[:, None] * inv_freq[None, :]
            emb = jnp.concatenate([freqs, freqs], axis=-1)
            cos = jnp.cos(emb)
            sin = jnp.sin(emb)
            x1 = x[..., ::2]
            x2 = x[..., 1::2]
            x_rot = jnp.stack([-x2, x1], axis=-1).reshape(x.shape)
            return x * cos + x_rot * sin
        key = jax.random.key(seed)
        ks = jax.random.split(key, 10)
        s = 0.02
        inp = {'x': jax.random.normal(ks[0], (B, T, E), dtype=jnp.float32), 'Wq': jax.random.normal(ks[1], (E, E), dtype=jnp.float32) * s, 'bq': jnp.zeros((E,), jnp.float32), 'Wk': jax.random.normal(ks[2], (E, E), dtype=jnp.float32) * s, 'bk': jnp.zeros((E,), jnp.float32), 'Wv': jax.random.normal(ks[3], (E, E), dtype=jnp.float32) * s, 'bv': jnp.zeros((E,), jnp.float32), 'Wg': jax.random.normal(ks[4], (E, E), dtype=jnp.float32) * s, 'bg': jnp.zeros((E,), jnp.float32), 'gamma': jax.random.normal(ks[5], (H,), dtype=jnp.float32)}
        return inp
    _L0_attn_all = _L0_attn_setup()
    _L0_attn_in = {k: v for k, v in _L0_attn_all.items() if k in ('Wq', 'bq', 'Wk', 'bk', 'Wv', 'bv', 'Wg', 'bg', 'gamma')}
    del _L0_attn_all

    def _L0_ffn_setup():
        import jax, jax.numpy as jnp
        import numpy as np
        H = 256
        E = 8
        TOP_K = 2
        FF = 4 * H
        B, S = (2, 512)

        def _moe_forward(x, gate_w, gate_b, w1, b1, w2, b2, sw1, sb1, sw2, sb2):
            b, s, h = x.shape
            xf = x.reshape(-1, h)
            scores = jax.nn.sigmoid(xf @ gate_w.T + gate_b)
            top_scores, top_idx = jax.lax.top_k(scores, TOP_K)
            top_scores = top_scores / (top_scores.sum(-1, keepdims=True) + 1e-06)
            comb = (jax.nn.one_hot(top_idx, E, dtype=xf.dtype) * top_scores[..., None]).sum(1)
            hdn = jax.nn.gelu(jnp.einsum('th,ehf->etf', xf, w1) + b1[:, None, :], approximate=False)
            y = jnp.einsum('etf,efh->eth', hdn, w2) + b2[:, None, :]
            routed = jnp.einsum('te,eth->th', comb, y)
            shared = (jax.nn.gelu(xf @ sw1 + sb1, approximate=False) @ sw2 + sb2) * 0.1
            return (routed + shared).reshape(b, s, h)
        key = jax.random.key(seed)
        ks = jax.random.split(key, 12)
        std = 0.02 / np.sqrt(H)
        return {'x': jax.random.normal(ks[0], (B, S, H), dtype=jnp.float32), 'gate_w': jax.random.normal(ks[1], (E, H), dtype=jnp.float32) * std, 'gate_b': jnp.zeros((E,), dtype=jnp.float32), 'w1': jax.random.normal(ks[2], (E, H, FF), dtype=jnp.float32) * (1.0 / np.sqrt(H)), 'b1': jnp.zeros((E, FF), dtype=jnp.float32), 'w2': jax.random.normal(ks[3], (E, FF, H), dtype=jnp.float32) * (1.0 / np.sqrt(FF)), 'b2': jnp.zeros((E, H), dtype=jnp.float32), 'sw1': jax.random.normal(ks[4], (H, FF), dtype=jnp.float32) * (1.0 / np.sqrt(H)), 'sb1': jnp.zeros((FF,), dtype=jnp.float32), 'sw2': jax.random.normal(ks[5], (FF, H), dtype=jnp.float32) * (1.0 / np.sqrt(FF)), 'sb2': jnp.zeros((H,), dtype=jnp.float32)}
    _L0_ffn_all = _L0_ffn_setup()
    _L0_ffn_in = {k: v for k, v in _L0_ffn_all.items() if k in ('gate_w', 'gate_b', 'w1', 'b1', 'w2', 'b2', 'sw1', 'sb1', 'sw2', 'sb2')}
    del _L0_ffn_all

    def _L1_xattn_setup():
        import jax, jax.numpy as jnp
        import numpy as np
        import math
        L, D, H, FF = (6, 256, 16, 1024)
        DH = D // H
        EPS = 1e-12

        def layer_norm(x, g, b):
            m = x.mean(-1, keepdims=True)
            v = ((x - m) ** 2).mean(-1, keepdims=True)
            return g * (x - m) / jnp.sqrt(v + EPS) + b

        def mha(xq, xkv, W, B, mask):

            def proj(x, w, b):
                y = x @ w + b
                bsz, n, _ = y.shape
                return y.reshape(bsz, n, H, DH).transpose(0, 2, 1, 3)
            q = proj(xq, W[0], B[0])
            k = proj(xkv, W[1], B[1])
            v = proj(xkv, W[2], B[2])
            score = jnp.einsum('bhqd,bhkd->bhqk', q, k) / math.sqrt(DH)
            if mask is not None:
                score = jnp.where(mask[:, None] == 0, -10000.0, score)
            attn = jax.nn.softmax(score, axis=-1)
            out = jnp.einsum('bhqk,bhkd->bhqd', attn, v)
            bsz = out.shape[0]
            out = out.transpose(0, 2, 1, 3).reshape(bsz, -1, D)
            return out @ W[3] + B[3]
        key = jax.random.key(seed)
        ks = jax.random.split(key, 8)
        Bsz, Nq, Nk = (8, 128, 128)
        trg = jax.random.normal(ks[0], (Bsz, Nq, D), jnp.float32)
        enc = jax.random.normal(ks[1], (Bsz, Nk, D), jnp.float32)
        mask = jax.random.randint(ks[2], (Bsz, Nq, Nq), 0, 2)
        s = D ** (-0.5)
        sa_w = jax.random.normal(ks[3], (L, 4, D, D), jnp.float32) * s
        sa_b = jnp.zeros((L, 4, D), jnp.float32)
        ca_w = jax.random.normal(ks[4], (L, 4, D, D), jnp.float32) * s
        ca_b = jnp.zeros((L, 4, D), jnp.float32)
        ln_g = jnp.ones((L, 3, D), jnp.float32)
        ln_b = jnp.zeros((L, 3, D), jnp.float32)
        w1 = jax.random.normal(ks[5], (L, D, FF), jnp.float32) * FF ** (-0.5)
        b1 = jnp.zeros((L, FF), jnp.float32)
        w2 = jax.random.normal(ks[6], (L, FF, D), jnp.float32) * s
        b2 = jnp.zeros((L, D), jnp.float32)
        return dict(trg=trg, enc=enc, mask=mask, sa_w=sa_w, sa_b=sa_b, ca_w=ca_w, ca_b=ca_b, ln_g=ln_g, ln_b=ln_b, w1=w1, b1=b1, w2=w2, b2=b2)
    _L1_xattn_all = _L1_xattn_setup()
    _L1_xattn_in = {k: v for k, v in _L1_xattn_all.items() if k in ('sa_w', 'sa_b', 'ca_w', 'ca_b', 'ln_g', 'ln_b', 'w1', 'b1', 'w2', 'b2')}
    del _L1_xattn_all

    def _L1_attn_setup():
        import math
        import jax, jax.numpy as jnp
        import numpy as np
        B, T, D, H = (4, 512, 256, 16)
        HD = D // H

        def apply_rope(x, base=10000.0):
            _, t, _, dh = x.shape
            half = dh // 2
            inv_freq = 1.0 / base ** (jnp.arange(half, dtype=jnp.float32) / float(half))
            pos = jnp.arange(t, dtype=jnp.float32)
            angles = pos[:, None] * inv_freq[None, :]
            sin = jnp.sin(angles)[None, :, None, :]
            cos = jnp.cos(angles)[None, :, None, :]
            x1 = x[..., :half]
            x2 = x[..., half:2 * half]
            rot1 = x1 * cos - x2 * sin
            rot2 = x1 * sin + x2 * cos
            return jnp.concatenate([rot1, rot2, x[..., 2 * half:]], axis=-1)
        key = jax.random.key(seed)
        k1, k2, k3 = jax.random.split(key, 3)
        x = jax.random.normal(k1, (B, T, D), dtype=jnp.float32)
        Wqkv = jax.random.normal(k2, (D, 3 * D), dtype=jnp.float32) / math.sqrt(D)
        Wo = jax.random.normal(k3, (D, D), dtype=jnp.float32) / math.sqrt(D)
        bo = jnp.zeros((D,), dtype=jnp.float32)
        return {'x': x, 'Wqkv': Wqkv, 'Wo': Wo, 'bo': bo}
    _L1_attn_all = _L1_attn_setup()
    _L1_attn_in = {k: v for k, v in _L1_attn_all.items() if k in ('Wqkv', 'Wo', 'bo')}
    del _L1_attn_all

    def _L1_ffn_setup():
        import jax, jax.numpy as jnp
        import numpy as np
        TOP_K = 2
        EPS = 1e-05

        def layer_norm(x, g, b):
            mu = jnp.mean(x, axis=-1, keepdims=True)
            var = jnp.mean(jnp.square(x - mu), axis=-1, keepdims=True)
            return (x - mu) * jax.lax.rsqrt(var + EPS) * g + b
        key = jax.random.key(seed)
        ks = jax.random.split(key, 12)
        B, S, D, F, E = (2, 512, 256, 1024, 8)
        std = 0.02
        return {'x': jax.random.normal(ks[0], (B, S, D), jnp.float32), 'g1': jnp.ones((D,), jnp.float32), 'be1': jnp.zeros((D,), jnp.float32), 'mix_w': jax.random.normal(ks[1], (D, D), jnp.float32) * std, 'mix_b': jnp.zeros((D,), jnp.float32), 'g2': jnp.ones((D,), jnp.float32), 'be2': jnp.zeros((D,), jnp.float32), 'router_w': jax.random.normal(ks[2], (D, E), jnp.float32) * std, 'w1': jax.random.normal(ks[3], (E, D, F), jnp.float32) * std, 'b1': jnp.zeros((E, F), jnp.float32), 'w2': jax.random.normal(ks[4], (E, F, D), jnp.float32) * std, 'b2': jnp.zeros((E, D), jnp.float32)}
    _L1_ffn_all = _L1_ffn_setup()
    _L1_ffn_in = {k: v for k, v in _L1_ffn_all.items() if k in ('g1', 'be1', 'mix_w', 'mix_b', 'g2', 'be2', 'router_w', 'w1', 'b1', 'w2', 'b2')}
    del _L1_ffn_all

    def _L2_xattn_setup():
        import jax, jax.numpy as jnp
        import numpy as np
        import math
        B, M, D, H, NK = (4, 512, 256, 16, 5)
        HD = D // H

        def _gather_pad0(x, idx):
            Bx, Hx, W, hd = x.shape
            valid = (idx >= 0) & (idx < W)
            idxc = jnp.clip(idx, 0, W - 1).reshape(Bx, Hx, -1)
            g = jnp.take_along_axis(x, idxc[..., None], axis=2)
            g = g.reshape(idx.shape + (hd,))
            return g * valid[..., None].astype(x.dtype)
        key = jax.random.key(seed)
        ks = jax.random.split(key, 9)
        w = lambda k, shape: jax.random.normal(k, shape, jnp.float32) * 0.02
        return {'k': jax.random.normal(ks[0], (B, M, D), jnp.float32), 'v': jax.random.normal(ks[1], (B, M, D), jnp.float32), 'q': jax.random.normal(ks[2], (B, M, D), jnp.float32), 'mask': jnp.zeros((B, M), jnp.int32), 'Wk': w(ks[3], (D, D)), 'bk': jnp.zeros((D,), jnp.float32), 'Wv': w(ks[4], (D, D)), 'bv': jnp.zeros((D,), jnp.float32), 'Wq': w(ks[5], (D, D)), 'bq': jnp.zeros((D,), jnp.float32), 'Woff': w(ks[6], (H * NK, D)), 'boff': jnp.zeros((H * NK,), jnp.float32), 'Wo': w(ks[7], (D, D)), 'bo': jnp.zeros((D,), jnp.float32)}
    _L2_xattn_all = _L2_xattn_setup()
    _L2_xattn_in = {k: v for k, v in _L2_xattn_all.items() if k in ('Wk', 'bk', 'Wv', 'bv', 'Wq', 'bq', 'Woff', 'boff', 'Wo', 'bo')}
    del _L2_xattn_all

    def _L2_attn_setup():
        import jax, jax.numpy as jnp
        import numpy as np
        import math
        D_MODEL = 256
        N_HEAD = 16
        D_HEAD = D_MODEL // N_HEAD
        D_KMAP = 128
        B, L = (4, 1024)

        def _fourier_kernel(x, proj_mat):
            p = jnp.einsum('blhd,dm->blhm', x, proj_mat) / math.sqrt(D_HEAD)
            return jnp.concatenate([jnp.cos(p), jnp.sin(p)], axis=-1) / math.sqrt(D_KMAP)
        key = jax.random.key(seed)
        ks = jax.random.split(key, 10)
        s = 1.0 / math.sqrt(D_MODEL)
        inp = {'x': jax.random.normal(ks[0], (B, L, D_MODEL), dtype=jnp.float32), 'proj_mat': jax.random.normal(ks[1], (D_HEAD, D_KMAP), dtype=jnp.float32), 'Wq': jax.random.uniform(ks[2], (D_MODEL, D_MODEL), minval=-s, maxval=s), 'bq': jax.random.uniform(ks[3], (D_MODEL,), minval=-s, maxval=s), 'Wk': jax.random.uniform(ks[4], (D_MODEL, D_MODEL), minval=-s, maxval=s), 'bk': jax.random.uniform(ks[5], (D_MODEL,), minval=-s, maxval=s), 'Wv': jax.random.uniform(ks[6], (D_MODEL, D_MODEL), minval=-s, maxval=s), 'bv': jax.random.uniform(ks[7], (D_MODEL,), minval=-s, maxval=s), 'Wo': jax.random.uniform(ks[8], (D_MODEL, D_MODEL), minval=-s, maxval=s), 'bo': jax.random.uniform(ks[9], (D_MODEL,), minval=-s, maxval=s)}
        return inp
    _L2_attn_all = _L2_attn_setup()
    _L2_attn_in = {k: v for k, v in _L2_attn_all.items() if k in ('proj_mat', 'Wq', 'bq', 'Wk', 'bk', 'Wv', 'bv', 'Wo', 'bo')}
    del _L2_attn_all

    def _L2_ffn_setup():
        import jax, jax.numpy as jnp
        import numpy as np
        DIM = 256
        HIDDEN = 768
        SCALE = 1.0 / 127.0

        def _dequant(w_int, dtype):
            return w_int.astype(dtype) * jnp.asarray(SCALE, dtype)
        key = jax.random.key(seed)
        k_x, k_g, k_u, k_d = jax.random.split(key, 4)
        x = jax.random.normal(k_x, (4, 512, DIM), dtype=jnp.float32)
        w_gate = jax.random.randint(k_g, (HIDDEN, DIM), -127, 128, dtype=jnp.int32)
        w_up = jax.random.randint(k_u, (HIDDEN, DIM), -127, 128, dtype=jnp.int32)
        w_down = jax.random.randint(k_d, (DIM, HIDDEN), -127, 128, dtype=jnp.int32)
        return {'x': x, 'w_gate': w_gate, 'w_up': w_up, 'w_down': w_down}
    _L2_ffn_all = _L2_ffn_setup()
    _L2_ffn_in = {k: v for k, v in _L2_ffn_all.items() if k in ('w_gate', 'w_up', 'w_down')}
    del _L2_ffn_all

    def _L3_xattn_setup():
        import jax, jax.numpy as jnp
        import numpy as np
        DIM = 256
        H = 16
        D = DIM // H
        SCALE = D ** (-0.5)
        LN_EPS = 1e-05

        def _layernorm(t, gamma, beta):
            mu = jnp.mean(t, axis=-1, keepdims=True)
            var = jnp.var(t, axis=-1, keepdims=True)
            return (t - mu) * jax.lax.rsqrt(var + LN_EPS) * gamma + beta
        key = jax.random.key(seed)
        ks = jax.random.split(key, 8)
        s = DIM ** (-0.5)
        return {'x': jax.random.normal(ks[0], (2, 512, DIM), dtype=jnp.float32), 'y': jax.random.normal(ks[1], (2, 512, DIM), dtype=jnp.float32), 'Wq': jax.random.normal(ks[2], (DIM, DIM), dtype=jnp.float32) * s, 'bq': jnp.zeros((DIM,), dtype=jnp.float32), 'Wkv': jax.random.normal(ks[3], (2 * DIM, DIM), dtype=jnp.float32) * s, 'bkv': jnp.zeros((2 * DIM,), dtype=jnp.float32), 'q_gamma': jnp.ones((D,), dtype=jnp.float32), 'q_beta': jnp.zeros((D,), dtype=jnp.float32), 'k_gamma': jnp.ones((D,), dtype=jnp.float32), 'k_beta': jnp.zeros((D,), dtype=jnp.float32), 'Wproj': jax.random.normal(ks[4], (DIM, DIM), dtype=jnp.float32) * s, 'bproj': jnp.zeros((DIM,), dtype=jnp.float32)}
    _L3_xattn_all = _L3_xattn_setup()
    _L3_xattn_in = {k: v for k, v in _L3_xattn_all.items() if k in ('Wq', 'bq', 'Wkv', 'bkv', 'q_gamma', 'q_beta', 'k_gamma', 'k_beta', 'Wproj', 'bproj')}
    del _L3_xattn_all

    def _L3_attn_setup():
        import jax, jax.numpy as jnp
        import numpy as np
        B, S, D_IN, D_HID, D_OUT, PE_DIM = (4, 1024, 256, 256, 256, 16)
        R_MIN, R_MAX = (0.9, 0.999)

        def _pos_emb(batch_size, seq_len, dim):
            positions = jnp.arange(seq_len)[:, None]
            div_term = jnp.exp(jnp.arange(0, dim, 2) * (-jnp.log(10000.0) / dim))
            pe = jnp.zeros((seq_len, dim))
            pe = pe.at[:, 0::2].set(jnp.sin(positions * div_term))
            pe = pe.at[:, 1::2].set(jnp.cos(positions * div_term))
            return jnp.broadcast_to(pe, (batch_size, seq_len, dim)) / 10
        key = jax.random.key(seed)
        ks = jax.random.split(key, 12)
        d_feat = D_IN + PE_DIM
        x = jax.random.normal(ks[0], (B, S, D_IN), dtype=jnp.float32)
        u = jax.random.uniform(ks[1], (D_HID,), minval=R_MIN, maxval=R_MAX)
        a_logit = jnp.log(u) - jnp.log1p(-u)
        sc = 0.02
        W_dx = jax.random.normal(ks[2], (d_feat, D_OUT), dtype=jnp.float32) * sc
        b_dx = jnp.zeros((D_OUT,), dtype=jnp.float32)
        W_x = jax.random.normal(ks[3], (d_feat, D_HID), dtype=jnp.float32) * sc
        b_x = jnp.zeros((D_HID,), dtype=jnp.float32)
        W_gx = jax.random.normal(ks[4], (D_HID, D_HID), dtype=jnp.float32) * sc
        b_gx = jnp.zeros((D_HID,), dtype=jnp.float32)
        W_ga = jax.random.normal(ks[5], (D_HID, D_HID), dtype=jnp.float32) * sc
        b_ga = jnp.zeros((D_HID,), dtype=jnp.float32)
        W_o = jax.random.normal(ks[6], (D_HID, D_OUT), dtype=jnp.float32) * sc
        b_o = jnp.zeros((D_OUT,), dtype=jnp.float32)
        return {'x': x, 'a_logit': a_logit, 'W_dx': W_dx, 'b_dx': b_dx, 'W_x': W_x, 'b_x': b_x, 'W_gx': W_gx, 'b_gx': b_gx, 'W_ga': W_ga, 'b_ga': b_ga, 'W_o': W_o, 'b_o': b_o}
    _L3_attn_all = _L3_attn_setup()
    _L3_attn_in = {k: v for k, v in _L3_attn_all.items() if k in ('a_logit', 'W_dx', 'b_dx', 'W_x', 'b_x', 'W_gx', 'b_gx', 'W_ga', 'b_ga', 'W_o', 'b_o')}
    del _L3_attn_all

    def _L3_ffn_setup():
        import jax, jax.numpy as jnp
        import numpy as np
        import math
        DIM = 256
        NUM_HEADS = 16
        SHARED_HEADS = 1
        ROUTED_HEADS = 3
        HEAD_DIM = DIM // NUM_HEADS
        B, N = (2, 512)
        key = jax.random.key(seed)
        ks = jax.random.split(key, 16)
        s = 1.0 / math.sqrt(DIM)
        inp = {'x': jax.random.normal(ks[0], (B, N, DIM), dtype=jnp.float32), 'Wq': jax.random.uniform(ks[1], (DIM, DIM), minval=-s, maxval=s), 'bq': jax.random.uniform(ks[2], (DIM,), minval=-s, maxval=s), 'Wk': jax.random.uniform(ks[3], (DIM, DIM), minval=-s, maxval=s), 'bk': jax.random.uniform(ks[4], (DIM,), minval=-s, maxval=s), 'Wv': jax.random.uniform(ks[5], (DIM, DIM), minval=-s, maxval=s), 'bv': jax.random.uniform(ks[6], (DIM,), minval=-s, maxval=s), 'Wp': jax.random.uniform(ks[7], (DIM, DIM), minval=-s, maxval=s), 'bp': jax.random.uniform(ks[8], (DIM,), minval=-s, maxval=s), 'Wr': jax.random.uniform(ks[9], (NUM_HEADS - SHARED_HEADS, DIM), minval=-s, maxval=s), 'br': jax.random.uniform(ks[10], (NUM_HEADS - SHARED_HEADS,), minval=-s, maxval=s), 'Ws': jax.random.uniform(ks[11], (2, DIM), minval=-s, maxval=s), 'bs': jax.random.uniform(ks[12], (2,), minval=-s, maxval=s), 'temperature': jnp.full((NUM_HEADS, 1, 1), float(np.log(np.expm1(1.0 / 0.24))), dtype=jnp.float32), 'query_embedding': 0.02 * jax.random.normal(ks[13], (NUM_HEADS, 1, HEAD_DIM), dtype=jnp.float32)}
        return inp
    _L3_ffn_all = _L3_ffn_setup()
    _L3_ffn_in = {k: v for k, v in _L3_ffn_all.items() if k in ('Wq', 'bq', 'Wk', 'bk', 'Wv', 'bv', 'Wp', 'bp', 'Wr', 'br', 'Ws', 'bs', 'temperature', 'query_embedding')}
    del _L3_ffn_all
    return {'x': x, 'ctx_1024': ctx_1024, 'mask_BxSxS_ik0': mask_BxSxS_ik0, 'mask_BxS2_if0': mask_BxS2_if0, 'L0_xattn_Wq1': _L0_xattn_in['Wq1'], 'L0_xattn_Wk1': _L0_xattn_in['Wk1'], 'L0_xattn_Wv1': _L0_xattn_in['Wv1'], 'L0_xattn_Wk2': _L0_xattn_in['Wk2'], 'L0_xattn_Wv2': _L0_xattn_in['Wv2'], 'L0_xattn_Wo': _L0_xattn_in['Wo'], 'L0_xattn_bo': _L0_xattn_in['bo'], 'L0_attn_Wq': _L0_attn_in['Wq'], 'L0_attn_bq': _L0_attn_in['bq'], 'L0_attn_Wk': _L0_attn_in['Wk'], 'L0_attn_bk': _L0_attn_in['bk'], 'L0_attn_Wv': _L0_attn_in['Wv'], 'L0_attn_bv': _L0_attn_in['bv'], 'L0_attn_Wg': _L0_attn_in['Wg'], 'L0_attn_bg': _L0_attn_in['bg'], 'L0_attn_gamma': _L0_attn_in['gamma'], 'L0_ffn_gate_w': _L0_ffn_in['gate_w'], 'L0_ffn_gate_b': _L0_ffn_in['gate_b'], 'L0_ffn_w1': _L0_ffn_in['w1'], 'L0_ffn_b1': _L0_ffn_in['b1'], 'L0_ffn_w2': _L0_ffn_in['w2'], 'L0_ffn_b2': _L0_ffn_in['b2'], 'L0_ffn_sw1': _L0_ffn_in['sw1'], 'L0_ffn_sb1': _L0_ffn_in['sb1'], 'L0_ffn_sw2': _L0_ffn_in['sw2'], 'L0_ffn_sb2': _L0_ffn_in['sb2'], 'L1_xattn_sa_w': _L1_xattn_in['sa_w'], 'L1_xattn_sa_b': _L1_xattn_in['sa_b'], 'L1_xattn_ca_w': _L1_xattn_in['ca_w'], 'L1_xattn_ca_b': _L1_xattn_in['ca_b'], 'L1_xattn_ln_g': _L1_xattn_in['ln_g'], 'L1_xattn_ln_b': _L1_xattn_in['ln_b'], 'L1_xattn_w1': _L1_xattn_in['w1'], 'L1_xattn_b1': _L1_xattn_in['b1'], 'L1_xattn_w2': _L1_xattn_in['w2'], 'L1_xattn_b2': _L1_xattn_in['b2'], 'L1_attn_Wqkv': _L1_attn_in['Wqkv'], 'L1_attn_Wo': _L1_attn_in['Wo'], 'L1_attn_bo': _L1_attn_in['bo'], 'L1_ffn_g1': _L1_ffn_in['g1'], 'L1_ffn_be1': _L1_ffn_in['be1'], 'L1_ffn_mix_w': _L1_ffn_in['mix_w'], 'L1_ffn_mix_b': _L1_ffn_in['mix_b'], 'L1_ffn_g2': _L1_ffn_in['g2'], 'L1_ffn_be2': _L1_ffn_in['be2'], 'L1_ffn_router_w': _L1_ffn_in['router_w'], 'L1_ffn_w1': _L1_ffn_in['w1'], 'L1_ffn_b1': _L1_ffn_in['b1'], 'L1_ffn_w2': _L1_ffn_in['w2'], 'L1_ffn_b2': _L1_ffn_in['b2'], 'L2_xattn_Wk': _L2_xattn_in['Wk'], 'L2_xattn_bk': _L2_xattn_in['bk'], 'L2_xattn_Wv': _L2_xattn_in['Wv'], 'L2_xattn_bv': _L2_xattn_in['bv'], 'L2_xattn_Wq': _L2_xattn_in['Wq'], 'L2_xattn_bq': _L2_xattn_in['bq'], 'L2_xattn_Woff': _L2_xattn_in['Woff'], 'L2_xattn_boff': _L2_xattn_in['boff'], 'L2_xattn_Wo': _L2_xattn_in['Wo'], 'L2_xattn_bo': _L2_xattn_in['bo'], 'L2_attn_proj_mat': _L2_attn_in['proj_mat'], 'L2_attn_Wq': _L2_attn_in['Wq'], 'L2_attn_bq': _L2_attn_in['bq'], 'L2_attn_Wk': _L2_attn_in['Wk'], 'L2_attn_bk': _L2_attn_in['bk'], 'L2_attn_Wv': _L2_attn_in['Wv'], 'L2_attn_bv': _L2_attn_in['bv'], 'L2_attn_Wo': _L2_attn_in['Wo'], 'L2_attn_bo': _L2_attn_in['bo'], 'L2_ffn_w_gate': _L2_ffn_in['w_gate'], 'L2_ffn_w_up': _L2_ffn_in['w_up'], 'L2_ffn_w_down': _L2_ffn_in['w_down'], 'L3_xattn_Wq': _L3_xattn_in['Wq'], 'L3_xattn_bq': _L3_xattn_in['bq'], 'L3_xattn_Wkv': _L3_xattn_in['Wkv'], 'L3_xattn_bkv': _L3_xattn_in['bkv'], 'L3_xattn_q_gamma': _L3_xattn_in['q_gamma'], 'L3_xattn_q_beta': _L3_xattn_in['q_beta'], 'L3_xattn_k_gamma': _L3_xattn_in['k_gamma'], 'L3_xattn_k_beta': _L3_xattn_in['k_beta'], 'L3_xattn_Wproj': _L3_xattn_in['Wproj'], 'L3_xattn_bproj': _L3_xattn_in['bproj'], 'L3_attn_a_logit': _L3_attn_in['a_logit'], 'L3_attn_W_dx': _L3_attn_in['W_dx'], 'L3_attn_b_dx': _L3_attn_in['b_dx'], 'L3_attn_W_x': _L3_attn_in['W_x'], 'L3_attn_b_x': _L3_attn_in['b_x'], 'L3_attn_W_gx': _L3_attn_in['W_gx'], 'L3_attn_b_gx': _L3_attn_in['b_gx'], 'L3_attn_W_ga': _L3_attn_in['W_ga'], 'L3_attn_b_ga': _L3_attn_in['b_ga'], 'L3_attn_W_o': _L3_attn_in['W_o'], 'L3_attn_b_o': _L3_attn_in['b_o'], 'L3_ffn_Wq': _L3_ffn_in['Wq'], 'L3_ffn_bq': _L3_ffn_in['bq'], 'L3_ffn_Wk': _L3_ffn_in['Wk'], 'L3_ffn_bk': _L3_ffn_in['bk'], 'L3_ffn_Wv': _L3_ffn_in['Wv'], 'L3_ffn_bv': _L3_ffn_in['bv'], 'L3_ffn_Wp': _L3_ffn_in['Wp'], 'L3_ffn_bp': _L3_ffn_in['bp'], 'L3_ffn_Wr': _L3_ffn_in['Wr'], 'L3_ffn_br': _L3_ffn_in['br'], 'L3_ffn_Ws': _L3_ffn_in['Ws'], 'L3_ffn_bs': _L3_ffn_in['bs'], 'L3_ffn_temperature': _L3_ffn_in['temperature'], 'L3_ffn_query_embedding': _L3_ffn_in['query_embedding']}

def reference(x, ctx_1024, mask_BxSxS_ik0, mask_BxS2_if0, L0_xattn_Wq1, L0_xattn_Wk1, L0_xattn_Wv1, L0_xattn_Wk2, L0_xattn_Wv2, L0_xattn_Wo, L0_xattn_bo, L0_attn_Wq, L0_attn_bq, L0_attn_Wk, L0_attn_bk, L0_attn_Wv, L0_attn_bv, L0_attn_Wg, L0_attn_bg, L0_attn_gamma, L0_ffn_gate_w, L0_ffn_gate_b, L0_ffn_w1, L0_ffn_b1, L0_ffn_w2, L0_ffn_b2, L0_ffn_sw1, L0_ffn_sb1, L0_ffn_sw2, L0_ffn_sb2, L1_xattn_sa_w, L1_xattn_sa_b, L1_xattn_ca_w, L1_xattn_ca_b, L1_xattn_ln_g, L1_xattn_ln_b, L1_xattn_w1, L1_xattn_b1, L1_xattn_w2, L1_xattn_b2, L1_attn_Wqkv, L1_attn_Wo, L1_attn_bo, L1_ffn_g1, L1_ffn_be1, L1_ffn_mix_w, L1_ffn_mix_b, L1_ffn_g2, L1_ffn_be2, L1_ffn_router_w, L1_ffn_w1, L1_ffn_b1, L1_ffn_w2, L1_ffn_b2, L2_xattn_Wk, L2_xattn_bk, L2_xattn_Wv, L2_xattn_bv, L2_xattn_Wq, L2_xattn_bq, L2_xattn_Woff, L2_xattn_boff, L2_xattn_Wo, L2_xattn_bo, L2_attn_proj_mat, L2_attn_Wq, L2_attn_bq, L2_attn_Wk, L2_attn_bk, L2_attn_Wv, L2_attn_bv, L2_attn_Wo, L2_attn_bo, L2_ffn_w_gate, L2_ffn_w_up, L2_ffn_w_down, L3_xattn_Wq, L3_xattn_bq, L3_xattn_Wkv, L3_xattn_bkv, L3_xattn_q_gamma, L3_xattn_q_beta, L3_xattn_k_gamma, L3_xattn_k_beta, L3_xattn_Wproj, L3_xattn_bproj, L3_attn_a_logit, L3_attn_W_dx, L3_attn_b_dx, L3_attn_W_x, L3_attn_b_x, L3_attn_W_gx, L3_attn_b_gx, L3_attn_W_ga, L3_attn_b_ga, L3_attn_W_o, L3_attn_b_o, L3_ffn_Wq, L3_ffn_bq, L3_ffn_Wk, L3_ffn_bk, L3_ffn_Wv, L3_ffn_bv, L3_ffn_Wp, L3_ffn_bp, L3_ffn_Wr, L3_ffn_br, L3_ffn_Ws, L3_ffn_bs, L3_ffn_temperature, L3_ffn_query_embedding):
    import jax
    import jax.numpy as jnp

    def _L0_xattn_ref(x1, x2, Wq1, Wk1, Wv1, Wk2, Wv2, Wo, bo):
        import jax, jax.numpy as jnp
        import numpy as np
        HEADS = 8
        DIM_HEAD = 64
        h, d = (HEADS, DIM_HEAD)
        scale = d ** (-0.5)
        B, N1, _ = x1.shape
        N2 = x2.shape[1]

        def split_heads(t, n):
            return t.reshape(B, n, h, d)
        q1 = split_heads(x1 @ Wq1, N1)
        k1 = split_heads(x1 @ Wk1, N1)
        v1 = split_heads(x1 @ Wv1, N1)
        k2 = split_heads(x2 @ Wk2, N2)
        v2 = split_heads(x2 @ Wv2, N2)
        k = jnp.concatenate([k1, k2], axis=1)
        v = jnp.concatenate([v1, v2], axis=1)
        sim = jnp.einsum('bihd,bjhd->bhij', q1.astype(jnp.float32), k.astype(jnp.float32)) * scale
        attn = jax.nn.softmax(sim, axis=-1)
        out = jnp.einsum('bhij,bjhd->bihd', attn, v)
        out = out.reshape(B, N1, h * d)
        return out @ Wo + bo

    def _L0_attn_ref(x, Wq, bq, Wk, bk, Wv, bv, Wg, bg, gamma):
        import jax, jax.numpy as jnp
        import numpy as np
        import math
        E = 256
        H = 16
        B = 2
        T = 512

        def _rotary(x):
            D = x.shape[-1]
            inv_freq = 1.0 / 10000.0 ** (jnp.arange(0, D, 2, dtype=jnp.float32) / D)
            t = jnp.arange(x.shape[-2], dtype=jnp.float32)
            freqs = t[:, None] * inv_freq[None, :]
            emb = jnp.concatenate([freqs, freqs], axis=-1)
            cos = jnp.cos(emb)
            sin = jnp.sin(emb)
            x1 = x[..., ::2]
            x2 = x[..., 1::2]
            x_rot = jnp.stack([-x2, x1], axis=-1).reshape(x.shape)
            return x * cos + x_rot * sin
        Bb, Tt, Ee = x.shape
        Hh = gamma.shape[0]
        Dd = Ee // Hh

        def proj(W, b):
            return (x @ W.T + b).reshape(Bb, Tt, Hh, Dd).transpose(0, 2, 1, 3)
        Q = _rotary(proj(Wq, bq))
        K = _rotary(proj(Wk, bk))
        V = proj(Wv, bv)
        g = jax.nn.sigmoid(gamma)
        idx = jnp.arange(Tt)
        diff = jnp.clip(idx[:, None] - idx[None, :], 0, None).astype(jnp.float32)
        t_w = jnp.exp(-g[:, None, None] * diff)
        scores = jnp.einsum('bhtd,bhsd->bhts', Q, K) / math.sqrt(Dd)
        out = jnp.einsum('bhts,bhsd->bhtd', scores * t_w[None], V)
        out = out.transpose(0, 2, 1, 3).reshape(Bb, Tt, Ee)
        gate = jax.nn.silu(x @ Wg.T + bg)
        return gate * out

    def _L0_ffn_ref(x, gate_w, gate_b, w1, b1, w2, b2, sw1, sb1, sw2, sb2):
        import jax, jax.numpy as jnp
        import numpy as np
        H = 256
        E = 8
        TOP_K = 2
        FF = 4 * H
        B, S = (2, 512)

        def _moe_forward(x, gate_w, gate_b, w1, b1, w2, b2, sw1, sb1, sw2, sb2):
            b, s, h = x.shape
            xf = x.reshape(-1, h)
            scores = jax.nn.sigmoid(xf @ gate_w.T + gate_b)
            top_scores, top_idx = jax.lax.top_k(scores, TOP_K)
            top_scores = top_scores / (top_scores.sum(-1, keepdims=True) + 1e-06)
            comb = (jax.nn.one_hot(top_idx, E, dtype=xf.dtype) * top_scores[..., None]).sum(1)
            hdn = jax.nn.gelu(jnp.einsum('th,ehf->etf', xf, w1) + b1[:, None, :], approximate=False)
            y = jnp.einsum('etf,efh->eth', hdn, w2) + b2[:, None, :]
            routed = jnp.einsum('te,eth->th', comb, y)
            shared = (jax.nn.gelu(xf @ sw1 + sb1, approximate=False) @ sw2 + sb2) * 0.1
            return (routed + shared).reshape(b, s, h)
        return _moe_forward(x, gate_w, gate_b, w1, b1, w2, b2, sw1, sb1, sw2, sb2)

    def _L1_xattn_ref(trg, enc, mask, sa_w, sa_b, ca_w, ca_b, ln_g, ln_b, w1, b1, w2, b2):
        import jax, jax.numpy as jnp
        import numpy as np
        import math
        L, D, H, FF = (6, 256, 16, 1024)
        DH = D // H
        EPS = 1e-12

        def layer_norm(x, g, b):
            m = x.mean(-1, keepdims=True)
            v = ((x - m) ** 2).mean(-1, keepdims=True)
            return g * (x - m) / jnp.sqrt(v + EPS) + b

        def mha(xq, xkv, W, B, mask):

            def proj(x, w, b):
                y = x @ w + b
                bsz, n, _ = y.shape
                return y.reshape(bsz, n, H, DH).transpose(0, 2, 1, 3)
            q = proj(xq, W[0], B[0])
            k = proj(xkv, W[1], B[1])
            v = proj(xkv, W[2], B[2])
            score = jnp.einsum('bhqd,bhkd->bhqk', q, k) / math.sqrt(DH)
            if mask is not None:
                score = jnp.where(mask[:, None] == 0, -10000.0, score)
            attn = jax.nn.softmax(score, axis=-1)
            out = jnp.einsum('bhqk,bhkd->bhqd', attn, v)
            bsz = out.shape[0]
            out = out.transpose(0, 2, 1, 3).reshape(bsz, -1, D)
            return out @ W[3] + B[3]

        def step(x, p):
            saw, sab, caw, cab, lg, lb, W1, B1, W2, B2 = p
            h = mha(x, x, saw, sab, mask)
            x = layer_norm(h + x, lg[0], lb[0])
            h = mha(x, enc, caw, cab, None)
            x = layer_norm(h + x, lg[1], lb[1])
            h = jax.nn.relu(x @ W1 + B1) @ W2 + B2
            x = layer_norm(h + x, lg[2], lb[2])
            return (x, None)
        out, _ = jax.lax.scan(step, trg, (sa_w, sa_b, ca_w, ca_b, ln_g, ln_b, w1, b1, w2, b2))
        return out

    def _L1_attn_ref(x, Wqkv, Wo, bo):
        import math
        import jax, jax.numpy as jnp
        import numpy as np
        B, T, D, H = (4, 512, 256, 16)
        HD = D // H

        def apply_rope(x, base=10000.0):
            _, t, _, dh = x.shape
            half = dh // 2
            inv_freq = 1.0 / base ** (jnp.arange(half, dtype=jnp.float32) / float(half))
            pos = jnp.arange(t, dtype=jnp.float32)
            angles = pos[:, None] * inv_freq[None, :]
            sin = jnp.sin(angles)[None, :, None, :]
            cos = jnp.cos(angles)[None, :, None, :]
            x1 = x[..., :half]
            x2 = x[..., half:2 * half]
            rot1 = x1 * cos - x2 * sin
            rot2 = x1 * sin + x2 * cos
            return jnp.concatenate([rot1, rot2, x[..., 2 * half:]], axis=-1)
        b, t, d = x.shape
        qkv = x @ Wqkv
        q, k, v = jnp.split(qkv, 3, axis=-1)
        q = q.reshape(b, t, H, HD)
        k = k.reshape(b, t, H, HD)
        v = v.reshape(b, t, H, HD)
        q = apply_rope(q)
        k = apply_rope(k)
        q = q / jnp.sqrt(jnp.sum(q * q, axis=-1, keepdims=True) + 1e-06)
        k = k / jnp.sqrt(jnp.sum(k * k, axis=-1, keepdims=True) + 1e-06)
        attn = jnp.einsum('bthd,bshd->bhts', q, k) / math.sqrt(HD)
        attn = jax.nn.softmax(attn, axis=-1)
        out = jnp.einsum('bhts,bshd->bthd', attn, v).reshape(b, t, d)
        return out @ Wo + bo

    def _L1_ffn_ref(x, g1, be1, mix_w, mix_b, g2, be2, router_w, w1, b1, w2, b2):
        import jax, jax.numpy as jnp
        import numpy as np
        TOP_K = 2
        EPS = 1e-05

        def layer_norm(x, g, b):
            mu = jnp.mean(x, axis=-1, keepdims=True)
            var = jnp.mean(jnp.square(x - mu), axis=-1, keepdims=True)
            return (x - mu) * jax.lax.rsqrt(var + EPS) * g + b
        res = x
        n = layer_norm(x, g1, be1)
        x = res + n + (n @ mix_w + mix_b)
        res = x
        n = layer_norm(x, g2, be2)
        B, S, D = n.shape
        E = w1.shape[0]
        flat = n.reshape(-1, D)
        probs = jax.nn.softmax(flat @ router_w, axis=-1)
        topw, topi = jax.lax.top_k(probs, TOP_K)
        combine = jnp.sum(jax.nn.one_hot(topi, E, dtype=flat.dtype) * topw[..., None], axis=1)
        h = jax.nn.silu(jnp.einsum('td,edf->tef', flat, w1) + b1)
        y = jnp.einsum('tef,efd->ted', h, w2) + b2
        out = jnp.einsum('te,ted->td', combine, y)
        return res + out.reshape(B, S, D)

    def _L2_xattn_ref(k, v, q, mask, Wk, bk, Wv, bv, Wq, bq, Woff, boff, Wo, bo):
        import jax, jax.numpy as jnp
        import numpy as np
        import math
        B, M, D, H, NK = (4, 512, 256, 16, 5)
        HD = D // H

        def _gather_pad0(x, idx):
            Bx, Hx, W, hd = x.shape
            valid = (idx >= 0) & (idx < W)
            idxc = jnp.clip(idx, 0, W - 1).reshape(Bx, Hx, -1)
            g = jnp.take_along_axis(x, idxc[..., None], axis=2)
            g = g.reshape(idx.shape + (hd,))
            return g * valid[..., None].astype(x.dtype)
        Bq, Q, _ = q.shape
        key_len = k.shape[1]
        K = jnp.einsum('bmd,ed->bme', k, Wk) + bk
        V = jnp.einsum('bmd,ed->bme', v, Wv) + bv
        Qp = jnp.einsum('bqd,ed->bqe', q, Wq) + bq
        off = jnp.einsum('bqd,ed->bqe', Qp, Woff) + boff
        off = off.reshape(Bq, Q, H, NK).transpose(0, 2, 1, 3)
        Kh = K.reshape(Bq, key_len, H, HD).transpose(0, 2, 1, 3)
        Vh = V.reshape(Bq, key_len, H, HD).transpose(0, 2, 1, 3)
        Qh = Qp.reshape(Bq, Q, H, HD).transpose(0, 2, 1, 3)
        loc = jnp.arange(Q, dtype=jnp.float32)[:, None]
        left = -NK // 2
        ref = jnp.arange(left, NK + left, dtype=jnp.float32)
        sign_lens = (1 - mask).sum(-1).astype(jnp.float32) - 1.0
        loc_x = jnp.mod(ref + off + loc, sign_lens[:, None, None, None])
        xg = loc_x / (key_len - 1) * 2.0 - 1.0
        ix = ((xg + 1.0) * key_len - 1.0) / 2.0
        x0 = jnp.floor(ix)
        dx = ix - x0
        i0 = x0.astype(jnp.int32)
        i1 = i0 + 1
        w0 = (1.0 - dx)[..., None]
        w1 = dx[..., None]
        sk = 0.5 * (w0 * _gather_pad0(Kh, i0) + w1 * _gather_pad0(Kh, i1))
        sv = 0.5 * (w0 * _gather_pad0(Vh, i0) + w1 * _gather_pad0(Vh, i1))
        scores = jnp.einsum('bhqd,bhqkd->bhqk', Qh / math.sqrt(HD), sk)
        attn = jax.nn.softmax(scores, axis=-1)
        ctx = jnp.einsum('bhqk,bhqkd->bhqd', attn, sv)
        ctx = ctx.transpose(0, 2, 1, 3).reshape(Bq, Q, H * HD)
        return jnp.einsum('bqd,ed->bqe', ctx, Wo) + bo

    def _L2_attn_ref(x, proj_mat, Wq, bq, Wk, bk, Wv, bv, Wo, bo):
        import jax, jax.numpy as jnp
        import numpy as np
        import math
        D_MODEL = 256
        N_HEAD = 16
        D_HEAD = D_MODEL // N_HEAD
        D_KMAP = 128
        B, L = (4, 1024)

        def _fourier_kernel(x, proj_mat):
            p = jnp.einsum('blhd,dm->blhm', x, proj_mat) / math.sqrt(D_HEAD)
            return jnp.concatenate([jnp.cos(p), jnp.sin(p)], axis=-1) / math.sqrt(D_KMAP)
        Bv, Lv, _ = x.shape
        q = (x @ Wq.T + bq).reshape(Bv, Lv, N_HEAD, D_HEAD)
        k = (x @ Wk.T + bk).reshape(Bv, Lv, N_HEAD, D_HEAD)
        v = (x @ Wv.T + bv).reshape(Bv, Lv, N_HEAD, D_HEAD)
        q_prime = _fourier_kernel(q, proj_mat)
        k_prime = _fourier_kernel(k, proj_mat)
        kv = jnp.einsum('blhm,blhd->bhmd', k_prime, v)
        out = jnp.einsum('blhm,bhmd->blhd', q_prime, kv)
        out = out.reshape(Bv, Lv, D_MODEL)
        return out @ Wo.T + bo

    def _L2_ffn_ref(x, w_gate, w_up, w_down):
        import jax, jax.numpy as jnp
        import numpy as np
        DIM = 256
        HIDDEN = 768
        SCALE = 1.0 / 127.0

        def _dequant(w_int, dtype):
            return w_int.astype(dtype) * jnp.asarray(SCALE, dtype)
        wg = _dequant(w_gate, x.dtype)
        wu = _dequant(w_up, x.dtype)
        wd = _dequant(w_down, x.dtype)
        gate = jnp.einsum('bsd,hd->bsh', x, wg)
        up = jnp.einsum('bsd,hd->bsh', x, wu)
        h = jax.nn.silu(gate) * up
        return jnp.einsum('bsh,dh->bsd', h, wd)

    def _L3_xattn_ref(x, y, Wq, bq, Wkv, bkv, q_gamma, q_beta, k_gamma, k_beta, Wproj, bproj):
        import jax, jax.numpy as jnp
        import numpy as np
        DIM = 256
        H = 16
        D = DIM // H
        SCALE = D ** (-0.5)
        LN_EPS = 1e-05

        def _layernorm(t, gamma, beta):
            mu = jnp.mean(t, axis=-1, keepdims=True)
            var = jnp.var(t, axis=-1, keepdims=True)
            return (t - mu) * jax.lax.rsqrt(var + LN_EPS) * gamma + beta
        B, N, C = x.shape
        M = y.shape[1]
        q = (x @ Wq.T + bq).reshape(B, N, H, D).transpose(0, 2, 1, 3)
        kv = (y @ Wkv.T + bkv).reshape(B, M, 2, H, D).transpose(2, 0, 3, 1, 4)
        k, v = (kv[0], kv[1])
        q = _layernorm(q, q_gamma, q_beta) * SCALE
        k = _layernorm(k, k_gamma, k_beta)
        attn = jax.nn.softmax(jnp.einsum('bhnd,bhmd->bhnm', q, k), axis=-1)
        out = jnp.einsum('bhnm,bhmd->bhnd', attn, v)
        out = out.transpose(0, 2, 1, 3).reshape(B, N, C)
        return out @ Wproj.T + bproj

    def _L3_attn_ref(x, a_logit, W_dx, b_dx, W_x, b_x, W_gx, b_gx, W_ga, b_ga, W_o, b_o):
        import jax, jax.numpy as jnp
        import numpy as np
        B, S, D_IN, D_HID, D_OUT, PE_DIM = (4, 1024, 256, 256, 256, 16)
        R_MIN, R_MAX = (0.9, 0.999)

        def _pos_emb(batch_size, seq_len, dim):
            positions = jnp.arange(seq_len)[:, None]
            div_term = jnp.exp(jnp.arange(0, dim, 2) * (-jnp.log(10000.0) / dim))
            pe = jnp.zeros((seq_len, dim))
            pe = pe.at[:, 0::2].set(jnp.sin(positions * div_term))
            pe = pe.at[:, 1::2].set(jnp.cos(positions * div_term))
            return jnp.broadcast_to(pe, (batch_size, seq_len, dim)) / 10
        batch_size, seq_len, _ = x.shape
        a_expit = jax.nn.sigmoid(a_logit)
        pe = _pos_emb(batch_size, seq_len, PE_DIM) / 10
        x = jnp.concatenate([x, pe], axis=-1)
        dx = x @ W_dx + b_dx
        xh = x @ W_x + b_x
        xh = jnp.sqrt(1 - a_expit ** 2) * xh
        gate_x = jax.nn.sigmoid(xh @ W_gx + b_gx)
        gate_a = jax.nn.sigmoid(xh @ W_ga + b_ga)
        a = gate_a * a_expit
        a_sq = a ** 2
        xg = gate_x * xh

        def step(h, inp):
            xi, ai, ai_sq = inp
            h = ai * h + jnp.sqrt(1 - ai_sq) * xi
            return (h, h)
        init = jnp.zeros((batch_size, xg.shape[-1]), dtype=xg.dtype)
        xs = (jnp.swapaxes(xg, 0, 1), jnp.swapaxes(a, 0, 1), jnp.swapaxes(a_sq, 0, 1))
        _, h = jax.lax.scan(step, init, xs)
        h = jnp.swapaxes(h, 0, 1)
        return (dx + h @ W_o + b_o) / 2

    def _L3_ffn_ref(x, Wq, bq, Wk, bk, Wv, bv, Wp, bp, Wr, br, Ws, bs, temperature, query_embedding):
        import jax, jax.numpy as jnp
        import numpy as np
        import math
        DIM = 256
        NUM_HEADS = 16
        SHARED_HEADS = 1
        ROUTED_HEADS = 3
        HEAD_DIM = DIM // NUM_HEADS
        B, N = (2, 512)
        Bsz, Nn, C = x.shape
        H, hd = (NUM_HEADS, HEAD_DIM)

        def heads(W, b):
            y = x @ W.T + b
            return y.reshape(Bsz, Nn, H, hd).transpose(0, 2, 1, 3)
        q = heads(Wq, bq)
        k = heads(Wk, bk)
        v = heads(Wv, bv)
        q_norm = q / jnp.linalg.norm(q, axis=-1, keepdims=True)
        q_scaled = (q_norm + query_embedding[None]) * jax.nn.softplus(temperature)[None]
        attn = jnp.einsum('bhqd,bhkd->bhqk', q_scaled, k) / math.sqrt(hd)
        attn = jax.nn.softmax(attn, axis=-1)
        h = jnp.einsum('bhqk,bhkd->bhqd', attn, v)
        h = h.transpose(0, 2, 1, 3).reshape(Bsz, Nn, C)
        gates = jax.nn.softmax(h @ Wr.T + br, axis=-1)
        _, idx = jax.lax.top_k(gates, ROUTED_HEADS)
        mask = jax.nn.one_hot(idx, H - SHARED_HEADS, dtype=gates.dtype).sum(axis=-2)
        routed_gates = gates * mask * ROUTED_HEADS
        sw = jax.nn.softmax(h @ Ws.T + bs, axis=-1)
        shared_gates = sw * SHARED_HEADS
        weight_0 = sw * 2.0
        shared_gates = weight_0[..., 0:1] * shared_gates
        routed_gates = weight_0[..., 1:2] * routed_gates
        masked_gates = jnp.concatenate([shared_gates, routed_gates], axis=-1)
        out = h * masked_gates.sum(axis=-1, keepdims=True)
        return out @ Wp.T + bp
    x = x + _L0_xattn_ref(_layernorm(x, axis=-1), ctx_1024, L0_xattn_Wq1, L0_xattn_Wk1, L0_xattn_Wv1, L0_xattn_Wk2, L0_xattn_Wv2, L0_xattn_Wo, L0_xattn_bo)
    x = x + _L0_attn_ref(_layernorm(x, axis=-1), L0_attn_Wq, L0_attn_bq, L0_attn_Wk, L0_attn_bk, L0_attn_Wv, L0_attn_bv, L0_attn_Wg, L0_attn_bg, L0_attn_gamma)
    x = x + _L0_ffn_ref(_layernorm(x, axis=-1), L0_ffn_gate_w, L0_ffn_gate_b, L0_ffn_w1, L0_ffn_b1, L0_ffn_w2, L0_ffn_b2, L0_ffn_sw1, L0_ffn_sb1, L0_ffn_sw2, L0_ffn_sb2)
    x = x + _L1_xattn_ref(_layernorm(x, axis=-1), ctx_1024, mask_BxSxS_ik0, L1_xattn_sa_w, L1_xattn_sa_b, L1_xattn_ca_w, L1_xattn_ca_b, L1_xattn_ln_g, L1_xattn_ln_b, L1_xattn_w1, L1_xattn_b1, L1_xattn_w2, L1_xattn_b2)
    x = x + _L1_attn_ref(_layernorm(x, axis=-1), L1_attn_Wqkv, L1_attn_Wo, L1_attn_bo)
    x = x + _L1_ffn_ref(_layernorm(x, axis=-1), L1_ffn_g1, L1_ffn_be1, L1_ffn_mix_w, L1_ffn_mix_b, L1_ffn_g2, L1_ffn_be2, L1_ffn_router_w, L1_ffn_w1, L1_ffn_b1, L1_ffn_w2, L1_ffn_b2)
    x = x + _L2_xattn_ref(ctx_1024, ctx_1024, _layernorm(x, axis=-1), mask_BxS2_if0, L2_xattn_Wk, L2_xattn_bk, L2_xattn_Wv, L2_xattn_bv, L2_xattn_Wq, L2_xattn_bq, L2_xattn_Woff, L2_xattn_boff, L2_xattn_Wo, L2_xattn_bo)
    x = x + _L2_attn_ref(_layernorm(x, axis=-1), L2_attn_proj_mat, L2_attn_Wq, L2_attn_bq, L2_attn_Wk, L2_attn_bk, L2_attn_Wv, L2_attn_bv, L2_attn_Wo, L2_attn_bo)
    x = x + _L2_ffn_ref(_layernorm(x, axis=-1), L2_ffn_w_gate, L2_ffn_w_up, L2_ffn_w_down)
    x = x + _L3_xattn_ref(_layernorm(x, axis=-1), ctx_1024, L3_xattn_Wq, L3_xattn_bq, L3_xattn_Wkv, L3_xattn_bkv, L3_xattn_q_gamma, L3_xattn_q_beta, L3_xattn_k_gamma, L3_xattn_k_beta, L3_xattn_Wproj, L3_xattn_bproj)
    x = x + _L3_attn_ref(_layernorm(x, axis=-1), L3_attn_a_logit, L3_attn_W_dx, L3_attn_b_dx, L3_attn_W_x, L3_attn_b_x, L3_attn_W_gx, L3_attn_b_gx, L3_attn_W_ga, L3_attn_b_ga, L3_attn_W_o, L3_attn_b_o)
    x = x + _L3_ffn_ref(_layernorm(x, axis=-1), L3_ffn_Wq, L3_ffn_bq, L3_ffn_Wk, L3_ffn_bk, L3_ffn_Wv, L3_ffn_bv, L3_ffn_Wp, L3_ffn_bp, L3_ffn_Wr, L3_ffn_br, L3_ffn_Ws, L3_ffn_bs, L3_ffn_temperature, L3_ffn_query_embedding)
    return x

_drawn_inputs = setup_inputs


def setup_inputs(seed=0):
    import zlib

    import numpy as np

    out = dict(_drawn_inputs(seed))
    spreads = {'L0_xattn_bo': (0.0, 0.1),
     'L0_attn_bq': (0.0, 0.397),
     'L0_attn_bk': (0.0, 0.388),
     'L0_attn_bv': (0.0, 0.1),
     'L0_attn_bg': (0.0, 0.1),
     'L0_ffn_gate_b': (0.0, 0.1),
     'L0_ffn_b1': (0.0, 0.1),
     'L0_ffn_b2': (0.0, 0.1),
     'L0_ffn_sb1': (0.0, 0.8),
     'L0_ffn_sb2': (0.0, 0.539),
     'L1_xattn_sa_b': (0.0, 0.1),
     'L1_xattn_ca_b': (0.0, 0.1),
     'L1_xattn_ln_g': (1.0, 0.2),
     'L1_xattn_ln_b': (0.0, 0.1),
     'L1_xattn_b1': (0.0, 0.1),
     'L1_xattn_b2': (0.0, 0.1),
     'L1_attn_bo': (0.0, 0.1),
     'L1_ffn_g1': (1.0, 0.2),
     'L1_ffn_be1': (0.0, 0.1),
     'L1_ffn_mix_b': (0.0, 0.1),
     'L1_ffn_g2': (1.0, 0.6),
     'L1_ffn_be2': (0.0, 0.8),
     'L1_ffn_b1': (0.0, 0.8),
     'L1_ffn_b2': (0.0, 0.8),
     'L2_xattn_bk': (0.0, 2.0),
     'L2_xattn_bv': (0.0, 0.8),
     'L2_xattn_bq': (0.0, 0.8),
     'L2_xattn_boff': (0.0, 0.8),
     'L2_xattn_bo': (0.0, 0.335),
     'L3_xattn_bq': (0.0, 2.0),
     'L3_xattn_bkv': (0.0, 2.0),
     'L3_xattn_q_gamma': (1.0, 0.6),
     'L3_xattn_q_beta': (0.0, 2.0),
     'L3_xattn_k_gamma': (1.0, 0.6),
     'L3_xattn_k_beta': (0.0, 2.0),
     'L3_xattn_bproj': (0.0, 2.0),
     'L3_attn_b_dx': (0.0, 2.0),
     'L3_attn_b_x': (0.0, 0.8),
     'L3_attn_b_gx': (0.0, 0.8),
     'L3_attn_b_ga': (0.0, 0.8),
     'L3_attn_b_o': (0.0, 2.0),
     'L3_ffn_temperature': (4.151041507720947, 0.6)}
    factors = {'L0_attn_gamma': 6.014,
     'L1_ffn_router_w': 5.122,
     'L1_ffn_w1': 6.361,
     'L1_ffn_w2': 5.758,
     'L2_xattn_Wk': 8.0,
     'L2_xattn_Wv': 4.534,
     'L2_xattn_Wq': 8.0,
     'L2_xattn_Woff': 8.0,
     'L2_xattn_Wo': 3.917,
     'L2_attn_bq': 7.521,
     'L2_attn_bk': 6.883,
     'L2_attn_bo': 7.682,
     'L3_xattn_Wq': 8.0,
     'L3_xattn_Wkv': 8.0,
     'L3_xattn_Wproj': 8.0,
     'L3_attn_a_logit': 8.0,
     'L3_attn_W_dx': 200.0,
     'L3_attn_W_x': 8.0,
     'L3_attn_W_gx': 8.0,
     'L3_attn_W_ga': 8.0,
     'L3_attn_W_o': 8.0,
     'L3_ffn_Wq': 8.0,
     'L3_ffn_bq': 63.729,
     'L3_ffn_Wk': 8.0,
     'L3_ffn_bk': 200.0,
     'L3_ffn_Wv': 8.0,
     'L3_ffn_bv': 44.886,
     'L3_ffn_Wp': 8.0,
     'L3_ffn_bp': 200.0,
     'L3_ffn_Wr': 200.0,
     'L3_ffn_br': 200.0,
     'L3_ffn_Ws': 8.0,
     'L3_ffn_bs': 200.0,
     'L3_ffn_query_embedding': 8.0}
    for name, (base, spread) in spreads.items():
        noise = np.random.default_rng([zlib.crc32(name.encode()), seed]).standard_normal(out[name].shape)
        drawn = base * np.exp(spread * noise) if base else spread * noise
        out[name] = jnp.asarray(drawn.astype(out[name].dtype))
    for name, factor in factors.items():
        out[name] = (out[name] * factor).astype(out[name].dtype)
    return out
```

```python
from contextlib import ExitStack

import numpy as np

import concourse.bass as bass
from concourse import mybir

F32 = mybir.dt.float32
I32 = mybir.dt.int32
ALU = mybir.AluOpType
ACT = mybir.ActivationFunctionType
AX = mybir.AxisListType

P = 128
NB = 32
LQ = 32
LK = 257
D = 256
DC = D // P
GB = P // LQ
NG = NB // GB
CT = GB * LK
VT = -(-CT // P)
FF = 1024
FC = FF // P
NE = 8
NL = 6
NK = 5
HID = 768



def constant_arrays():
    p = np.arange(P)
    f = np.float32
    inv = 1.0 / 10000.0 ** (np.arange(8) / 8.0)
    ang = (np.arange(LQ, dtype=f)[None, :] * inv.astype(f)[p % 8][:, None]).astype(f)
    rot_pairs = np.zeros((P, P), f)
    rot_halves = np.zeros((P, P), f)
    for o in range(P):
        if o % 2 == 0:
            rot_pairs[o + 1, o] = -1
        else:
            rot_pairs[o - 1, o] = 1
        if o % 16 < 8:
            rot_halves[o + 8, o] = -1
        else:
            rot_halves[o - 8, o] = 1
    div = np.exp(np.arange(0, 16, 2) * (-np.log(10000.0) / 16))
    pe = np.zeros((16, LQ))
    pe[0::2] = np.sin(np.arange(LQ)[None, :] * div[:, None])
    pe[1::2] = np.cos(np.arange(LQ)[None, :] * div[:, None])
    pe_rows = np.zeros((P, P), f)
    pe_rows[:16] = np.tile(pe / 100.0, (1, GB))
    return {
        "ident": np.eye(P, dtype=f),
        "head_ones": (p[:, None] // 16 == p[None, :] // 16).astype(f),
        "rot_pairs": rot_pairs,
        "rot_halves": rot_halves,
        "cos": np.cos(ang).astype(f),
        "sin": np.sin(ang).astype(f),
        "qmask16": (((p[:, None] // 16) % 4 == np.arange(4)) * 0.25).astype(f),
        "qmask64": (((p[:, None, None] // 64) + 2 * np.arange(2)[:, None] == np.arange(4)) * 0.125).astype(f).reshape(P, 8),
        "rowmask": (p[:, None] // LQ == np.arange(4)).astype(f),
        "pick": (p[:, None] % LQ == np.arange(LQ)).astype(f),
        "key_index": np.tile(np.arange(LK + 1, dtype=f), (P, 1)),
        "loc_base": ((p[:, None] % LQ) + np.arange(NK) - 3).astype(f),
        "lag": np.maximum(p[:, None] % LQ - np.arange(LQ), 0).astype(f),
        "same_seq": (p[:, None] // LQ == p[None, :] // LQ).astype(f),
        "pe": pe_rows,
        "minus_half": np.full((P, NG), -0.5, f),
        "half": np.full((P, NG), 0.5, f),
        "eps5": np.full((P, 1), 1e-5, f),
        "eps6": np.full((P, 1), 1e-6, f),
        "one": np.ones((P, 1), f),
        "zero": np.zeros((P, 1), f),
        "rank": np.tile((NE - np.arange(NE)).astype(f), (P, 1)),
        "centre": np.eye(P, dtype=f) - (p[:, None] // 16 == p[None, :] // 16).astype(f) / 16,
    }


CONST = constant_arrays()


def offsets(widths):
    at, out = 0, {}
    for name, w in widths:
        out[name] = (at, w)
        at += w
    return out, at


CONST_AT, CONST_W = offsets([(k, v.shape[1]) for k, v in CONST.items()])

COLS = [("L0_attn_bq", 2), ("L0_attn_bk", 2), ("L0_attn_bg", 2), 
        ("L2_xattn_bk", 2), ("L2_xattn_bq", 2), ("L2_attn_bq", 2), ("L2_attn_bk", 2),
        ("L3_xattn_bq", 2), ("L3_xattn_bkv", 4), ("L3_attn_a_logit", 2), ("L3_attn_b_x", 2), ("L3_attn_b_gx", 2),
        ("L3_attn_b_ga", 2), ("L3_ffn_bq", 2), ("L3_ffn_bk", 2), ("L3_ffn_query_embedding", 2), ("temperature", 2)]
COLS += [(f"sa_b{layer}", 8) for layer in range(NL)] + [(f"ca_b{layer}", 8) for layer in range(NL)]
COLS += [(f"L0_ffn_b1_{e}", 8) for e in range(NE)] + [("L0_ffn_sb1", 8)] + [(f"L1_ffn_b1_{e}", 8) for e in range(NE)]
COLS += [(f"L1_b1_{layer}", 8) for layer in range(NL)]
COLS += [("q_gamma", 1), ("q_beta", 1), ("k_gamma", 1), ("k_beta", 1)]
COL_AT, COL_W = offsets(COLS)
SMALL = [("L0_gate", 2 * NE), ("L1_router", 2 * NE), ("Woff", 2 * 80), ("Wrs", 2 * 17)]
SMALL_AT, SMALL_W = offsets(SMALL)
SHORT = [("boff", 80), ("gate_b", NE), ("brs", 17)]
SHORT_AT, SHORT_W = offsets(SHORT)
ROWS = ["L0_xattn_bo", "L0_attn_bv", "L0_ffn_sb2", "L1_attn_bo", "L1_ffn_g1", "L1_ffn_be1", "L1_ffn_mix_b", "L1_ffn_g2", "L1_ffn_be2",
        "L2_xattn_bv", "L2_xattn_bo", "L2_attn_bv", "L2_attn_bo", "L3_xattn_bv", "L3_xattn_bproj", "L3_attn_b_dx", "L3_attn_b_o",
        "L3_ffn_bv", "L3_ffn_bp"]
ROW = 5
WA, WB, WC = 6144, 4096, 2048


class Core:
    pass


def signals(st, nc, tag, names):
    made = {n: st.enter_context(nc.semaphore(f"{tag}_{n}")) for n in names.split()}
    return made, list(made.values())


def end_round(nc, handles):
    nums = sorted(h.num for h in handles)
    at = 0
    while at < len(nums):
        end = at
        while end + 1 < len(nums) and nums[end + 1] == nums[end] + 1:
            end += 1
        nc.gpsimd.sem_clear(range(nums[at], nums[end] + 1))
        at = end + 1
    nc.all_engine_barrier(sem_only=True)


def chain(eng, sem):
    count = [0]

    def link(ins):
        count[0] += 1
        ins.then_inc(sem, 1)
        eng.wait_ge(sem, count[0])
    return link


def bc(ap, shape):
    return ap.to_broadcast(shape)


def layer_norm(eng, link, v, s, n, out, x, stats):
    link(v.bn_stats(stats[:, 0:6], x))
    v.bn_aggr(stats[:, 6:8], stats[:, 0:6]).then_inc(s["var_ready"], 1)
    eng.wait_ge(s["power_ready"], n + 1)
    return v.tensor_scalar(out, x, stats[:, 6:7], stats[:, 8:9], ALU.subtract, ALU.mult)


def power(E, pool, s, n, out, x, add, exponent="minus_half"):
    pool.wait_ge(s["var_ready"], n + 1)
    E.nc.gpsimd.tensor_scalar(out, x, add, None, ALU.add).then_inc(s["added_eps"], 1)
    pool.wait_ge(s["added_eps"], n + 1)
    e = E.c(exponent)[:, 0:out.free_size()]
    if len(out.shape) == 3:
        e = e.unsqueeze(2)
    E.nc.gpsimd.tensor_tensor(out, out, e, ALU.pow).then_inc(s["power_ready"], 1)


def await_weights(E, name):
    sem, n = E.loads[name]
    E.nc.sync.wait_ge(sem, 16 * n)
    E.nc.sync.sem_clear(sem)
    E.nc.all_engine_barrier(sem_only=True)


def send_for(E, name, pairs):
    if name not in E.loads:
        E.loads[name] = (E.st.enter_context(E.nc.semaphore(f"{name}_weights")), len(pairs))
    for dst, src in pairs:
        E.nc.sync.dma_start(dst, src).then_inc(E.loads[name][0], 16)


def chunked(w):
    return w.rearrange("(c p) n -> p c n", p=P)


def fill(E, tag, pairs):
    nc = E.nc
    with ExitStack() as st:
        s, handles = signals(st, nc, tag + "_fill", "filled")
        with nc.Block(no_gpsimd_drain=True) as block:

            @block.vector
            def _(dve):
                for ap, value in pairs:
                    nc.vector.memset(ap, value).then_inc(s["filled"], 1)
                dve.wait_ge(s["filled"], len(pairs))
        end_round(nc, handles)


def cross_attention(E, tag, dh, wq, wk, wv, wo, rows, bq=None, bk=None, self_w=None, norm=None, deform=None,
                    source=None, finish="residual"):
    nc, ps = E.nc, E.ps
    M = (P * 2 // 64) if dh == 64 else 2
    F = 4 * dh
    U = GB if dh == 64 else 2 * GB
    SK = LQ if self_w else 0
    KS = LK + SK
    NCH = 4 if self_w else 3
    PW = NCH * P
    EXPS = 4 if self_w else 2
    ROUND = 2
    cm = "qmask64" if dh == 64 else "qmask16"
    src = E.x if source is None else source

    jobs = [("n", None, "act"), ("q", None, "dve")]
    if self_w:
        jobs += [("k1", None, "act"), ("v1", None, "dve")]
    if norm:
        jobs += [("qvar", None, "dve")]
    if deform:
        jobs += [("off", None, "dve")]
    for j in range(GB):
        jobs += [("K", (m, j), "act") for m in range(M)]
        jobs += [("V", i, "dve") for i in range(2 * j, 2 * j + 2 + (j == GB - 1))]
        if norm:
            jobs += [("kvar", (m, j), "dve") for m in range(M)]
    J = len(jobs)
    per = {e: sum(k[2] == e for k in jobs) for e in ("dve", "act")}

    def evacuated(n):
        e = jobs[n % J][2]
        return e, (n // J) * per[e] + sum(k[2] == e for k in jobs[:n % J + 1])

    where = {(k, a): i for i, (k, a, _) in enumerate(jobs)}

    with ExitStack() as st:
        s, handles = signals(st, nc, tag, "n_ready job_done evac_dve evac_act scores_done max_ready exp_done "
                             "transposed copied_dve copied_act pv_done heads_ready picked attn_copied y_ready x_done "
                             "ctx1 ctx0 dve_step act_step pool_step norm_sq loc_ready hats logs rstd_ready var_ready added_eps power_ready")

        def sb(name, shape):
            return st.enter_context(nc.sbuf_tensor(f"{tag}_{name}", shape, F32))

        n_sb = sb("n", [P, D])
        stats = sb("stats", [P, 9])
        nT = sb("nT", [P, DC, P])
        qT = sb("qT", [P, M, P])
        qblk = sb("qblk", [P, M, GB, 4, LQ])
        KT = sb("KT", [P, M, CT])
        V = sb("V", [P, VT, M * P])
        probs = sb("probs", [P, GB, 2, PW])
        pT = sb("pT", [P, 2, 2, NCH * P])
        negmax = sb("negmax", [P, 2, 2])
        sums = sb("sums", [P, 2, 2])
        own_sums = sb("own_sums", [P, 2, 2])
        rmask = sb("rmask", [P, 2, 4])
        heads = sb("heads", [P, 2, 2, F])
        attnT = sb("attnT", [P, M, P])
        ytmp = sb("ytmp", [P, D])
        if self_w:
            k1T = sb("k1T", [P, M, P])
            v1 = sb("v1", [P, M * P])
        if norm:
            sq = sb("sq", [P, 2, LK])
            rstd = sb("rstd", [P, 2, LK])
        if deform:
            qrep = sb("qrep", [P, DC, GB, 4, LQ])
            offb = sb("offb", [P, GB, 80])
            loc = sb("loc", [P, GB, 4, NK])
            t1 = sb("t1", [P, GB, 4, NK])
            t2 = sb("t2", [P, GB, 4, NK])
            S_sb = sb("S_sb", [P, 2, LK])
            hat = sb("hat", [P, 2, NK, LK + 1])
            prod = sb("prod", [P, LK])
            sc = sb("sc", [P, 2, 8])
            att = sb("att", [P, 2, 8])

        fill(E, tag, [(probs[:], 0.0)])

        with nc.Fori(0, NG // ROUND) as pair:
            g0 = pair * ROUND
            with nc.Block(no_gpsimd_drain=True) as block:

                @block.sync
                def _(sp):
                    sp.dma_start(E.ctx[:, 1], E.ctx_dram[bass.ds(g0 + 1, 1)].rearrange("a p c n -> (a p) c n")).then_inc(s["ctx1"], 16)
                    last_read = max(i for i, k in enumerate(jobs) if k[0] in ("K", "V"))
                    sp.wait_ge(s["job_done"], last_read + 1)
                    sp.dma_start(E.ctx[:, 0], E.ctx_dram[bass.ds(g0 + 2, 1)].rearrange("a p c n -> (a p) c n")).then_inc(s["ctx0"], 16)
                    sp.wait_ge(s["ctx0"], 16)

                def wait_evacuated(eng, n):
                    e, c = evacuated(n)
                    eng.wait_ge(s["evac_dve"] if e == "dve" else s["evac_act"], c)

                @block.tensor
                def _(pe):
                    mm, tr = nc.tensor.matmul, nc.tensor.transpose
                    for gi in range(ROUND):
                        cx = E.ctx[:, gi]
                        for i, (kind, arg, _e) in enumerate(jobs):
                            n = gi * J + i
                            o = ps[:, n % 4]
                            if n >= 4:
                                wait_evacuated(pe, n - 4)
                            if gi and i == 0:
                                pe.wait_ge(s["exp_done"], EXPS * gi * U)
                            if kind == "n":
                                pe.wait_ge(s["n_ready"], gi + 1)
                                for c in range(DC):
                                    last = tr(o[:, c * P:(c + 1) * P], n_sb[:, c * P:(c + 1) * P], E.c("ident"))
                            elif kind in ("q", "k1"):
                                wait_evacuated(pe, gi * J)
                                w = wq if kind == "q" else self_w[0]
                                for m in range(M):
                                    for c in range(DC):
                                        last = mm(o[:, m * P:(m + 1) * P], w[:, c, m * P:(m + 1) * P], nT[:, c], start=c == 0, stop=c == DC - 1)
                            elif kind == "v1":
                                for c in range(DC):
                                    last = mm(o[:, 0:M * P], nT[:, c], self_w[1][:, c], start=c == 0, stop=c == DC - 1)
                            elif kind == "qvar":
                                wait_evacuated(pe, gi * J + where["q", None])
                                last = mm(o[:, 0:M * P], E.c("head_ones"), ytmp[:], start=True, stop=True)
                            elif kind == "off":
                                wait_evacuated(pe, gi * J + where["q", None])
                                for j in range(GB):
                                    for c in range(DC):
                                        last = mm(o[:, j * 80:(j + 1) * 80],
                                                  qrep[:, c, j].rearrange("p a b -> p (a b)"),
                                                  E.small("Woff")[:, c], start=c == 0, stop=c == DC - 1)
                            elif kind == "K":
                                m, j = arg
                                if gi == 1 and (m, j) == (0, 0):
                                    pe.wait_ge(s["ctx1"], 16)
                                for c in range(DC):
                                    last = mm(o[:, 0:LK], wk[:, c, m * P:(m + 1) * P], cx[:, c, j * LK:(j + 1) * LK], start=c == 0, stop=c == DC - 1)
                            elif kind == "kvar":
                                pe.wait_ge(s["norm_sq"], gi * GB * M + arg[1] * M + arg[0] + 1)
                                last = mm(o[:, 0:LK], E.c("head_ones"), sq[:, arg[0] % 2], start=True, stop=True)
                            elif kind == "V":
                                w = min(P, CT - arg * P)
                                for c in range(DC):
                                    last = mm(o[0:w, 0:M * P], cx[:, c, arg * P:arg * P + w], wv[:, c], start=c == 0, stop=c == DC - 1)
                            last.then_inc(s["job_done"], 1)

                        def unit(u):
                            return (u // GB, u % GB) if dh == 16 else (None, u)

                        def scores(u):
                            cc, j = unit(u)
                            k = gi * U + u
                            if u < 2:
                                wait_evacuated(pe, gi * J + J - 1)
                                wait_evacuated(pe, gi * J + max(i for i in range(J) if jobs[i][2] == "act"))
                            else:
                                pe.wait_ge(s["exp_done"], EXPS * (k - 1))
                            for t in range(2):
                                o = ps[:, 2 * (k % 2) + t]
                                if dh == 16:
                                    h = slice(64 * t, 64 * t + 64)
                                    last = mm(o[:, 0:LK], qblk[h, cc, j].rearrange("p a b -> p (a b)"), KT[h, cc, j * LK:(j + 1) * LK], start=True, stop=True)
                                else:
                                    for i in range(2):
                                        c = 2 * t + i
                                        last = mm(o[:, 0:LK], qblk[:, c, j].rearrange("p a b -> p (a b)"), KT[:, c, j * LK:(j + 1) * LK], start=i == 0, stop=i == 1)
                                    for i in range(2):
                                        c = 2 * t + i
                                        last = mm(o[:, LK:KS], qblk[:, c, j].rearrange("p a b -> p (a b)"), k1T[:, c, j * LQ:(j + 1) * LQ], start=i == 0, stop=i == 1)
                            last.then_inc(s["scores_done"], 1)

                        def transposes(u):
                            _, j = unit(u)
                            k = gi * U + u
                            pe.wait_ge(s["exp_done"], EXPS * (k + 1))
                            if k:
                                pe.wait_ge(s["copied_dve"], k)
                                pe.wait_ge(s["copied_act"], k)
                            for t in range(2):
                                for c in range(NCH):
                                    last = tr(ps[:, 4 + t, c * P:(c + 1) * P], probs[:, j, t, c * P:(c + 1) * P], E.c("ident"))
                            last.then_inc(s["transposed"], 1)

                        def values(u):
                            cc, j = unit(u)
                            k = gi * U + u
                            pe.wait_ge(s["copied_dve"], k + 1)
                            pe.wait_ge(s["copied_act"], k + 1)
                            if k:
                                pe.wait_ge(s["heads_ready"], k)
                            if u == 0 and gi:
                                pe.wait_ge(s["x_done"], gi)
                            for t in range(2):
                                f = (2 * cc + t) * F if dh == 16 else t * F
                                o = ps[:, 6, t * F:(t + 1) * F]
                                for c in range(3):
                                    w = P if c < 2 else j + 1
                                    last = mm(o, pT[0:w, k % 2, t, c * P:(c + 1) * P], V[0:w, 2 * j + c, f:f + F], start=c == 0, stop=c == 2 and not self_w)
                                if self_w:
                                    last = mm(o, pT[:, k % 2, t, 3 * P:4 * P], v1[:, f:f + F], start=False, stop=True)
                            last.then_inc(s["pv_done"], 1)

                        def pick(u):
                            cc, j = unit(u)
                            k = gi * U + u
                            pe.wait_ge(s["heads_ready"], k + 1)
                            if u == 0 and gi:
                                pe.wait_ge(s["attn_copied"], gi)
                            for i in range(2 * F // P):
                                c = cc if dh == 16 else i
                                w = heads[:, k % 2].rearrange("p t f -> p (t f)")[:, i * P:(i + 1) * P]
                                last = mm(ps[:, 7, c * P + j * LQ:c * P + (j + 1) * LQ], w, E.c("pick"), start=True, stop=True)
                            last.then_inc(s["picked"], 1)

                        for k in range(U + 3):
                            if k < U:
                                scores(k)
                            if 0 <= k - 1 < U:
                                transposes(k - 1)
                            if 0 <= k - 2 < U:
                                values(k - 2)
                            if 0 <= k - 3 < U:
                                pick(k - 3)
                        pe.wait_ge(s["attn_copied"], gi + 1)
                        for c in range(M):
                            last = mm(ps[:, 6, 0:D], attnT[:, c], wo[:, c], start=c == 0, stop=c == M - 1)
                        last.then_inc(s["y_ready"], 1)

                @block.vector
                def _(dve):
                    v = nc.vector
                    link = chain(dve, s["dve_step"])

                    def block_diagonal(q):
                        for m in range(M):
                            mask = E.c(cm)[:, (m % 2) * 4:(m % 2) * 4 + 4] if dh == 64 else E.c(cm)
                            last = v.tensor_tensor(
                                qblk[:, m], q[:, m].rearrange("p (j q) -> p j q", j=GB).unsqueeze(2).to_broadcast([P, GB, 4, LQ]),
                                mask.unsqueeze(1).unsqueeze(3).to_broadcast([P, GB, 4, LQ]), ALU.mult)
                        return last

                    for gi in range(ROUND):
                        xg = src[:, bass.ds(g0 + gi, 1)].rearrange("p a d -> p (a d)")
                        if finish == "residual":
                            layer_norm(dve, link, v, s, gi, n_sb[:], xg, stats).then_inc(s["n_ready"], 1)
                        else:
                            v.tensor_copy(n_sb[:], xg).then_inc(s["n_ready"], 1)
                        for i, (kind, arg, e) in enumerate(jobs):
                            if e != "dve":
                                continue
                            n = gi * J + i
                            o = ps[:, n % 4]
                            dve.wait_ge(s["job_done"], n + 1)
                            if kind == "q":
                                q2 = qT[:].rearrange("p m t -> p (m t)")
                                if bq is None:
                                    link(v.tensor_copy(q2, o[:, 0:M * P]))
                                else:
                                    for m in range(M):
                                        last = v.tensor_scalar(qT[:, m], o[:, m * P:(m + 1) * P], bq[:, m:m + 1], None, ALU.add)
                                    link(last)
                                if norm:
                                    last = v.tensor_tensor(ytmp[:], q2, q2, ALU.mult)
                                else:
                                    if deform:
                                        for m in range(M):
                                            v.tensor_copy(qrep[:, m], qT[:, m].rearrange("p (j q) -> p j q", j=GB).unsqueeze(2).to_broadcast([P, GB, 4, LQ]))
                                    last = block_diagonal(qT)
                            elif kind == "qvar":
                                dve.wait_ge(s["rstd_ready"], gi * (1 + GB * M) + 1)
                                link(v.scalar_tensor_tensor(ytmp[:], qT[:].rearrange("p m t -> p (m t)"), norm[0], rstd[:, 0, 0:D], ALU.mult, ALU.mult))
                                link(v.tensor_scalar(qT[:].rearrange("p m t -> p (m t)"), ytmp[:], norm[1], None, ALU.add))
                                last = block_diagonal(qT)
                            elif kind == "kvar":
                                m, j = arg
                                kk = KT[:, m, j * LK:(j + 1) * LK]
                                dve.wait_ge(s["rstd_ready"], gi * (1 + GB * M) + 2 + j * M + m)
                                link(v.scalar_tensor_tensor(kk, kk, norm[2], rstd[:, m % 2], ALU.mult, ALU.mult))
                                last = v.tensor_scalar(kk, kk, norm[3], None, ALU.add)
                            elif kind == "off":
                                link(v.tensor_tensor(offb[:], o[:, 0:GB * 80].rearrange("p (j n) -> p j n", j=GB), deform["boff"].unsqueeze(1).to_broadcast([P, GB, 80]), ALU.add))
                                link(v.tensor_tensor(
                                    offb[:].rearrange("p j (t h k) -> p (j t) h k", t=4, h=4), offb[:].rearrange("p j (t h k) -> p (j t) h k", t=4, h=4),
                                    E.c("rowmask").unsqueeze(1).unsqueeze(3).to_broadcast([P, GB * 4, 4, NK]), ALU.mult))
                                link(v.tensor_reduce(loc[:].rearrange("p j t k -> p (j t) k"), offb[:].rearrange("p j (t h k) -> p (j t) k h", t=4, h=4), AX.X, ALU.add))
                                flat = loc[:].rearrange("p j t k -> p (j t) k")
                                link(v.tensor_tensor(flat, flat, E.c("loc_base").unsqueeze(1).to_broadcast([P, GB * 4, NK]), ALU.add))
                                flat3 = loc[:].rearrange("p j t k -> p j (t k)")
                                a3, b3 = t1[:].rearrange("p j t k -> p j (t k)"), t2[:].rearrange("p j t k -> p j (t k)")
                                length = deform["length"][:, bass.ds((g0 + gi) * GB, GB)].unsqueeze(2).to_broadcast([P, GB, 4 * NK])
                                inverse = deform["inverse"][:, bass.ds((g0 + gi) * GB, GB)].unsqueeze(2).to_broadcast([P, GB, 4 * NK])
                                link(v.tensor_tensor(a3, flat3, inverse, ALU.mult))
                                link(v.tensor_scalar(a3, a3, 12582912.0, None, ALU.add))
                                link(v.tensor_scalar(a3, a3, -12582912.0, None, ALU.add))
                                link(v.tensor_tensor(a3, a3, length, ALU.mult))
                                link(v.tensor_tensor(flat3, flat3, a3, ALU.subtract))
                                link(v.tensor_tensor(b3, flat3, length, ALU.mult))
                                link(v.tensor_scalar(b3, b3, 0.0, None, ALU.is_lt))
                                link(v.tensor_tensor(b3, b3, length, ALU.mult))
                                link(v.tensor_tensor(flat3, flat3, b3, ALU.add))
                                link(v.tensor_scalar(flat3, flat3, 2.0 / (LK - 1), -1.0, ALU.mult, ALU.add))
                                link(v.tensor_scalar(flat3, flat3, 1.0, float(LK), ALU.add, ALU.mult))
                                link(v.tensor_scalar(flat3, flat3, -1.0, -0.5, ALU.add, ALU.mult))
                                last = v.tensor_copy(t2[:], loc[:])
                            elif kind in ("V", "v1"):
                                w = min(P, CT - arg * P) if kind == "V" else P
                                dst = V[0:w, arg] if kind == "V" else v1[:]
                                if "bv" in rows:
                                    last = v.tensor_tensor(dst, o[0:w, 0:M * P], rows["bv"][0:w], ALU.add)
                                else:
                                    last = v.tensor_copy(dst, o[0:w, 0:M * P])
                            last.then_inc(s["evac_dve"], 1)

                        def head_sums(u):
                            k = gi * U + u
                            dve.wait_ge(s["exp_done"], EXPS * (k + 1))
                            if k:
                                dve.wait_ge(s["heads_ready"], k)
                            if deform:
                                link(v.tensor_copy(rmask[:], E.c("rowmask").unsqueeze(1).to_broadcast([P, 2, 4])))
                            else:
                                if self_w:
                                    link(v.tensor_tensor(sums[:, k % 2], sums[:, k % 2], own_sums[:, k % 2], ALU.add))
                                link(v.reciprocal(sums[:, k % 2], sums[:, k % 2]))
                                link(v.tensor_tensor(rmask[:], E.c("rowmask").unsqueeze(1).to_broadcast([P, 2, 4]),
                                                     sums[:, k % 2].unsqueeze(2).to_broadcast([P, 2, 4]), ALU.mult))
                            dve.wait_ge(s["pv_done"], k + 1)
                            if k >= 2:
                                dve.wait_ge(s["picked"], k - 1)
                            v.tensor_tensor(heads[:, k % 2].rearrange("p t (h d) -> p (t h) d", h=4),
                                            ps[:, 6, 0:2 * F].rearrange("p (a d) -> p a d", d=dh),
                                            rmask[:].rearrange("p t h -> p (t h)").unsqueeze(2).to_broadcast([P, 8, dh]), ALU.mult).then_inc(s["heads_ready"], 1)

                        def deformable(u):
                            cc, j = u // GB, u % GB
                            k = gi * U + u
                            dve.wait_ge(s["scores_done"], k + 1)
                            link(v.tensor_copy(S_sb[:], ps[:, 2 * (k % 2):2 * (k % 2) + 2, 0:LK]))
                            for t in range(2):
                                dve.wait_ge(s["hats"], 2 * k + t + 1)
                                for q in range(NK):
                                    link(v.scalar_tensor_tensor(prod[:], hat[:, t, q, 0:LK], 0.5, S_sb[:, t], ALU.mult, ALU.mult, accum_out=sc[:, t, q:q + 1]))
                            link(v.tensor_reduce(negmax[:, k % 2], sc[:, :, 0:NK], AX.X, ALU.max, negate=True))
                            link(v.tensor_tensor(att[:, :, 0:NK], sc[:, :, 0:NK], negmax[:, k % 2].unsqueeze(2).to_broadcast([P, 2, NK]), ALU.add))
                            v.tensor_copy(sc[:, :, 0:NK], att[:, :, 0:NK]).then_inc(s["max_ready"], 1)
                            dve.wait_ge(s["loc_ready"], k + 1)
                            link(v.tensor_reduce(sums[:, k % 2], att[:, :, 0:NK], AX.X, ALU.add))
                            link(v.reciprocal(sums[:, k % 2], sums[:, k % 2]))
                            link(v.tensor_scalar(sums[:, k % 2], sums[:, k % 2], 0.5, None, ALU.mult))
                            link(v.tensor_tensor(att[:, :, 0:NK], att[:, :, 0:NK], sums[:, k % 2].unsqueeze(2).to_broadcast([P, 2, NK]), ALU.mult))
                            if k >= GB:
                                dve.wait_ge(s["transposed"], k - GB + 1)
                            for t in range(2):
                                pr = probs[:, j, t, j:j + LK]
                                link(v.tensor_scalar(pr, hat[:, t, 0, 0:LK], att[:, t, 0:1], None, ALU.mult))
                                for q in range(1, NK):
                                    last = v.scalar_tensor_tensor(pr, hat[:, t, q, 0:LK], att[:, t, q:q + 1], pr, ALU.mult, ALU.add)
                                    if q < NK - 1:
                                        link(last)
                                last.then_inc(s["exp_done"], 1)

                        for k in range(U + 2):
                            if k < U:
                                if deform:
                                    deformable(k)
                                else:
                                    K = gi * U + k
                                    dve.wait_ge(s["scores_done"], K + 1)
                                    v.tensor_reduce(negmax[:, K % 2], ps[:, 2 * (K % 2):2 * (K % 2) + 2, 0:KS], AX.X, ALU.max, negate=True).then_inc(s["max_ready"], 1)
                            if 0 <= k - 1 < U:
                                K = gi * U + k - 1
                                dve.wait_ge(s["transposed"], K + 1)
                                if K >= 2:
                                    dve.wait_ge(s["pv_done"], K - 1)
                                v.tensor_copy(pT[:, K % 2, 1], ps[:, 5, 0:NCH * P]).then_inc(s["copied_dve"], 1)
                            if 0 <= k - 2 < U:
                                head_sums(k - 2)
                        dve.wait_ge(s["y_ready"], gi + 1)
                        xg = src[:, bass.ds(g0 + gi, 1)].rearrange("p a d -> p (a d)")
                        link(v.tensor_tensor(ytmp[:], ps[:, 6, 0:D], rows["bo"], ALU.add))
                        if finish == "residual":
                            v.tensor_tensor(xg, ytmp[:], xg, ALU.add).then_inc(s["x_done"], 1)
                        else:
                            link(v.tensor_tensor(ytmp[:], ytmp[:], n_sb[:], ALU.add))
                            link(layer_norm(dve, link, v, s, gi, ytmp[:], ytmp[:], stats))
                            link(v.tensor_tensor(ytmp[:], ytmp[:], rows["g"], ALU.mult))
                            v.tensor_tensor(xg, ytmp[:], rows["b"], ALU.add).then_inc(s["x_done"], 1)

                @block.gpsimd
                def _(pool):
                    for gi in range(ROUND):
                        power(E, pool, s, gi, stats[:, 8:9], stats[:, 7:8], 1e-5 if finish == "residual" else 1e-12)

                @block.scalar
                def _(act):
                    a = nc.scalar.activation
                    for gi in range(ROUND):
                        for i, (kind, arg, e) in enumerate(jobs):
                            n = gi * J + i
                            o = ps[:, n % 4]
                            if kind in ("qvar", "kvar"):
                                act.wait_ge(s["job_done"], n + 1)
                                r = rstd[:, 0, 0:D] if kind == "qvar" else rstd[:, arg[0] % 2]
                                k = gi * (1 + GB * M) + (0 if kind == "qvar" else 1 + arg[1] * M + arg[0])
                                if kind == "qvar" and gi:
                                    wait_evacuated(act, gi * J - 1)
                                a(r, o[:, 0:r.shape[1]], ACT.Ln, scale=1.0 / 16, bias=E.c("eps5")).then_inc(s["logs"], 1)
                                act.wait_ge(s["logs"], k + 1)
                                a(r, r, ACT.Exp, scale=-0.5).then_inc(s["rstd_ready"], 1)
                            if e != "act":
                                continue
                            act.wait_ge(s["job_done"], n + 1)
                            if kind == "n":
                                last = nc.scalar.copy(nT[:].rearrange("p c t -> p (c t)"), o[:, 0:D])
                            elif kind == "k1":
                                last = nc.scalar.copy(k1T[:].rearrange("p c t -> p (c t)"), o[:, 0:M * P])
                            else:
                                m, j = arg
                                if norm:
                                    jn = gi * GB * M + j * M + m
                                    if jn >= 2:
                                        wait_evacuated(act, gi * J + where["kvar", (m, j - 1)] if j else (gi - 1) * J + where["kvar", (m, GB - 1)])
                                    a(sq[:, m % 2], o[:, 0:LK], ACT.Square, bias=bk[:, m:m + 1]).then_inc(s["norm_sq"], 1)
                                if bk is None:
                                    last = nc.scalar.copy(KT[:, m, j * LK:(j + 1) * LK], o[:, 0:LK])
                                else:
                                    last = a(KT[:, m, j * LK:(j + 1) * LK], o[:, 0:LK], ACT.Identity, bias=bk[:, m:m + 1])
                            last.then_inc(s["evac_act"], 1)
                        for k in range(U + 1):
                            if k < U:
                                K = gi * U + k
                                j = k % GB
                                if deform:
                                    cc = k // GB
                                    if k == 0:
                                        wait_evacuated(act, gi * J + where["off", None])
                                    if K:
                                        act.wait_ge(s["exp_done"], 2 * K)
                                    for t in range(2):
                                        for q in range(NK):
                                            a(hat[:, t, q, 0:LK], E.c("key_index")[:, 0:LK], ACT.Abs, bias=t2[:, j, 2 * cc + t, q:q + 1]).then_inc(s["act_step"], 1)
                                        act.wait_ge(s["act_step"], NK * (2 * K + t + 1))
                                        a(hat[:, t, :, 0:LK], hat[:, t, :, 0:LK], ACT.Relu, bias=E.c("one"), scale=-1.0).then_inc(s["hats"], 1)
                                    act.wait_ge(s["max_ready"], K + 1)
                                    a(att[:, :, 0:NK], sc[:, :, 0:NK], ACT.Exp).then_inc(s["loc_ready"], 1)
                                else:
                                    act.wait_ge(s["max_ready"], K + 1)
                                    if K >= GB:
                                        act.wait_ge(s["transposed"], K - GB + 1)
                                    if K >= 2:
                                        act.wait_ge(s["heads_ready"], K - 1)
                                    for t in range(2):
                                        a(probs[:, j, t, j:j + LK], ps[:, 2 * (K % 2) + t, 0:LK], ACT.Exp,
                                          bias=negmax[:, K % 2, t:t + 1], accum_out=sums[:, K % 2, t:t + 1]).then_inc(s["exp_done"], 1)
                                        if self_w:
                                            a(probs[:, j, t, 3 * P + LQ * j:3 * P + LQ * (j + 1)], ps[:, 2 * (K % 2) + t, LK:KS], ACT.Exp,
                                              bias=negmax[:, K % 2, t:t + 1], accum_out=own_sums[:, K % 2, t:t + 1]).then_inc(s["exp_done"], 1)
                            if 0 <= k - 1 < U:
                                K = gi * U + k - 1
                                act.wait_ge(s["transposed"], K + 1)
                                if K >= 2:
                                    act.wait_ge(s["pv_done"], K - 1)
                                nc.scalar.copy(pT[:, K % 2, 0], ps[:, 4, 0:NCH * P]).then_inc(s["copied_act"], 1)
                        act.wait_ge(s["picked"], (gi + 1) * U)
                        nc.scalar.copy(attnT[:].rearrange("p c t -> p (c t)"), ps[:, 7, 0:M * P]).then_inc(s["attn_copied"], 1)

            end_round(nc, handles)


def self_attention(E, tag, w, rows, bq=None, bk=None, rope=None, unit_norm=False, query_scale=None, mask=False,
                   decay=None, gate_bias=None, heads_gate=None, source=None, finish="residual"):
    nc, ps = E.nc, E.ps
    ROUND = 2
    wq, wk, wv, wo = w
    src = E.x if source is None else source
    with ExitStack() as st:
        s, handles = signals(st, nc, tag, "n_ready nT_psum nT_ready qk_psum qk_sb v_psum v_ready gate_ready rot_psum squared norm_psum "
                             "qblk_ready scores_done shifted exp_done probs_ready transposed pT_ready pv_done heads_ready "
                             "picked attn_ready y_ready dve_step logs rstd_ready var_ready added_eps power_ready")

        def sb(name, shape):
            return st.enter_context(nc.sbuf_tensor(f"{tag}_{name}", [P, ROUND] + shape, F32))

        n_sb, stats, nT = sb("n", [D]), sb("stats", [9]), sb("nT", [DC, P])
        qk, v_sb, qblk = sb("qk", [4, P]), sb("v", [D]), sb("qblk", [DC, GB, 4, LQ])
        probs, pT = sb("probs", [16, LQ]), sb("pT", [4, P])
        tmp, big = sb("tmp", [4, P]), sb("sums", [16])
        rmask, heads, attnT, ytmp = sb("rmask", [16, 4]), sb("heads", [GB, 4, 64]), sb("attnT", [DC, P]), sb("ytmp", [D])
        gate = sb("gate", [DC, P])
        rsum = sb("rsum", [16])
        top = sb("top", [32])
        norm_cols = 512 if unit_norm else 256

        with nc.Fori(0, NG // ROUND) as pair:
            g0 = pair * ROUND
            with nc.Block(no_gpsimd_drain=True) as block:

                @block.tensor
                def _(pe):
                    mm, tr = nc.tensor.matmul, nc.tensor.transpose
                    for gi in range(ROUND):
                        pe.wait_ge(s["n_ready"], gi + 1)
                        for c in range(DC):
                            last = tr(ps[:, 4 * gi, c * P:(c + 1) * P], n_sb[:, gi, c * P:(c + 1) * P], E.c("ident"))
                        last.then_inc(s["nT_psum"], 1)
                    for gi in range(ROUND):
                        pe.wait_ge(s["nT_ready"], gi + 1)
                        for i, wi in enumerate((wq, wk)):
                            for m in range(DC):
                                for c in range(DC):
                                    last = mm(ps[:, 4 * gi, (2 * i + m) * P:(2 * i + m + 1) * P], wi[:, c, m * P:(m + 1) * P], nT[:, gi, c], start=c == 0, stop=c == DC - 1)
                        last.then_inc(s["qk_psum"], 1)
                        for c in range(DC):
                            last = mm(ps[:, 4 * gi + 1, 0:D], nT[:, gi, c], wv[:, c], start=c == 0, stop=c == DC - 1)
                        if gate_bias is not None:
                            for m in range(DC):
                                for c in range(DC):
                                    last = mm(ps[:, 4 * gi + 3, m * P:(m + 1) * P], wo[:, c, m * P:(m + 1) * P], nT[:, gi, c], start=c == 0, stop=c == DC - 1)
                        last.then_inc(s["v_psum"], 1)
                    if rope:
                        for gi in range(ROUND):
                            pe.wait_ge(s["qk_sb"], gi + 1)
                            mm(ps[:, 4 * gi + 2], E.c(rope), qk[:, gi].rearrange("p a b -> p (a b)"), start=True, stop=True).then_inc(s["rot_psum"], 1)
                    if unit_norm or query_scale:
                        for gi in range(ROUND):
                            pe.wait_ge(s["squared"], gi + 1)
                            mm(ps[:, 4 * gi + 3, 0:norm_cols], E.c("head_ones"), tmp[:, gi].rearrange("p a b -> p (a b)")[:, 0:norm_cols], start=True, stop=True).then_inc(s["norm_psum"], 1)
                    for gi in range(ROUND):
                        pe.wait_ge(s["qblk_ready"], gi + 1)
                        if gate_bias is not None:
                            pe.wait_ge(s["gate_ready"], gi + 1)
                        for half in range(2):
                            for c in range(DC):
                                for j in range(GB):
                                    h = slice(64 * half, 64 * half + 64)
                                    at = (c * GB + j) * LQ
                                    last = mm(ps[:, 4 * gi + 2 + half, at:at + LQ], qblk[h, gi, c, j].rearrange("p a b -> p (a b)"),
                                              qk[h, gi, 2 + c, j * LQ:(j + 1) * LQ], start=True, stop=True)
                        last.then_inc(s["scores_done"], 1)
                    for gi in range(ROUND):
                        pe.wait_ge(s["exp_done"] if decay is None else s["probs_ready"], gi + 1)
                        for t in range(4):
                            last = tr(ps[:, 4 * gi, t * P:(t + 1) * P], probs[:, gi, t * GB:(t + 1) * GB].rearrange("p a b -> p (a b)"), E.c("ident"))
                        last.then_inc(s["transposed"], 1)
                    for gi in range(ROUND):
                        pe.wait_ge(s["pT_ready"], gi + 1)
                        pe.wait_ge(s["v_ready"], gi + 1)
                        for j in range(GB):
                            h = slice(LQ * j, LQ * j + LQ)
                            for half in range(2):
                                for c in range(DC):
                                    f = slice((2 * c + half) * 64, (2 * c + half + 1) * 64)
                                    last = mm(ps[:, 4 * gi + j, f], pT[h, gi, half * DC + c], v_sb[h, gi, f], start=True, stop=True)
                        last.then_inc(s["pv_done"], 1)
                    for gi in range(ROUND):
                        pe.wait_ge(s["heads_ready"], gi + 1)
                        for j in range(GB):
                            for c in range(DC):
                                at = c * P + j * LQ
                                last = mm(ps[:, 4 * gi + 1, at:at + LQ], heads[:, gi, j, 2 * c:2 * c + 2].rearrange("p a b -> p (a b)"), E.c("pick"), start=True, stop=True)
                        last.then_inc(s["picked"], 1)
                    for gi in range(ROUND):
                        pe.wait_ge(s["attn_ready"], gi + 1)
                        if gate_bias is not None:
                            for c in range(DC):
                                last = tr(ps[:, 4 * gi, c * P:(c + 1) * P], attnT[:, gi, c], E.c("ident"))
                        else:
                            for c in range(DC):
                                last = mm(ps[:, 4 * gi, 0:D], attnT[:, gi, c], wo[:, c], start=c == 0, stop=c == DC - 1)
                            if heads_gate:
                                for c in range(DC):
                                    last = mm(ps[:, 4 * gi, D:D + 17], attnT[:, gi, c], E.small("Wrs")[:, c], start=c == 0, stop=c == DC - 1)
                        last.then_inc(s["y_ready"], 1)

                @block.vector
                def _(dve):
                    v = nc.vector
                    link = chain(dve, s["dve_step"])
                    for gi in range(ROUND):
                        xg = src[:, bass.ds(g0 + gi, 1)].rearrange("p a d -> p (a d)")
                        if finish == "residual":
                            layer_norm(dve, link, v, s, gi, n_sb[:, gi], xg, stats[:, gi]).then_inc(s["n_ready"], 1)
                        else:
                            v.tensor_copy(n_sb[:, gi], xg).then_inc(s["n_ready"], 1)
                    for gi in range(ROUND):
                        dve.wait_ge(s["v_psum"], gi + 1)
                        if "bv" in rows:
                            v.tensor_tensor(v_sb[:, gi], ps[:, 4 * gi + 1, 0:D], rows["bv"], ALU.add).then_inc(s["v_ready"], 1)
                        else:
                            v.tensor_copy(v_sb[:, gi], ps[:, 4 * gi + 1, 0:D]).then_inc(s["v_ready"], 1)
                    if rope:
                        for gi in range(ROUND):
                            q4 = qk[:, gi].rearrange("p a (j q) -> p (a j) q", j=GB)
                            t4 = tmp[:, gi].rearrange("p a (j q) -> p (a j) q", j=GB)
                            dve.wait_ge(s["rot_psum"], gi + 1)
                            link(v.tensor_tensor(t4, ps[:, 4 * gi + 2].rearrange("p (a q) -> p a q", q=LQ), E.c("sin").unsqueeze(1).to_broadcast([P, 16, LQ]), ALU.mult))
                            link(v.tensor_tensor(q4, q4, E.c("cos").unsqueeze(1).to_broadcast([P, 16, LQ]), ALU.mult))
                            link(v.tensor_tensor(q4, q4, t4, ALU.add))
                    if unit_norm or query_scale:
                        for gi in range(ROUND):
                            if not rope:
                                dve.wait_ge(s["qk_sb"], gi + 1)
                            q2 = qk[:, gi].rearrange("p a b -> p (a b)")[:, 0:norm_cols]
                            v.tensor_tensor(tmp[:, gi].rearrange("p a b -> p (a b)")[:, 0:norm_cols], q2, q2, ALU.mult).then_inc(s["squared"], 1)
                        for gi in range(ROUND):
                            q2 = qk[:, gi].rearrange("p a b -> p (a b)")[:, 0:norm_cols]
                            t2 = tmp[:, gi].rearrange("p a b -> p (a b)")[:, 0:norm_cols]
                            dve.wait_ge(s["norm_psum"], gi + 1)
                            dve.wait_ge(s["rstd_ready"], gi + 1)
                            link(v.tensor_tensor(q2, q2, t2, ALU.mult))
                            if query_scale:
                                for m in range(DC):
                                    link(v.tensor_scalar(qk[:, gi, m], qk[:, gi, m], query_scale[0][:, m:m + 1], query_scale[1][:, m:m + 1], ALU.add, ALU.mult))
                    for gi in range(ROUND):
                        if not (rope or unit_norm or query_scale):
                            dve.wait_ge(s["qk_sb"], gi + 1)
                        for m in range(DC):
                            last = v.tensor_tensor(qblk[:, gi, m], qk[:, gi, m].rearrange("p (j q) -> p j q", j=GB).unsqueeze(2).to_broadcast([P, GB, 4, LQ]),
                                                   E.c("qmask16").unsqueeze(1).unsqueeze(3).to_broadcast([P, GB, 4, LQ]), ALU.mult)
                        last.then_inc(s["qblk_ready"], 1)
                    for gi in range(ROUND):
                        dve.wait_ge(s["scores_done"], gi + 1)
                        S = ps[:, 4 * gi + 2:4 * gi + 4, 0:D].rearrange("p b (a k) -> p b a k", k=LQ)
                        pr = probs[:, gi].rearrange("p (b a) k -> p b a k", b=2)
                        if decay is not None:
                            for half in range(2):
                                for c in range(DC):
                                    last = v.tensor_tensor(pr[:, half, c * GB:(c + 1) * GB], S[:, half, c * GB:(c + 1) * GB],
                                                           decay[:, 2 * c + half].unsqueeze(1).to_broadcast([P, GB, LQ]), ALU.mult)
                            last.then_inc(s["probs_ready"], 1)
                            continue
                        if mask:
                            for half in range(2):
                                for c in range(DC):
                                    last = v.tensor_tensor(pr[:, half, c * GB:(c + 1) * GB], S[:, half, c * GB:(c + 1) * GB], E.keep[:, bass.ds((g0 + gi) * GB, GB)], ALU.mult)
                            link(last)
                            for half in range(2):
                                for c in range(DC):
                                    last = v.tensor_tensor(pr[:, half, c * GB:(c + 1) * GB], pr[:, half, c * GB:(c + 1) * GB], E.floor[:, bass.ds((g0 + gi) * GB, GB)], ALU.add)
                            link(last)
                            S = pr
                        b2 = big[:, gi].rearrange("p (b a) -> p b a", b=2)
                        link(v.tensor_reduce(b2, S, AX.X, ALU.max))
                        v.tensor_tensor(pr, S, b2.unsqueeze(3).to_broadcast([P, 2, 8, LQ]), ALU.subtract).then_inc(s["shifted"], 1)
                    for gi in range(ROUND):
                        if decay is None:
                            dve.wait_ge(s["exp_done"], gi + 1)
                            link(v.tensor_reduce(rsum[:, gi], probs[:, gi], AX.X, ALU.add))
                            link(v.reciprocal(rsum[:, gi], rsum[:, gi]))
                            for half in range(2):
                                last = v.tensor_tensor(rmask[:, gi].rearrange("p (j c b) h -> p j c b h", j=GB, c=DC)[:, :, :, half],
                                                       rsum[:, gi, half * 8:half * 8 + 8].rearrange("p (c j) -> p j c", j=GB).unsqueeze(3).to_broadcast([P, GB, DC, 4]),
                                                       E.c("rowmask").unsqueeze(1).unsqueeze(1).to_broadcast([P, GB, DC, 4]), ALU.mult)
                            link(last)
                        else:
                            link(v.tensor_copy(rmask[:, gi], E.c("rowmask").unsqueeze(1).to_broadcast([P, 16, 4])))
                    for gi in range(ROUND):
                        dve.wait_ge(s["pv_done"], gi + 1)
                        v.tensor_tensor(heads[:, gi].rearrange("p j t (h d) -> p j (t h) d", h=4),
                                        ps[:, 4 * gi:4 * gi + 4, 0:D].rearrange("p j (a d) -> p j a d", d=16),
                                        rmask[:, gi].rearrange("p (j t) h -> p j (t h)", j=GB).unsqueeze(3).to_broadcast([P, GB, 16, 16]), ALU.mult).then_inc(s["heads_ready"], 1)
                    if gate_bias is not None:
                        for gi in range(ROUND):
                            dve.wait_ge(s["picked"], gi + 1)
                            v.tensor_tensor(attnT[:, gi].rearrange("p a b -> p (a b)"), ps[:, 4 * gi + 1, 0:D], gate[:, gi].rearrange("p a b -> p (a b)"), ALU.mult).then_inc(s["attn_ready"], 1)
                    for gi in range(ROUND):
                        xg = src[:, bass.ds(g0 + gi, 1)].rearrange("p a d -> p (a d)")
                        y = ytmp[:, gi]
                        dve.wait_ge(s["y_ready"], gi + 1)
                        if gate_bias is not None:
                            link(v.tensor_tensor(xg, xg, ps[:, 4 * gi, 0:D], ALU.add))
                            continue
                        if heads_gate:
                            tp = top[:, gi]
                            g17 = big[:, gi]
                            lg = probs[:, gi].rearrange("p a b -> p (a b)")
                            link(v.tensor_tensor(lg[:, 0:17], ps[:, 4 * gi, D:D + 17], heads_gate, ALU.add))
                            for lo, hi, at in ((0, 15, 20), (15, 17, 21)):
                                link(v.tensor_reduce(tp[:, at:at + 1], lg[:, lo:hi], AX.X, ALU.max))
                                link(v.tensor_scalar(lg[:, lo:hi], lg[:, lo:hi], tp[:, at:at + 1], None, ALU.subtract))
                            v.tensor_copy(lg[:, 32:49], lg[:, 0:17]).then_inc(s["shifted"], 1)
                            dve.wait_ge(s["exp_done"], ROUND + gi + 1)
                            link(v.tensor_reduce(tp[:, 22:23], lg[:, 64:79], AX.X, ALU.add))
                            link(v.tensor_reduce(tp[:, 23:24], lg[:, 79:81], AX.X, ALU.add))
                            link(v.reciprocal(tp[:, 24:26], tp[:, 22:24]))
                            link(v.tensor_scalar(lg[:, 64:79], lg[:, 64:79], tp[:, 24:25], None, ALU.mult))
                            link(v.tensor_scalar(lg[:, 79:81], lg[:, 79:81], tp[:, 25:26], None, ALU.mult))
                            link(v.max(tp[:, 0:8], lg[:, 64:79]))
                            link(v.tensor_reduce(tp[:, 26:27], tp[:, 0:3], AX.X, ALU.add))
                            link(v.tensor_reduce(tp[:, 27:28], lg[:, 79:81], AX.X, ALU.add))
                            link(v.tensor_scalar(tp[:, 26:27], tp[:, 26:27], lg[:, 80:81], 6.0, ALU.mult, ALU.mult))
                            link(v.tensor_scalar(tp[:, 27:28], tp[:, 27:28], lg[:, 79:80], 2.0, ALU.mult, ALU.mult))
                            link(v.tensor_tensor(tp[:, 26:27], tp[:, 26:27], tp[:, 27:28], ALU.add))
                            link(v.scalar_tensor_tensor(y, ps[:, 4 * gi, 0:D], tp[:, 26:27], rows["bo"], ALU.mult, ALU.add))
                        else:
                            link(v.tensor_tensor(y, ps[:, 4 * gi, 0:D], rows["bo"], ALU.add))
                        if finish == "residual":
                            link(v.tensor_tensor(xg, xg, y, ALU.add))
                        else:
                            link(v.tensor_tensor(y, y, n_sb[:, gi], ALU.add))
                            link(layer_norm(dve, link, v, s, gi, y, y, stats[:, gi]))
                            link(v.tensor_tensor(y, y, rows["g"], ALU.mult))
                            link(v.tensor_tensor(xg, y, rows["b"], ALU.add))

                @block.gpsimd
                def _(pool):
                    if finish == "residual":
                        for gi in range(ROUND):
                            power(E, pool, s, gi, stats[:, gi, 8:9], stats[:, gi, 7:8], 1e-5)
                    if finish == "norm":
                        for gi in range(ROUND):
                            power(E, pool, s, gi, stats[:, gi, 8:9], stats[:, gi, 7:8], 1e-12)

                @block.scalar
                def _(act):
                    a = nc.scalar.activation
                    for gi in range(ROUND):
                        act.wait_ge(s["nT_psum"], gi + 1)
                        nc.scalar.copy(nT[:, gi].rearrange("p c t -> p (c t)"), ps[:, 4 * gi, 0:D]).then_inc(s["nT_ready"], 1)
                    for gi in range(ROUND):
                        act.wait_ge(s["qk_psum"], gi + 1)
                        if bq is None:
                            last = nc.scalar.copy(qk[:, gi].rearrange("p a b -> p (a b)"), ps[:, 4 * gi])
                        else:
                            for i in range(4):
                                b = (bq, bk)[i // 2]
                                last = a(qk[:, gi, i], ps[:, 4 * gi, i * P:(i + 1) * P], ACT.Identity, bias=b[:, i % 2:i % 2 + 1])
                        last.then_inc(s["qk_sb"], 1)
                    if gate_bias is not None:
                        for gi in range(ROUND):
                            act.wait_ge(s["v_psum"], gi + 1)
                            for m in range(DC):
                                last = a(gate[:, gi, m], ps[:, 4 * gi + 3, m * P:(m + 1) * P], ACT.Silu, bias=gate_bias[:, m:m + 1])
                            last.then_inc(s["gate_ready"], 1)
                    if unit_norm or query_scale:
                        for gi in range(ROUND):
                            act.wait_ge(s["norm_psum"], gi + 1)
                            t2 = tmp[:, gi].rearrange("p a b -> p (a b)")[:, 0:norm_cols]
                            a(t2, ps[:, 4 * gi + 3, 0:norm_cols], ACT.Ln, bias=E.c("eps6" if unit_norm else "zero")).then_inc(s["logs"], 1)
                            act.wait_ge(s["logs"], gi + 1)
                            a(t2, t2, ACT.Exp, scale=-0.5).then_inc(s["rstd_ready"], 1)
                    if decay is None:
                        for gi in range(ROUND):
                            act.wait_ge(s["shifted"], gi + 1)
                            pr = probs[:, gi].rearrange("p a b -> p (a b)")
                            a(pr, pr, ACT.Exp).then_inc(s["exp_done"], 1)
                    for gi in range(ROUND):
                        act.wait_ge(s["transposed"], gi + 1)
                        nc.scalar.copy(pT[:, gi].rearrange("p a b -> p (a b)"), ps[:, 4 * gi]).then_inc(s["pT_ready"], 1)
                    if gate_bias is None:
                        for gi in range(ROUND):
                            act.wait_ge(s["picked"], gi + 1)
                            nc.scalar.copy(attnT[:, gi].rearrange("p a b -> p (a b)"), ps[:, 4 * gi + 1, 0:D]).then_inc(s["attn_ready"], 1)
                    if heads_gate:
                        for gi in range(ROUND):
                            act.wait_ge(s["shifted"], ROUND + gi + 1)
                            lg = probs[:, gi].rearrange("p a b -> p (a b)")
                            a(lg[:, 64:81], lg[:, 32:49], ACT.Exp).then_inc(s["exp_done"], 1)

            end_round(nc, handles)


def feature_major(E, tag, nT, source=None, pre=None, gating=None, extra_bias=None):
    nc, ps = E.nc, E.ps
    with ExitStack() as st:
        s, handles = signals(st, nc, tag, "n_ready nT_psum nT_ready n1T_psum n1T_ready mix_done logits_done act_in act_out comb_ready combT_psum "
                             "combT_ready b2_done dve_step var_ready added_eps power_ready")
        n_sb = st.enter_context(nc.sbuf_tensor(f"{tag}_n8", [P, NG, D], F32))
        stats = st.enter_context(nc.sbuf_tensor(f"{tag}_stats", [P, NG, 9], F32))
        if pre:
            n1T = st.enter_context(nc.sbuf_tensor(f"{tag}_n1T", [P, DC, NG * P], F32))
            g1, be1, mix, mix_b, g2, be2 = pre
        if gating:
            gw, gb, kind, comb, b2 = gating
            sc, eq, one1, t8 = (st.enter_context(nc.sbuf_tensor(f"{tag}_{n}", [P, NG, NE], F32)) for n in ("sc", "eq", "one1", "t8"))
            m1 = st.enter_context(nc.sbuf_tensor(f"{tag}_m1", [P, NG], F32))
            m2 = st.enter_context(nc.sbuf_tensor(f"{tag}_m2", [P, NG], F32))
            combT = st.enter_context(nc.sbuf_tensor(f"{tag}_combT", [NE, NG, P], F32))
        with nc.Block(no_gpsimd_drain=True) as block:

            @block.tensor
            def _(pe):
                mm, tr = nc.tensor.matmul, nc.tensor.transpose
                if pre:
                    for g in range(NG):
                        pe.wait_ge(s["n_ready"], g + 1)
                        for c in range(DC):
                            last = tr(ps[:, g, c * P:(c + 1) * P], n_sb[:, g, c * P:(c + 1) * P], E.c("ident"))
                        last.then_inc(s["n1T_psum"], 1)
                    for g in range(NG):
                        pe.wait_ge(s["n1T_ready"], g + 1)
                        for c in range(DC):
                            last = mm(ps[:, g, D:2 * D], n1T[:, c, g * P:(g + 1) * P], mix[:, c], start=c == 0, stop=c == DC - 1)
                        last.then_inc(s["mix_done"], 1)
                for g in range(NG):
                    pe.wait_ge(s["n_ready"], g + 1 + (NG if pre else 0))
                    for c in range(DC):
                        last = tr(ps[:, g, c * P:(c + 1) * P], n_sb[:, g, c * P:(c + 1) * P], E.c("ident"))
                    last.then_inc(s["nT_psum"], 1)
                if gating:
                    for g in range(NG):
                        pe.wait_ge(s["nT_ready"], g + 1)
                        for c in range(DC):
                            last = mm(ps[:, g, D:D + NE], nT[:, c, g * P:(g + 1) * P], gw[:, c], start=c == 0, stop=c == DC - 1)
                    last.then_inc(s["logits_done"], 1)
                    pe.wait_ge(s["comb_ready"], 1)
                    for g in range(NG):
                        last = tr(ps[0:NE, g, 0:P], comb[:, g], E.c("ident"))
                    last.then_inc(s["combT_psum"], 1)
                    pe.wait_ge(s["combT_ready"], 1)
                    for g in range(NG):
                        mm(ps[:, g, D:2 * D], combT[:, g], b2, start=True, stop=True).then_inc(s["b2_done"], 1)

            @block.gpsimd
            def _(pool):
                if source is not None:
                    return
                power(E, pool, s, 0, stats[:, :, 8:9], stats[:, :, 7:8], 1e-5)
                if pre:
                    power(E, pool, s, 1, stats[:, :, 8:9], stats[:, :, 7:8], 1e-5)
                    for g in range(NG):
                        power(E, pool, s, 2 + g, stats[:, g, 8:9], stats[:, g, 7:8], 1e-5)

            @block.scalar
            def _(act):
                if pre:
                    for g in range(NG):
                        act.wait_ge(s["n1T_psum"], g + 1)
                        nc.scalar.copy(n1T[:, :, g * P:(g + 1) * P], ps[:, g, 0:D].rearrange("p (c t) -> p c t", c=DC)).then_inc(s["n1T_ready"], 1)
                for g in range(NG):
                    act.wait_ge(s["nT_psum"], g + 1)
                    nc.scalar.copy(nT[:, :, g * P:(g + 1) * P], ps[:, g, 0:D].rearrange("p (c t) -> p c t", c=DC)).then_inc(s["nT_ready"], 1)
                if gating:
                    act.wait_ge(s["act_in"], 1)
                    nc.scalar.activation(sc[:], t8[:], ACT.Sigmoid if kind == "sigmoid" else ACT.Exp).then_inc(s["act_out"], 1)
                    act.wait_ge(s["combT_psum"], 1)
                    nc.scalar.copy(combT[:], ps[0:NE, :, 0:P]).then_inc(s["combT_ready"], 1)

            @block.vector
            def _(dve):
                v = nc.vector
                link = chain(dve, s["dve_step"])

                def row(r, n=NG):
                    return r.unsqueeze(1).to_broadcast([P, n, D])

                def statistics(x, n):
                    for g in range(NG):
                        last = v.bn_stats(stats[:, g, 0:6], x[:, g])
                    link(last)
                    for g in range(NG):
                        last = v.bn_aggr(stats[:, g, 6:8], stats[:, g, 0:6])
                    last.then_inc(s["var_ready"], 1)
                    dve.wait_ge(s["power_ready"], n + 1)

                if source is not None:
                    for g in range(NG):
                        v.tensor_copy(n_sb[:, g], source[:, g]).then_inc(s["n_ready"], 1)
                    return
                if pre:
                    statistics(E.x, 0)
                    for g in range(NG):
                        last = v.tensor_scalar(n_sb[:, g], E.x[:, g], stats[:, g, 6:7], stats[:, g, 8:9], ALU.subtract, ALU.mult)
                    link(last)
                    link(v.tensor_tensor(E.x[:], E.x[:], n_sb[:], ALU.add))
                    statistics(n_sb, 1)
                    link(v.tensor_copy(E.z[:], n_sb[:]))
                    for g in range(NG):
                        link(v.tensor_scalar(n_sb[:, g], n_sb[:, g], stats[:, g, 6:7], stats[:, g, 8:9], ALU.subtract, ALU.mult))
                        link(v.tensor_tensor(n_sb[:, g], n_sb[:, g], g1, ALU.mult))
                        v.tensor_tensor(n_sb[:, g], n_sb[:, g], be1, ALU.add).then_inc(s["n_ready"], 1)
                    dve.wait_ge(s["n_ready"], NG)
                    link(v.tensor_tensor(E.z[:], E.z[:], n_sb[:], ALU.add))
                    link(v.tensor_tensor(E.z[:], E.z[:], row(mix_b), ALU.add))
                    link(v.tensor_tensor(E.x[:], E.x[:], n_sb[:], ALU.add))
                    link(v.tensor_tensor(E.x[:], E.x[:], row(mix_b), ALU.add))
                    for g in range(NG):
                        dve.wait_ge(s["mix_done"], g + 1)
                        v.tensor_tensor(E.x[:, g], E.x[:, g], ps[:, g, D:2 * D], ALU.add)
                        link(v.tensor_tensor(E.z[:, g], E.z[:, g], ps[:, g, D:2 * D], ALU.add))
                        link(layer_norm(dve, link, v, s, 2 + g, n_sb[:, g], E.z[:, g], stats[:, g]))
                        link(v.tensor_tensor(n_sb[:, g], n_sb[:, g], g2, ALU.mult))
                        v.tensor_tensor(n_sb[:, g], n_sb[:, g], be2, ALU.add).then_inc(s["n_ready"], 1)
                else:
                    statistics(E.x, 0)
                    for g in range(NG):
                        v.tensor_scalar(n_sb[:, g], E.x[:, g], stats[:, g, 6:7], stats[:, g, 8:9], ALU.subtract, ALU.mult).then_inc(s["n_ready"], 1)
                if gating:
                    dve.wait_ge(s["logits_done"], 1)
                    lg = ps[:, :, D:D + NE]
                    if kind == "sigmoid":
                        v.tensor_tensor(t8[:], lg, gb.unsqueeze(1).to_broadcast([P, NG, NE]), ALU.add).then_inc(s["act_in"], 1)
                    else:
                        link(v.tensor_reduce(m1[:], lg, AX.X, ALU.max))
                        v.tensor_tensor(t8[:], lg, m1[:].unsqueeze(2).to_broadcast([P, NG, NE]), ALU.subtract).then_inc(s["act_in"], 1)
                    dve.wait_ge(s["act_out"], 1)
                    if kind != "sigmoid":
                        link(v.tensor_reduce(m1[:], sc[:], AX.X, ALU.add))
                        link(v.reciprocal(m1[:], m1[:]))
                        link(v.tensor_tensor(sc[:], sc[:], m1[:].unsqueeze(2).to_broadcast([P, NG, NE]), ALU.mult))

                    def first_of_largest(out, scores, m):
                        link(v.tensor_reduce(m, scores, AX.X, ALU.max))
                        link(v.tensor_tensor(eq[:], scores, m.unsqueeze(2).to_broadcast([P, NG, NE]), ALU.is_equal))
                        link(v.tensor_tensor(eq[:], eq[:], E.c("rank").unsqueeze(1).to_broadcast([P, NG, NE]), ALU.mult))
                        link(v.tensor_reduce(m2[:], eq[:], AX.X, ALU.max))
                        link(v.tensor_tensor(out, eq[:], m2[:].unsqueeze(2).to_broadcast([P, NG, NE]), ALU.is_equal))

                    first_of_largest(one1[:], sc[:], m1[:])
                    link(v.scalar_tensor_tensor(t8[:], one1[:], -4.0, sc[:], ALU.mult, ALU.add))
                    m3 = stats[:, :, 0]
                    first_of_largest(comb, t8[:], m3)
                    link(v.tensor_tensor(comb, comb, one1[:], ALU.add))
                    last = v.tensor_tensor(comb, comb, sc[:], ALU.mult)
                    if kind == "sigmoid":
                        link(last)
                        link(v.tensor_tensor(m1[:], m1[:], m3, ALU.add))
                        link(v.tensor_scalar(m1[:], m1[:], 1e-6, None, ALU.add))
                        link(v.reciprocal(m1[:], m1[:]))
                        last = v.tensor_tensor(comb, comb, m1[:].unsqueeze(2).to_broadcast([P, NG, NE]), ALU.mult)
                    last.then_inc(s["comb_ready"], 1)
                    dve.wait_ge(s["b2_done"], NG)
                    link(v.tensor_tensor(E.x[:], E.x[:], ps[:, :, D:2 * D], ALU.add))
                if extra_bias is not None:
                    link(v.scalar_tensor_tensor(E.x[:], row(extra_bias[0]), extra_bias[1], E.x[:], ALU.mult, ALU.add))
        end_round(nc, handles)


def mlp_block(E, s, bufs, nT, steps, chunks, func, glu=False, loads=()):
    nc, ps = E.nc, E.ps
    hid, sil = bufs
    W = 2 if glu else 1
    HALF = NG * P // 2
    TH = NG // 2
    with nc.Block(no_gpsimd_drain=True) as block:

        @block.sync
        def _(sp):
            for need, sem, pairs in loads:
                if need:
                    sp.wait_ge(s["down_done"], need)
                for dst, src in pairs:
                    sp.dma_start(dst, src).then_inc(sem, 16)
            for need, sem, pairs in loads:
                sp.wait_ge(sem, 16 * len(pairs))

        @block.tensor
        def _(pe):
            mm = nc.tensor.matmul

            def up(i):
                step = steps[i]
                if step.get("await"):
                    pe.wait_ge(*step["await"])
                for m in range(chunks):
                    n = i * chunks + m
                    for w in range(W):
                        b = (n * W + w) % 4
                        if w == 0 and (n + 1) * W > 4:
                            pe.wait_ge(s["hid_ready"], n + 1 - 4 // W)
                        for c in range(DC):
                            last = mm(ps[:, b], step["up"][w][:, c, m * P:(m + 1) * P], nT[:, c, step["half"] * HALF:(step["half"] + 1) * HALF], start=c == 0, stop=c == DC - 1)
                    last.then_inc(s["up_done"], 1)

            def down(i):
                step = steps[i]
                pe.wait_ge(s["hid_ready"], (i + 1) * chunks)
                for t in range(TH):
                    n = i * TH + t
                    if n >= 4:
                        pe.wait_ge(s["added"], n - 3)
                    for k in range(chunks):
                        last = mm(ps[:, 4 + n % 4, 0:D], hid[:, i % 2, k, t * P:(t + 1) * P], step["down"][:, k], start=k == 0, stop=k == chunks - 1)
                    last.then_inc(s["down_done"], 1)

            up(0)
            for i in range(len(steps)):
                if i + 1 < len(steps):
                    up(i + 1)
                down(i)

        @block.scalar
        def _(act):
            for i, step in enumerate(steps):
                if i >= 2:
                    act.wait_ge(s["down_done"], (i - 1) * TH)
                for m in range(chunks):
                    n = i * chunks + m
                    act.wait_ge(s["up_done"], n + 1)
                    if glu:
                        if n >= 2:
                            act.wait_ge(s["hid_ready"], n - 1)
                        nc.scalar.activation(sil[:, n % 2], ps[:, (2 * n) % 4], ACT.Silu).then_inc(s["sil_ready"], 1)
                    else:
                        nc.scalar.activation(hid[:, i % 2, m], ps[:, n % 4], func, bias=step["b1"](m)).then_inc(s["hid_ready"], 1)

        @block.vector
        def _(dve):
            v = nc.vector

            def add(i):
                step = steps[i]
                if i:
                    dve.wait_ge(s["added"], i * TH)
                for t in range(TH):
                    n = i * TH + t
                    g = step["half"] * TH + t
                    dve.wait_ge(s["down_done"], n + 1)
                    dst = step["into"][:, g]
                    v.scalar_tensor_tensor(dst, ps[:, 4 + n % 4, 0:D], step["weight"](g), dst, ALU.mult, ALU.add).then_inc(s["added"], 1)

            for i in range(len(steps)):
                if glu:
                    if i >= 2:
                        dve.wait_ge(s["down_done"], (i - 1) * TH)
                    for m in range(chunks):
                        n = i * chunks + m
                        dve.wait_ge(s["sil_ready"], n + 1)
                        v.tensor_tensor(hid[:, i % 2, m], sil[:, n % 2], ps[:, (2 * n + 1) % 4], ALU.mult).then_inc(s["hid_ready"], 1)
                    if i:
                        add(i - 1)
                else:
                    add(i)
            if glu:
                add(len(steps) - 1)


MLP_SIGNALS = "up_done hid_ready sil_ready down_done added load_a load_b"


def expert_mixture(E, tag, w1, w2, b1_at, comb, nT, func, shared=None):
    nc = E.nc

    def views(w):
        return w[:, 0:2 * FF].rearrange("p (c n) -> p c n", c=DC), w[:, 2 * FF:4 * FF].rearrange("p (c n) -> p c n", c=FC)

    def load(w, e):
        up, down = views(w)
        return [(up, w1[bass.ds(e, 1)].rearrange("a (c p) n -> (a p) c n", p=P)), (down, w2[bass.ds(e, 1)].rearrange("a (c p) n -> (a p) c n", p=P))]

    with ExitStack() as st:
        s, handles = signals(st, nc, tag, MLP_SIGNALS)
        hid = st.enter_context(nc.sbuf_tensor(f"{tag}_hid", [P, 2, FC, NG * P // 2], F32))
        with nc.Fori(0, NE // 2) as pair:
            e0 = pair * 2
            steps = []
            for k, w in enumerate((E.wA, E.wB)):
                up, down = views(w)
                for half in range(2):
                    steps.append({"up": [up], "down": down, "half": half, "into": E.x,
                                  "b1": lambda m, k=k: E.cols[:, bass.ds((e0 + k) * FC + (b1_at + m), 1)],
                                  "weight": lambda g, k=k: comb[:, g, bass.ds(e0 + k, 1)]})
            steps[2]["await"] = (s["load_b"], 32)
            mlp_block(E, s, (hid, None), nT, steps, FC, func,
                      loads=[(0, s["load_b"], load(E.wB, e0 + 1)), (NG, s["load_a"], load(E.wA, e0 + 2))])
            end_round(nc, handles)
        if shared is not None:
            up, down = views(E.wA)
            steps = [{"up": [up], "down": down, "half": half, "into": E.x, "b1": lambda m: E.cols[:, b1_at + NE * FC + m:b1_at + NE * FC + m + 1],
                      "weight": lambda g: shared} for half in range(2)]
            mlp_block(E, s, (hid, None), nT, steps, FC, func)
            end_round(nc, handles)


def decoder_mlp(E, tag, w1, w2, b1, rows):
    nc, h = E.nc, E.h
    with ExitStack() as st:
        nT = st.enter_context(nc.sbuf_tensor(f"{tag}_nT", [P, DC, NG * P], F32))
        feature_major(E, tag + "t", nT, source=h)
        hid = st.enter_context(nc.sbuf_tensor(f"{tag}_hid", [P, 2, FC, NG * P // 2], F32))
        s, handles = signals(st, nc, tag, MLP_SIGNALS)
        steps = [{"up": [w1], "down": w2, "half": half, "into": h, "b1": b1, "weight": lambda g: 1.0} for half in range(2)]
        mlp_block(E, s, (hid, None), nT, steps, FC, ACT.Relu)
        end_round(nc, handles)
        t, post = signals(st, nc, tag + "n", "dve_step var_ready added_eps power_ready")
        stats = st.enter_context(nc.sbuf_tensor(f"{tag}_stats", [P, NG, 9], F32))
        with nc.Block(no_gpsimd_drain=True) as block:

            @block.vector
            def _(dve):
                v = nc.vector
                link = chain(dve, t["dve_step"])
                row = lambda n: rows[n].unsqueeze(1).to_broadcast([P, NG, D])
                link(v.tensor_tensor(h[:], h[:], row("b2"), ALU.add))
                for g in range(NG):
                    last = v.bn_stats(stats[:, g, 0:6], h[:, g])
                link(last)
                for g in range(NG):
                    last = v.bn_aggr(stats[:, g, 6:8], stats[:, g, 0:6])
                last.then_inc(t["var_ready"], 1)
                dve.wait_ge(t["power_ready"], 1)
                for g in range(NG):
                    last = v.tensor_scalar(h[:, g], h[:, g], stats[:, g, 6:7], stats[:, g, 8:9], ALU.subtract, ALU.mult)
                link(last)
                link(v.tensor_tensor(h[:], h[:], row("g"), ALU.mult))
                link(v.tensor_tensor(h[:], h[:], row("b"), ALU.add))

            @block.gpsimd
            def _(pool):
                power(E, pool, t, 0, stats[:, :, 8:9], stats[:, :, 7:8], 1e-12)
        end_round(nc, post)


def decoder(E, A):
    nc = E.nc
    with ExitStack() as st:
        s, handles = signals(st, nc, "dec", "ints dve_step var_ready added_eps power_ready")
        ints = st.enter_context(nc.sbuf_tensor("mask_ints", [P, NB, LQ], I32))
        E.keep = st.enter_context(nc.sbuf_tensor("mask_keep", [P, NB, LQ], F32))
        E.floor = st.enter_context(nc.sbuf_tensor("mask_floor", [P, NB, LQ], F32))
        stats = st.enter_context(nc.sbuf_tensor("dec_stats", [P, NG, 9], F32))
        with nc.Block(no_gpsimd_drain=True) as block:

            @block.sync
            def _(sp):
                for i in range(4):
                    sp.dma_start(ints[LQ * i:LQ * (i + 1)], A["mask_BxSxS_ik0"].rearrange("b q k -> q b k")).then_inc(s["ints"], 16)

            @block.vector
            def _(dve):
                v = nc.vector
                link = chain(dve, s["dve_step"])
                dve.wait_ge(s["ints"], 64)
                link(v.tensor_scalar(E.keep[:], ints[:], 0.0, None, ALU.not_equal))
                link(v.tensor_scalar(E.floor[:], E.keep[:], -1.0, 10000.0, ALU.add, ALU.mult))
                for g in range(NG):
                    link(layer_norm(dve, link, v, s, g, E.h[:, g], E.x[:, g], stats[:, g]))

            @block.gpsimd
            def _(pool):
                for g in range(NG):
                    power(E, pool, s, g, stats[:, g, 8:9], stats[:, g, 7:8], 1e-5)
        end_round(nc, handles)

        four = lambda w: [w[:, i * 512:(i + 1) * 512].rearrange("p (c n) -> p c n", c=DC) for i in range(4)]

        def attention_load(key, W, R, layer):
            return [(W[:, 0:2048].rearrange("p (a c n) -> p a c n", a=4, c=DC), A[f"{key}_w"][bass.ds(layer, 1)].rearrange("l a (c p) n -> (l p) a c n", p=P)),
                    (R[:, 0:4], A[f"{key}_rows"][bass.ds(layer, 1)].rearrange("l r d -> l (r d)").partition_broadcast(P).rearrange("p l (r d) -> p (l r) d", r=4))]

        def mlp_load(layer):
            return [(E.wB[:, 0:2 * FF].rearrange("p (c n) -> p c n", c=DC), A["L1_xattn_w1"][bass.ds(layer, 1)].rearrange("a (c p) n -> (a p) c n", p=P)),
                    (E.wB[:, 2 * FF:4 * FF].rearrange("p (c n) -> p c n", c=FC), A["L1_xattn_w2"][bass.ds(layer, 1)].rearrange("a (c p) n -> (a p) c n", p=P)),
                    (E.rB[:, 0:3], A["mlp_rows"][bass.ds(layer, 1)].rearrange("l r d -> l (r d)").partition_broadcast(P).rearrange("p l (r d) -> p (l r) d", r=3))]

        def rows(R):
            return {"bv": R[:, 0], "bo": R[:, 1], "g": R[:, 2], "b": R[:, 3]}

        send_for(E, "sa", attention_load("sa", E.wC, E.rC, 0))
        bias = st.enter_context(nc.sbuf_tensor("layer_bias", [P, 24], F32))
        with nc.Fori(0, NL) as layer:
            await_weights(E, "sa")
            send_for(E, "ca", attention_load("ca", E.wA, E.rA, layer))
            send_for(E, "mlp", mlp_load(layer))
            b, bh = signals(st, nc, "bias", "moved") if not E.bias_sem else E.bias_sem
            E.bias_sem = (b, bh)
            with nc.Block(no_gpsimd_drain=True) as block:

                @block.vector
                def _(dve):
                    for i, name in enumerate(("sa_b0", "ca_b0", "L1_b1_0")):
                        nc.vector.tensor_copy(bias[:, 8 * i:8 * i + 8], E.cols[:, bass.ds(layer * 8 + COL_AT[name][0], 8)]).then_inc(b["moved"], 1)
                    dve.wait_ge(b["moved"], 3)
            end_round(nc, bh)
            w = four(E.wC)
            self_attention(E, "sa", w, rows(E.rC), bq=bias[:, 0:2], bk=bias[:, 2:4], mask=True, source=E.h, finish="norm")
            await_weights(E, "ca")
            send_for(E, "sa", attention_load("sa", E.wC, E.rC, layer + 1))
            w = four(E.wA)
            cross_attention(E, "ca", 16, *w, rows(E.rA), bq=bias[:, 8:10], bk=bias[:, 10:12], source=E.h, finish="norm")
            await_weights(E, "mlp")
            decoder_mlp(E, "dm", E.wB[:, 0:2 * FF].rearrange("p (c n) -> p c n", c=DC), E.wB[:, 2 * FF:4 * FF].rearrange("p (c n) -> p c n", c=FC),
                        lambda m: bias[:, 16 + m:17 + m], {"b2": E.rB[:, 0], "g": E.rB[:, 1], "b": E.rB[:, 2]})
        await_weights(E, "sa")
        t, th = signals(st, nc, "dec_end", "added")
        with nc.Block(no_gpsimd_drain=True) as block:

            @block.vector
            def _(dve):
                nc.vector.tensor_tensor(E.x[:], E.x[:], E.h[:], ALU.add).then_inc(t["added"], 1)
                dve.wait_ge(t["added"], 1)
        end_round(nc, th)


def prepare_decay(E, gamma_sb, decay):
    nc = E.nc
    with ExitStack() as st:
        s, handles = signals(st, nc, "decay", "sig act_step neg")
        with nc.Block(no_gpsimd_drain=True) as block:

            @block.scalar
            def _(act):
                nc.scalar.activation(gamma_sb[:], gamma_sb[:], ACT.Sigmoid).then_inc(s["sig"], 1)
                act.wait_ge(s["neg"], 1)
                for t in range(4):
                    nc.scalar.activation(decay[:, t], E.c("lag"), ACT.Exp, scale=gamma_sb[:, t:t + 1])

            @block.vector
            def _(dve):
                dve.wait_ge(s["sig"], 1)
                nc.vector.tensor_scalar(gamma_sb[:], gamma_sb[:], -1.0, None, ALU.mult).then_inc(s["neg"], 1)
        end_round(nc, handles)


def prepare_lengths(E, mask_ints, length, inverse):
    nc, ps = E.nc, E.ps
    with ExitStack() as st:
        s, handles = signals(st, nc, "len", "dve_step diag summed")
        m = st.enter_context(nc.sbuf_tensor("len_m", [NB, LK], F32))
        n = st.enter_context(nc.sbuf_tensor("len_n", [NB, 1], F32))
        diag = st.enter_context(nc.sbuf_tensor("len_diag", [NB, NB], F32))
        ones = st.enter_context(nc.sbuf_tensor("len_ones", [NB, P], F32))
        with nc.Block(no_gpsimd_drain=True) as block:

            @block.vector
            def _(dve):
                v = nc.vector
                link = chain(dve, s["dve_step"])
                link(v.memset(ones[:], 1.0))
                link(v.tensor_scalar(m[:], mask_ints[:], -1.0, 1.0, ALU.mult, ALU.add))
                link(v.tensor_reduce(n[:], m[:], AX.X, ALU.add))
                link(v.tensor_scalar(n[:], n[:], -1.0, None, ALU.add))
                v.tensor_scalar(diag[:], E.c("ident")[0:NB, 0:NB], n[:, 0:1], None, ALU.mult).then_inc(s["diag"], 1)
                dve.wait_ge(s["summed"], 1)
                link(v.tensor_copy(length[:], ps[:, 0, 0:NB]))
                link(v.reciprocal(inverse[:], length[:]))

            @block.tensor
            def _(pe):
                pe.wait_ge(s["diag"], 1)
                nc.tensor.matmul(ps[:, 0, 0:NB], ones[:], diag[:], start=True, stop=True).then_inc(s["summed"], 1)
        end_round(nc, handles)


def prepare_centred(E, raw, centred, bias_in, bias_out):
    nc, ps = E.nc, E.ps
    with ExitStack() as st:
        s, handles = signals(st, nc, "cent", "done copied")
        with nc.Block(no_gpsimd_drain=True) as block:

            @block.tensor
            def _(pe):
                for i, w in enumerate(raw):
                    for c in range(DC):
                        for m in range(DC):
                            last = nc.tensor.matmul(ps[:, 2 * i + c, m * P:(m + 1) * P], w[:, m, c * P:(c + 1) * P], E.c("centre"), start=True, stop=True)
                for i, b in enumerate(bias_in):
                    last = nc.tensor.matmul(ps[:, 4, 2 * i:2 * i + 2], E.c("centre"), b, start=True, stop=True)
                last.then_inc(s["done"], 1)

            @block.vector
            def _(dve):
                dve.wait_ge(s["done"], 1)
                for i, w in enumerate(centred):
                    nc.vector.tensor_copy(w[:], ps[:, 2 * i:2 * i + 2, 0:D])
                nc.vector.tensor_copy(bias_out[:], ps[:, 4, 0:4]).then_inc(s["copied"], 1)
                dve.wait_ge(s["copied"], 1)
        end_round(nc, handles)


def fourier_attention(E, w, rows, bq, bk, proj):
    nc, ps = E.nc, E.ps
    wq, wk, wv, wo = w
    NCHK = 4
    MAGIC = 12582912.0
    TURN = 6.283185
    with ExitStack() as st:
        s, handles = signals(st, nc, "four", "n_ready nT_psum nT_ready qk_psum qk_ready v_psum v_ready p_done turns_ready rounded frac_ready sin_ready abs_ready cos_ready "
                             "scores_done masked o_done o_ready oT_psum oT_ready y_ready x_done dve_step var_ready added_eps power_ready")

        def sb(name, shape):
            return st.enter_context(nc.sbuf_tensor(f"four_{name}", [P] + shape, F32))

        n_sb, stats, nT, qk, v_sb = sb("n", [D]), sb("stats", [9]), sb("nT", [DC, P]), sb("qk", [4, P]), sb("v", [D])
        turns, frac, rnd = sb("turns", [2, 1024]), sb("frac", [2, 1024]), sb("rnd", [1024])
        sin, cos, sc, o_sb, oT, ytmp = sb("sin", [2, 1024]), sb("cos", [2, 1024]), sb("sc", [2, 4, P]), sb("o", [D]), sb("oT", [DC, P]), sb("ytmp", [D])
        half_pi = sb("half_pi", [1])
        fill(E, "four", [(half_pi[:], float(np.pi / 2))])
        with nc.Fori(0, NG) as g:
            with nc.Block(no_gpsimd_drain=True) as block:

                @block.tensor
                def _(pe):
                    mm, tr = nc.tensor.matmul, nc.tensor.transpose
                    pe.wait_ge(s["n_ready"], 1)
                    for c in range(DC):
                        last = tr(ps[:, 7, c * P:(c + 1) * P], n_sb[:, c * P:(c + 1) * P], E.c("ident"))
                    last.then_inc(s["nT_psum"], 1)
                    pe.wait_ge(s["nT_ready"], 1)
                    for i, wi in enumerate((wq, wk)):
                        for m in range(DC):
                            for c in range(DC):
                                last = mm(ps[:, 6, (2 * i + m) * P:(2 * i + m + 1) * P], wi[:, c, m * P:(m + 1) * P], nT[:, c], start=c == 0, stop=c == DC - 1)
                    last.then_inc(s["qk_psum"], 1)
                    for c in range(DC):
                        last = mm(ps[:, 7, 0:D], nT[:, c], wv[:, c], start=c == 0, stop=c == DC - 1)
                    last.then_inc(s["v_psum"], 1)
                    pe.wait_ge(s["qk_ready"], 1)

                    def project(hc):
                        if hc >= 2:
                            pe.wait_ge(s["turns_ready"], hc - 1)
                        for i in range(2):
                            for a in range(4):
                                h = 4 * hc + a
                                last = mm(ps[:, 2 * (hc % 2) + i, a * P:(a + 1) * P], proj[:, h % 8], qk[:, 2 * i + h // 8], start=True, stop=True)
                        last.then_inc(s["p_done"], 1)

                    def scores(hc):
                        pe.wait_ge(s["sin_ready"], hc + 1)
                        pe.wait_ge(s["cos_ready"], hc + 1)
                        if hc >= 2:
                            pe.wait_ge(s["masked"], hc - 1)
                        for a in range(4):
                            for i, f in enumerate((cos, sin)):
                                last = mm(ps[:, 4 + hc % 2, a * P:(a + 1) * P], f[:, hc % 2, 512 + a * P:512 + (a + 1) * P], f[:, hc % 2, a * P:(a + 1) * P], start=i == 0, stop=i == 1)
                        last.then_inc(s["scores_done"], 1)

                    def values(hc):
                        pe.wait_ge(s["masked"], hc + 1)
                        if hc == 0:
                            pe.wait_ge(s["v_ready"], 1)
                        for a in range(4):
                            h = 4 * hc + a
                            last = mm(ps[:, 6, h * 16:h * 16 + 16], sc[:, hc % 2, a], v_sb[:, h * 16:h * 16 + 16], start=True, stop=True)
                        last.then_inc(s["o_done"], 1)

                    for k in range(NCHK + 2):
                        if k < NCHK:
                            project(k)
                        if 0 <= k - 1 < NCHK:
                            scores(k - 1)
                        if 0 <= k - 2 < NCHK:
                            values(k - 2)
                    pe.wait_ge(s["o_ready"], 1)
                    for c in range(DC):
                        last = tr(ps[:, 7, c * P:(c + 1) * P], o_sb[:, c * P:(c + 1) * P], E.c("ident"))
                    last.then_inc(s["oT_psum"], 1)
                    pe.wait_ge(s["oT_ready"], 1)
                    for c in range(DC):
                        last = mm(ps[:, 6, 0:D], oT[:, c], wo[:, c], start=c == 0, stop=c == DC - 1)
                    last.then_inc(s["y_ready"], 1)

                @block.vector
                def _(dve):
                    v = nc.vector
                    link = chain(dve, s["dve_step"])
                    xg = E.x[:, bass.ds(g, 1)].rearrange("p a d -> p (a d)")
                    layer_norm(dve, link, v, s, 0, n_sb[:], xg, stats).then_inc(s["n_ready"], 1)
                    dve.wait_ge(s["v_psum"], 1)
                    v.tensor_tensor(v_sb[:], ps[:, 7, 0:D], rows["bv"], ALU.add).then_inc(s["v_ready"], 1)

                    def reduce_angles(hc):
                        u, f = turns[:, hc % 2], frac[:, hc % 2]
                        dve.wait_ge(s["turns_ready"], hc + 1)
                        link(v.tensor_scalar(rnd[:], u, MAGIC, -MAGIC, ALU.add, ALU.add))
                        if hc >= 2:
                            dve.wait_ge(s["cos_ready"], hc - 1)
                        v.tensor_tensor(f, u, rnd[:], ALU.subtract).then_inc(s["frac_ready"], 1)
                        dve.wait_ge(s["frac_ready"], hc + 1)
                        v.scalar_tensor_tensor(u, f, -1.0, f, ALU.mult, ALU.max).then_inc(s["abs_ready"], 1)

                    def mask(hc):
                        dve.wait_ge(s["scores_done"], hc + 1)
                        if hc >= 2:
                            dve.wait_ge(s["o_done"], hc - 1)
                        v.scalar_tensor_tensor(sc[:, hc % 2], ps[:, 4 + hc % 2].rearrange("p (a q) -> p a q", a=4), 1.0 / 128,
                                               E.c("same_seq").unsqueeze(1).to_broadcast([P, 4, P]), ALU.mult, ALU.mult).then_inc(s["masked"], 1)

                    for k in range(NCHK + 1):
                        if k < NCHK:
                            reduce_angles(k)
                        if k:
                            mask(k - 1)
                    dve.wait_ge(s["y_ready"], 1)
                    link(v.tensor_tensor(ytmp[:], ps[:, 6, 0:D], rows["bo"], ALU.add))
                    link(v.tensor_tensor(xg, xg, ytmp[:], ALU.add))

                @block.gpsimd
                def _(pool):
                    power(E, pool, s, 0, stats[:, 8:9], stats[:, 7:8], 1e-5)

                @block.scalar
                def _(act):
                    a = nc.scalar.activation
                    act.wait_ge(s["nT_psum"], 1)
                    nc.scalar.copy(nT[:].rearrange("p c t -> p (c t)"), ps[:, 7, 0:D]).then_inc(s["nT_ready"], 1)
                    act.wait_ge(s["qk_psum"], 1)
                    for i in range(4):
                        b = (bq, bk)[i // 2]
                        last = a(qk[:, i], ps[:, 6, i * P:(i + 1) * P], ACT.Identity, bias=b[:, i % 2:i % 2 + 1])
                    last.then_inc(s["qk_ready"], 1)

                    def to_turns(hc):
                        act.wait_ge(s["p_done"], hc + 1)
                        if hc >= 2:
                            act.wait_ge(s["cos_ready"], hc - 1)
                        nc.scalar.mul(turns[:, hc % 2], ps[:, 2 * (hc % 2):2 * (hc % 2) + 2].rearrange("p a b -> p (a b)"), float(0.25 / (2 * np.pi))).then_inc(s["turns_ready"], 1)

                    to_turns(0)
                    for k in range(NCHK):
                        if k + 1 < NCHK:
                            to_turns(k + 1)
                        act.wait_ge(s["frac_ready"], k + 1)
                        if k >= 2:
                            act.wait_ge(s["scores_done"], k - 1)
                        a(sin[:, k % 2], frac[:, k % 2], ACT.Sin, scale=TURN).then_inc(s["sin_ready"], 1)
                        act.wait_ge(s["abs_ready"], k + 1)
                        a(cos[:, k % 2], turns[:, k % 2], ACT.Sin, scale=-TURN, bias=half_pi[:]).then_inc(s["cos_ready"], 1)
                    act.wait_ge(s["o_done"], NCHK)
                    nc.scalar.copy(o_sb[:], ps[:, 6, 0:D]).then_inc(s["o_ready"], 1)
                    act.wait_ge(s["oT_psum"], 1)
                    nc.scalar.copy(oT[:].rearrange("p c t -> p (c t)"), ps[:, 7, 0:D]).then_inc(s["oT_ready"], 1)

            end_round(nc, handles)


def gated_mlp(E, w_ints, up, down):
    nc = E.nc
    HC = HID // P
    with ExitStack() as st:
        s, handles = signals(st, nc, "glu", MLP_SIGNALS)
        t, pre = signals(st, nc, "deq", "scaled")
        nT = st.enter_context(nc.sbuf_tensor("glu_nT", [P, DC, NG * P], F32))
        hid = st.enter_context(nc.sbuf_tensor("glu_hid", [P, 2, HC, NG * P // 2], F32))
        sil = st.enter_context(nc.sbuf_tensor("glu_sil", [P, 2, NG * P // 2], F32))
        with nc.Block(no_gpsimd_drain=True) as block:

            @block.vector
            def _(dve):
                for i, (dst, src) in enumerate(w_ints):
                    nc.vector.tensor_scalar(dst, src, float(np.float32(1.0 / 127.0)), None, ALU.mult).then_inc(t["scaled"], 1)
                dve.wait_ge(t["scaled"], len(w_ints))
        end_round(nc, pre)
        feature_major(E, "glut", nT)
        steps = [{"up": up, "down": down, "half": half, "into": E.x, "weight": lambda g: 1.0} for half in range(2)]
        mlp_block(E, s, (hid, sil), nT, steps, HC, None, glu=True)
        end_round(nc, handles)


def gated_recurrence(E, w, rows):
    nc, ps = E.nc, E.ps
    w_dx, w_x, w_gx, w_ga, w_o, pe_dx, pe_x = w
    HALF = NG * P // 2
    col = E.col
    with ExitStack() as st:
        def sb(name, shape):
            return st.enter_context(nc.sbuf_tensor(f"rec_{name}", [P] + shape, F32))

        nT = sb("nT", [DC, NG * P])
        feature_major(E, "rect", nT)
        s, handles = signals(st, nc, "rec", "expit rest_ready root_ready xh_psum xh_ready gates_psum gates_ready scan_done y_ready x_done dve_step var_ready added_eps power_ready")
        expit, keep = sb("expit", [DC]), sb("keep", [DC])
        xh, gx, ga = sb("xh", [DC, HALF]), sb("gx", [DC, HALF]), sb("ga", [DC, HALF])
        co, hh, ytmp = sb("co", [DC, HALF]), sb("hh", [2, DC, HALF]), sb("ytmp", [2, D])
        with nc.Block(no_gpsimd_drain=True) as block:

            @block.tensor
            def _(pe):
                mm = nc.tensor.matmul
                for half in range(2):
                    if half:
                        pe.wait_ge(s["xh_ready"], half)
                    for m in range(DC):
                        for c in range(DC):
                            mm(ps[:, m], w_x[:, c, m * P:(m + 1) * P], nT[:, c, half * HALF:(half + 1) * HALF], start=c == 0, stop=False)
                        last = mm(ps[:, m], pe_x[:, m * P:(m + 1) * P], E.c("pe")[0:16].unsqueeze(1).to_broadcast([16, HALF // P, P]), start=False, stop=True)
                    last.then_inc(s["xh_psum"], 1)
                    pe.wait_ge(s["xh_ready"], half + 1)
                    if half:
                        pe.wait_ge(s["gates_ready"], half)
                    for i, wg in enumerate((w_gx, w_ga)):
                        for m in range(DC):
                            for c in range(DC):
                                last = mm(ps[:, 2 + 2 * i + m], wg[:, c, m * P:(m + 1) * P], xh[:, c], start=c == 0, stop=c == DC - 1)
                    last.then_inc(s["gates_psum"], 1)
                for half in range(2):
                    pe.wait_ge(s["scan_done"], half + 1)
                    for t in range(HALF // P):
                        n = half * (HALF // P) + t
                        if n >= 2:
                            pe.wait_ge(s["x_done"], n - 1)
                        g = n
                        o = ps[:, 6 + n % 2, 0:D]
                        for c in range(DC):
                            mm(o, nT[:, c, g * P:(g + 1) * P], w_dx[:, c], start=c == 0, stop=False)
                        mm(o, E.c("pe")[0:16], pe_dx, start=False, stop=False)
                        for c in range(DC):
                            last = mm(o, hh[:, half, c, t * P:(t + 1) * P], w_o[:, c], start=False, stop=c == DC - 1)
                        last.then_inc(s["y_ready"], 1)

            @block.gpsimd
            def _(pool):
                power(E, pool, s, 0, keep[:], keep[:], 0.0, "half")

            @block.scalar
            def _(act):
                a = nc.scalar.activation
                a(expit[:], col("L3_attn_a_logit"), ACT.Sigmoid).then_inc(s["expit"], 1)
                for half in range(2):
                    act.wait_ge(s["gates_psum"], half + 1)
                    if half:
                        act.wait_ge(s["scan_done"], half)
                    for i, (dst, b) in enumerate(((gx, "L3_attn_b_gx"), (ga, "L3_attn_b_ga"))):
                        for m in range(DC):
                            last = a(dst[:, m], ps[:, 2 + 2 * i + m], ACT.Sigmoid, bias=col(b)[:, m:m + 1])
                    last.then_inc(s["gates_ready"], 1)
                    act.wait_ge(s["rest_ready"], half + 1)
                    a(co[:], co[:], ACT.Sqrt).then_inc(s["root_ready"], 1)

            @block.vector
            def _(dve):
                v = nc.vector
                link = chain(dve, s["dve_step"])
                dve.wait_ge(s["expit"], 1)
                link(v.tensor_tensor(keep[:], expit[:], expit[:], ALU.mult))
                v.tensor_scalar(keep[:], keep[:], -1.0, 1.0, ALU.mult, ALU.add).then_inc(s["var_ready"], 1)
                dve.wait_ge(s["power_ready"], 1)
                for half in range(2):
                    dve.wait_ge(s["xh_psum"], half + 1)
                    for m in range(DC):
                        last = v.tensor_scalar(xh[:, m], ps[:, m], col("L3_attn_b_x")[:, m:m + 1], keep[:, m:m + 1], ALU.add, ALU.mult)
                    last.then_inc(s["xh_ready"], 1)
                    dve.wait_ge(s["gates_ready"], half + 1)
                    for m in range(DC):
                        last = v.tensor_scalar(ga[:, m], ga[:, m], expit[:, m:m + 1], None, ALU.mult)
                    link(last)
                    link(v.tensor_tensor(co[:], ga[:], ga[:], ALU.mult))
                    v.tensor_scalar(co[:], co[:], -1.0, 1.0, ALU.mult, ALU.add).then_inc(s["rest_ready"], 1)
                    link(v.tensor_tensor(gx[:], gx[:], xh[:], ALU.mult))
                    dve.wait_ge(s["root_ready"], half + 1)
                    link(v.tensor_tensor(co[:], co[:], gx[:], ALU.mult))
                    for m in range(DC):
                        last = v.memset(ga[:, m].rearrange("p (b t) -> p b t", t=LQ)[:, :, 0:1], 0.0)
                    link(last)
                    for m in range(DC):
                        last = v.tensor_tensor_scan(hh[:, half, m], ga[:, m], co[:, m], 0.0, ALU.mult, ALU.add)
                    last.then_inc(s["scan_done"], 1)
                for n in range(NG):
                    dve.wait_ge(s["y_ready"], n + 1)
                    y = ytmp[:, n % 2]
                    link(v.tensor_tensor(y, ps[:, 6 + n % 2, 0:D], rows["b_dx"], ALU.add))
                    link(v.tensor_tensor(y, y, rows["b_o"], ALU.add))
                    v.scalar_tensor_tensor(E.x[:, n], y, 0.5, E.x[:, n], ALU.mult, ALU.add).then_inc(s["x_done"], 1)
                dve.wait_ge(s["x_done"], NG)
        end_round(nc, handles)


def prepare_softplus(E, out):
    nc = E.nc
    with ExitStack() as st:
        s, handles = signals(st, nc, "sp", "abs exp ln dve_step")
        a = st.enter_context(nc.sbuf_tensor("sp_a", [P, DC], F32))
        with nc.Block(no_gpsimd_drain=True) as block:

            @block.vector
            def _(dve):
                v = nc.vector
                link = chain(dve, s["dve_step"])
                v.scalar_tensor_tensor(a[:], E.col("temperature"), -1.0, E.col("temperature"), ALU.mult, ALU.max).then_inc(s["abs"], 1)
                link(v.tensor_scalar(out[:], E.col("temperature"), 0.0, None, ALU.max))
                dve.wait_ge(s["ln"], 1)
                link(v.tensor_tensor(out[:], out[:], a[:], ALU.add))

            @block.scalar
            def _(act):
                act.wait_ge(s["abs"], 1)
                nc.scalar.activation(a[:], a[:], ACT.Exp, scale=-1.0).then_inc(s["exp"], 1)
                act.wait_ge(s["exp"], 1)
                nc.scalar.activation(a[:], a[:], ACT.Ln, bias=E.c("one")).then_inc(s["ln"], 1)
        end_round(nc, handles)


def build(nc, A, only=None):
    with ExitStack() as st:
        def sb(name, shape, dt=F32):
            return st.enter_context(nc.sbuf_tensor(name, shape, dt))

        E = Core()
        E.nc, E.st, E.loads, E.bias_sem = nc, st, {}, None
        E.ps = st.enter_context(nc.psum_tensor("banks", [P, 8, 512], F32))
        E.x, E.h = sb("x_state", [P, NG, D]), sb("h_state", [P, NG, D])
        E.z = E.h
        E.ctx = sb("ctx_tiles", [P, 2, DC, CT])
        E.ctx_dram = A["ctx"]
        E.wA, E.wB, E.wC = sb("weights_a", [P, WA]), sb("weights_b", [P, WB]), sb("weights_c", [P, WC])
        E.rA, E.rB, E.rC = (sb(f"rows_{k}", [P, ROW, D]) for k in "abc")
        const, cols, small, short = sb("const", [P, CONST_W]), sb("cols", [P, COL_W]), sb("small", [P, SMALL_W]), sb("short", [P, SHORT_W])
        b2 = sb("expert_b2", [NE, 2, D])
        gamma_sb, decay = sb("gamma", [P, 4]), sb("decay", [P, 4, LQ])
        comb = sb("comb", [P, NG, NE])
        proj = sb("proj", [P, 8, P])
        E.cols = cols
        E.c = lambda n: const[:, CONST_AT[n][0]:sum(CONST_AT[n])]
        E.col = lambda n: cols[:, COL_AT[n][0]:sum(COL_AT[n])]
        E.small = lambda n: small[:, SMALL_AT[n][0]:sum(SMALL_AT[n])].rearrange("p (c n) -> p c n", c=DC)
        E.short = lambda n: short[:, SHORT_AT[n][0]:sum(SHORT_AT[n])]

        def cut(w, at, names, out=D):
            return [(w[:, at + i * DC * out:at + (i + 1) * DC * out].rearrange("p (c n) -> p c n", c=DC), chunked(A[n])) for i, n in enumerate(names)]

        def rows(r, at, names):
            i = ROWS.index(names[0])
            return [(r[:, at:at + len(names)], A["rows"][i:i + len(names)].rearrange("r d -> (r d)").partition_broadcast(P).rearrange("p (r d) -> p r d", d=D))]

        def expert0(w1, w2):
            return [(E.wA[:, 0:2 * FF].rearrange("p (c n) -> p c n", c=DC), chunked(A[w1][0])),
                    (E.wA[:, 2 * FF:4 * FF].rearrange("p (c n) -> p c n", c=FC), chunked(A[w2][0]))]

        L0x = cut(E.wA, 0, ["L0_xattn_Wk2", "L0_xattn_Wv2", "L0_xattn_Wq1", "L0_xattn_Wk1", "L0_xattn_Wv1"], 512)
        L0x_wo = E.wA[:, 5120:6144].rearrange("p (c n) -> p c n", c=4)
        L0a = cut(E.wC, 0, ["L0_attn_Wq", "L0_attn_Wk", "L0_attn_Wv", "L0_attn_Wg"])
        L1a = cut(E.wA, 4096, ["L1_attn_Wq", "L1_attn_Wk", "L1_attn_Wv", "L1_attn_Wo"])
        L1f = cut(E.wC, 0, ["L1_ffn_mix_w"])
        L2x = cut(E.wA, 4096, ["L2_xattn_Wq", "L2_xattn_Wk", "L2_xattn_Wv", "L2_xattn_Wo"])
        L2a = cut(E.wC, 0, ["L2_attn_Wq", "L2_attn_Wk", "L2_attn_Wv", "L2_attn_Wo"])
        L3x = cut(E.wB, 2048, ["L3_xattn_Wq", "L3_xattn_Wk", "L3_xattn_Wv", "L3_xattn_Wproj"])
        L3a = cut(E.wA, 3072, ["L3_attn_W_dx", "L3_attn_W_x", "L3_attn_W_gx", "L3_attn_W_ga", "L3_attn_W_o"])
        L3a_pe = [(E.wA[0:16, 5632 + i * D:5632 + (i + 1) * D], A[n]) for i, n in enumerate(("L3_attn_W_dx_pe", "L3_attn_W_x_pe"))]
        L3f = cut(E.wC, 0, ["L3_ffn_Wq", "L3_ffn_Wk", "L3_ffn_Wv", "L3_ffn_Wp"])
        ints = [(E.wA[:, i * 2 * HID:(i + 1) * 2 * HID].bitcast(I32).rearrange("p (c n) -> p c n", c=DC), chunked(A[n])) for i, n in enumerate(("w_gate", "w_up"))]
        ints.append((E.wB[:, 0:2 * HID].bitcast(I32).rearrange("p (c n) -> p c n", c=HID // P), chunked(A["w_down"])))

        def at(pairs):
            return [p[0] for p in pairs]

        fill(E, "proj", [(proj[:], 0.0)])
        first = [(const[:], A["const"]), (E.x[:], A["x"].rearrange("(g p) d -> p g d", p=P)), (cols[:], A["cols"]), (small[:], A["small"]),
                 (short[:], A["short"].partition_broadcast(P)), (E.ctx[:, 0], A["ctx"][0]), (b2[:], A["expert_b2"])]
        first += [(gamma_sb[LQ * i:LQ * (i + 1)], A["gamma"][i].partition_broadcast(LQ)) for i in range(4)]
        first += [(proj[16 * h:16 * h + 16, h], A["L2_attn_proj_mat"]) for h in range(8)]
        send_for(E, "first", first)
        send_for(E, "L0x", L0x + [(L0x_wo, chunked(A["L0_xattn_Wo"]))] + rows(E.rA, 0, ["L0_xattn_bo"]))
        send_for(E, "L0a", L0a + rows(E.rC, 0, ["L0_attn_bv"]))
        await_weights(E, "first")
        run = lambda n: only is None or n in only

        await_weights(E, "L0x")
        if run(0):
            wk2, wv2, wq1, wk1, wv1 = at(L0x)
            cross_attention(E, "l0x", 64, wq1, wk2, wv2, L0x_wo, {"bo": E.rA[:, 0]}, self_w=(wk1, wv1))
        await_weights(E, "L0a")
        send_for(E, "L0f", expert0("L0_w1", "L0_w2") + rows(E.rB, 0, ["L0_ffn_sb2"]))
        if run(1):
            prepare_decay(E, gamma_sb, decay)
            self_attention(E, "l0a", at(L0a), {"bv": E.rC[:, 0]}, bq=E.col("L0_attn_bq"), bk=E.col("L0_attn_bk"), rope="rot_pairs", decay=decay, gate_bias=E.col("L0_attn_bg"))
        await_weights(E, "L0f")
        if run(2):
            with nc.sbuf_tensor("l0f_nT", [P, DC, NG * P], F32) as nT:
                feature_major(E, "l0ft", nT, gating=(E.small("L0_gate"), E.short("gate_b"), "sigmoid", comb[:], b2[:, 0]), extra_bias=(E.rB[:, 0], 0.1))
                expert_mixture(E, "l0f", A["L0_w1"], A["L0_w2"], COL_AT["L0_ffn_b1_0"][0], comb, nT, ACT.Gelu, shared=0.1)
        send_for(E, "L1a", L1a + rows(E.rA, 4, ["L1_attn_bo"]))
        if run(3):
            decoder(E, A)
        await_weights(E, "L1a")
        send_for(E, "L1f", L1f + expert0("L1_w1", "L1_w2") + rows(E.rC, 0, ["L1_ffn_g1", "L1_ffn_be1", "L1_ffn_mix_b", "L1_ffn_g2", "L1_ffn_be2"]))
        if run(4):
            self_attention(E, "l1a", at(L1a), {"bo": E.rA[:, 4]}, rope="rot_halves", unit_norm=True)
        await_weights(E, "L1f")
        send_for(E, "L2x", L2x + rows(E.rA, 0, ["L2_xattn_bv", "L2_xattn_bo"]))
        if run(5):
            with nc.sbuf_tensor("l1f_nT", [P, DC, NG * P], F32) as nT:
                feature_major(E, "l1ft", nT, pre=(E.rC[:, 0], E.rC[:, 1], at(L1f)[0], E.rC[:, 2], E.rC[:, 3], E.rC[:, 4]),
                              gating=(E.small("L1_router"), None, "softmax", comb[:], b2[:, 1]))
                expert_mixture(E, "l1f", A["L1_w1"], A["L1_w2"], COL_AT["L1_ffn_b1_0"][0], comb, nT, ACT.Silu)
        await_weights(E, "L2x")
        send_for(E, "L2a", L2a + rows(E.rC, 0, ["L2_attn_bv", "L2_attn_bo"]))
        send_for(E, "L2f", ints)
        if run(6):
            with nc.sbuf_tensor("length", [P, NB], F32) as length, nc.sbuf_tensor("inverse", [P, NB], F32) as inverse, nc.sbuf_tensor("mask_s2", [NB, LK], I32) as m:
                send_for(E, "mask", [(m[:], A["mask_BxS2_if0"])])
                await_weights(E, "mask")
                prepare_lengths(E, m, length, inverse)
                cross_attention(E, "l2x", 16, *at(L2x), {"bv": E.rA[:, 0], "bo": E.rA[:, 1]}, bq=E.col("L2_xattn_bq"), bk=E.col("L2_xattn_bk"),
                                deform={"boff": E.short("boff"), "length": length, "inverse": inverse})
        await_weights(E, "L2a")
        send_for(E, "L3x", L3x + rows(E.rB, 0, ["L3_xattn_bv", "L3_xattn_bproj"]))
        if run(7):
            fourier_attention(E, at(L2a), {"bv": E.rC[:, 0], "bo": E.rC[:, 1]}, E.col("L2_attn_bq"), E.col("L2_attn_bk"), proj)
        await_weights(E, "L2f")
        send_for(E, "L3f", L3f + rows(E.rC, 0, ["L3_ffn_bv", "L3_ffn_bp"]))
        send_for(E, "L3a", L3a + L3a_pe + rows(E.rA, 0, ["L3_attn_b_dx", "L3_attn_b_o"]))
        if run(8):
            gate, up, down = [i[0].bitcast(F32) for i in ints]
            gated_mlp(E, list(zip((gate, up, down), at(ints))), [gate, up], down)
        await_weights(E, "L3x")
        if run(9):
            with ExitStack() as own:
                cw = [own.enter_context(nc.sbuf_tensor(f"centred{i}", [P, DC, D], F32)) for i in range(2)]
                cb = own.enter_context(nc.sbuf_tensor("centred_bias", [P, 4], F32))
                wq, wk, wv, wp = at(L3x)
                prepare_centred(E, (wq, wk), cw, (E.col("L3_xattn_bq"), E.col("L3_xattn_bkv")[:, 0:2]), cb)
                cross_attention(E, "l3x", 16, cw[0][:], cw[1][:], wv, wp, {"bv": E.rB[:, 0], "bo": E.rB[:, 1]}, bq=cb[:, 0:2], bk=cb[:, 2:4],
                                norm=[E.col(n) for n in ("q_gamma", "q_beta", "k_gamma", "k_beta")])
        await_weights(E, "L3a")
        if run(10):
            gated_recurrence(E, at(L3a) + at(L3a_pe), {"b_dx": E.rA[:, 0], "b_o": E.rA[:, 1]})
        await_weights(E, "L3f")
        if run(11):
            with nc.sbuf_tensor("softplus", [P, DC], F32) as sp:
                prepare_softplus(E, sp)
                self_attention(E, "l3f", at(L3f), {"bv": E.rC[:, 0], "bo": E.rC[:, 1]}, bq=E.col("L3_ffn_bq"), bk=E.col("L3_ffn_bk"),
                               query_scale=(E.col("L3_ffn_query_embedding"), sp), heads_gate=E.short("brs"))
        send_for(E, "out", [(A["out"].rearrange("(g p) d -> p g d", p=P), E.x[:])])
        await_weights(E, "out")


def arrays_of(inputs):
    a = {k: np.asarray(v) for k, v in inputs.items()}
    f = lambda x: np.ascontiguousarray(x)

    def columns(v):
        return np.asarray(v).reshape(-1, P).T

    a.update(sa={}, ca={})
    vec = {n: a[n] for n in COL_NAMES_DIRECT}
    for layer in range(NL):
        vec[f"sa_b{layer}"], vec[f"ca_b{layer}"], vec[f"L1_b1_{layer}"] = a["L1_xattn_sa_b"][layer], a["L1_xattn_ca_b"][layer], a["L1_xattn_b1"][layer]
    for e in range(NE):
        vec[f"L0_ffn_b1_{e}"], vec[f"L1_ffn_b1_{e}"] = a["L0_ffn_b1"][e], a["L1_ffn_b1"][e]
    vec["temperature"] = np.repeat(a["L3_ffn_temperature"].reshape(-1), 16)
    for n in ("q_gamma", "q_beta", "k_gamma", "k_beta"):
        vec[n] = np.tile(a[f"L3_xattn_{n}"], 8)
    small = {"L0_gate": a["L0_ffn_gate_w"].T, "L1_router": a["L1_ffn_router_w"], "Woff": a["L2_xattn_Woff"].T,
             "Wrs": np.concatenate([a["L3_ffn_Wr"], a["L3_ffn_Ws"]]).T}
    row = dict(a, L3_xattn_bv=a["L3_xattn_bkv"][D:])
    again = lambda w: np.concatenate([w, w[:1]])
    g, b = a["L1_xattn_ln_g"], a["L1_xattn_ln_b"]
    out = {
        "x": a["x"].reshape(NB * LQ, D),
        "ctx": again(a["ctx_1024"].reshape(NG, CT, DC, P).transpose(0, 3, 2, 1)),
        "const": np.concatenate(list(CONST.values()), 1),
        "cols": np.concatenate([columns(vec[n]) for n, _ in COLS], 1),
        "small": np.concatenate([small[n].reshape(DC, P, -1).transpose(1, 0, 2).reshape(P, -1) for n, _ in SMALL], 1),
        "short": np.concatenate([a["L2_xattn_boff"], a["L0_ffn_gate_b"], a["L3_ffn_br"], a["L3_ffn_bs"]]),
        "rows": np.stack([row[n] for n in ROWS]),
        "gamma": a["L0_attn_gamma"].reshape(4, 4).T,
        "expert_b2": np.stack([a["L0_ffn_b2"], a["L1_ffn_b2"]], 1),
        "L0_w1": np.concatenate([a["L0_ffn_w1"], a["L0_ffn_sw1"][None]]),
        "L0_w2": np.concatenate([a["L0_ffn_w2"], a["L0_ffn_sw2"][None]]),
        "L1_w1": again(a["L1_ffn_w1"]),
        "L1_w2": again(a["L1_ffn_w2"]),
        "sa_w": again(a["L1_xattn_sa_w"]),
        "ca_w": a["L1_xattn_ca_w"],
        "sa_rows": again(np.stack([a["L1_xattn_sa_b"][:, 2], a["L1_xattn_sa_b"][:, 3], g[:, 0], b[:, 0]], 1)),
        "ca_rows": np.stack([a["L1_xattn_ca_b"][:, 2], a["L1_xattn_ca_b"][:, 3], g[:, 1], b[:, 1]], 1),
        "mlp_rows": np.stack([a["L1_xattn_b2"], g[:, 2], b[:, 2]], 1),
        "w_gate": a["L2_ffn_w_gate"].T, "w_up": a["L2_ffn_w_up"].T, "w_down": a["L2_ffn_w_down"].T,
        "L3_attn_W_dx": a["L3_attn_W_dx"][:D], "L3_attn_W_x": a["L3_attn_W_x"][:D],
        "L3_attn_W_dx_pe": a["L3_attn_W_dx"][D:], "L3_attn_W_x_pe": a["L3_attn_W_x"][D:],
        "L3_xattn_Wq": a["L3_xattn_Wq"], "L3_xattn_Wk": a["L3_xattn_Wkv"][:D],
        "L3_xattn_Wv": a["L3_xattn_Wkv"][D:].T, "L3_xattn_Wproj": a["L3_xattn_Wproj"].T,
    }
    for i, n in enumerate(("Wq", "Wk", "Wv")):
        out[f"L1_attn_{n}"] = a["L1_attn_Wqkv"][:, i * D:(i + 1) * D]
    for n in ("mask_BxSxS_ik0", "mask_BxS2_if0", "L0_xattn_Wq1", "L0_xattn_Wk1", "L0_xattn_Wv1", "L0_xattn_Wk2", "L0_xattn_Wv2", "L0_xattn_Wo",
              "L1_xattn_w1", "L1_xattn_w2", "L1_attn_Wo", "L1_ffn_mix_w", "L2_attn_proj_mat", "L3_attn_W_gx", "L3_attn_W_ga", "L3_attn_W_o"):
        out[n] = a[n]
    for block, names in (("L0_attn", "Wq Wk Wv Wg"), ("L2_xattn", "Wq Wk Wv Wo"), ("L2_attn", "Wq Wk Wv Wo"), ("L3_ffn", "Wq Wk Wv Wp")):
        for n in names.split():
            out[f"{block}_{n}"] = a[f"{block}_{n}"].T
    return {k: f(v) for k, v in out.items()}


COL_NAMES_DIRECT = [n for n, _ in COLS if n[:2] in ("L0", "L2", "L3") and "_b1_" not in n]


def kernel(**inputs):
    import concourse.bacc as bacc
    from concourse.bass_utils import run_bass_kernel_spmd

    arrays = arrays_of(inputs)
    nc = bacc.Bacc("TRN2", target_bir_lowering=False, num_devices=1)
    A = {k: nc.dram_tensor(f"in_{k}", v.shape, mybir.dt.from_np(v.dtype), kind="ExternalInput").ap() for k, v in arrays.items()}
    A["out"] = nc.dram_tensor("out", (NB * LQ, D), F32, kind="ExternalOutput").ap()
    build(nc, A)
    r = run_bass_kernel_spmd(nc, [{f"in_{k}": v for k, v in arrays.items()}], core_ids=[0])
    return r.results[0]["out"].reshape(NB, LQ, D)
```

```python
from contextlib import ExitStack

import numpy as np

import concourse.bass as bass
from concourse import mybir

F32 = mybir.dt.float32
I32 = mybir.dt.int32
ALU = mybir.AluOpType
ACT = mybir.ActivationFunctionType
AX = mybir.AxisListType

P = 128
NB = 32
LQ = 32
LK = 257
D = 256
DC = D // P
GB = P // LQ
NG = NB // GB
CT = GB * LK
VT = -(-CT // P)
FF = 1024
FC = FF // P
NE = 8
NL = 6
NK = 5
HID = 768



def constant_arrays():
    p = np.arange(P)
    f = np.float32
    inv = 1.0 / 10000.0 ** (np.arange(8) / 8.0)
    ang = (np.arange(LQ, dtype=f)[None, :] * inv.astype(f)[p % 8][:, None]).astype(f)
    rot_pairs = np.zeros((P, P), f)
    rot_halves = np.zeros((P, P), f)
    for o in range(P):
        if o % 2 == 0:
            rot_pairs[o + 1, o] = -1
        else:
            rot_pairs[o - 1, o] = 1
        if o % 16 < 8:
            rot_halves[o + 8, o] = -1
        else:
            rot_halves[o - 8, o] = 1
    div = np.exp(np.arange(0, 16, 2) * (-np.log(10000.0) / 16))
    pe = np.zeros((16, LQ))
    pe[0::2] = np.sin(np.arange(LQ)[None, :] * div[:, None])
    pe[1::2] = np.cos(np.arange(LQ)[None, :] * div[:, None])
    pe_rows = np.zeros((P, P), f)
    pe_rows[:16] = np.tile(pe / 100.0, (1, GB))
    return {
        "ident": np.eye(P, dtype=f),
        "head_ones": (p[:, None] // 16 == p[None, :] // 16).astype(f),
        "rot_pairs": rot_pairs,
        "rot_halves": rot_halves,
        "cos": np.cos(ang).astype(f),
        "sin": np.sin(ang).astype(f),
        "qmask16": (((p[:, None] // 16) % 4 == np.arange(4)) * 0.25).astype(f),
        "pairmask": ((p[:, None] // 16) % 2 == np.arange(2)).astype(f),
        "headmask": (p[:, None] // 16 == np.arange(8)).astype(f),
        "qmask8": ((p[:, None] // 16 == np.arange(8)) * 0.25).astype(f),
        "qmask64": (((p[:, None, None] // 64) + 2 * np.arange(2)[:, None] == np.arange(4)) * 0.125).astype(f).reshape(P, 8),
        "rowmask": (p[:, None] // LQ == np.arange(4)).astype(f),
        "pick": (p[:, None] % LQ == np.arange(LQ)).astype(f),
        "key_index": np.tile(np.arange(LK + 1, dtype=f), (P, 1)),
        "loc_base": ((p[:, None] % LQ) + np.arange(NK) - 3).astype(f),
        "lag": np.maximum(p[:, None] % LQ - np.arange(LQ), 0).astype(f),
        "same_seq": (p[:, None] // LQ == p[None, :] // LQ).astype(f),
        "pe": pe_rows,
        "minus_half": np.full((P, NG), -0.5, f),
        "half": np.full((P, NG), 0.5, f),
        "eps5": np.full((P, 1), 1e-5, f),
        "eps6": np.full((P, 1), 1e-6, f),
        "one": np.ones((P, 1), f),
        "zero": np.zeros((P, 1), f),
        "rank": np.tile((NE - np.arange(NE)).astype(f), (P, 1)),
        "centre": np.eye(P, dtype=f) - (p[:, None] // 16 == p[None, :] // 16).astype(f) / 16,
    }


CONST = constant_arrays()


def offsets(widths):
    at, out = 0, {}
    for name, w in widths:
        out[name] = (at, w)
        at += w
    return out, at


CONST_AT, CONST_W = offsets([(k, v.shape[1]) for k, v in CONST.items()])

COLS = [("L0_attn_bq", 2), ("L0_attn_bk", 2), ("L0_attn_bg", 2), 
        ("L2_xattn_bk", 2), ("L2_xattn_bq", 2), ("L2_attn_bq", 2), ("L2_attn_bk", 2),
        ("L3_xattn_bq", 2), ("L3_xattn_bkv", 4), ("L3_attn_a_logit", 2), ("L3_attn_b_x", 2), ("L3_attn_b_gx", 2),
        ("L3_attn_b_ga", 2), ("L3_ffn_bq", 2), ("L3_ffn_bk", 2), ("L3_ffn_query_embedding", 2), ("temperature", 2)]
COLS += [(f"sa_b{layer}", 8) for layer in range(NL)] + [(f"ca_b{layer}", 8) for layer in range(NL)]
COLS += [(f"L0_ffn_b1_{e}", 8) for e in range(NE)] + [("L0_ffn_sb1", 8)] + [(f"L1_ffn_b1_{e}", 8) for e in range(NE)]
COLS += [(f"L1_b1_{layer}", 8) for layer in range(NL)]
COLS += [("q_gamma", 1), ("q_beta", 1), ("k_gamma", 1), ("k_beta", 1)]
COL_AT, COL_W = offsets(COLS)
SMALL = [("L0_gate", 2 * NE), ("L1_router", 2 * NE), ("Woff", 2 * 80), ("Wrs", 2 * 17)]
SMALL_AT, SMALL_W = offsets(SMALL)
SHORT = [("boff", 80), ("gate_b", NE), ("brs", 17)]
SHORT_AT, SHORT_W = offsets(SHORT)
ROWS = ["L0_xattn_bo", "L0_attn_bv", "L0_ffn_sb2", "L1_attn_bo", "L1_ffn_g1", "L1_ffn_be1", "L1_ffn_mix_b", "L1_ffn_g2", "L1_ffn_be2",
        "L2_xattn_bv", "L2_xattn_bo", "L2_attn_bv", "L2_attn_bo", "L3_xattn_bv", "L3_xattn_bproj", "L3_attn_b_dx", "L3_attn_b_o",
        "L3_ffn_bv", "L3_ffn_bp"]
ROW = 5
WA, WB, WC = 6144, 4096, 2048


class Core:
    pass


def signals(st, nc, tag, names):
    made = {n: st.enter_context(nc.semaphore(f"{tag}_{n}")) for n in names.split()}
    return made, list(made.values())


def end_round(nc, handles):
    nums = sorted(h.num for h in handles)
    at = 0
    while at < len(nums):
        end = at
        while end + 1 < len(nums) and nums[end + 1] == nums[end] + 1:
            end += 1
        nc.gpsimd.sem_clear(range(nums[at], nums[end] + 1))
        at = end + 1
    nc.all_engine_barrier(sem_only=True)


def chain(eng, sem):
    count = [0]

    def link(ins, behind=0):
        count[0] += 1
        ins.then_inc(sem, 1)
        if count[0] > behind:
            eng.wait_ge(sem, count[0] - behind)
    return link


def bc(ap, shape):
    return ap.to_broadcast(shape)


def layer_norm(eng, link, v, s, n, out, x, stats):
    link(v.bn_stats(stats[:, 0:6], x))
    v.bn_aggr(stats[:, 6:8], stats[:, 0:6]).then_inc(s["var_ready"], 1)
    eng.wait_ge(s["power_ready"], n + 1)
    return v.tensor_scalar(out, x, stats[:, 6:7], stats[:, 8:9], ALU.subtract, ALU.mult)


def power(E, pool, s, n, out, x, add, exponent="minus_half"):
    pool.wait_ge(s["var_ready"], n + 1)
    E.nc.gpsimd.tensor_scalar(out, x, add, None, ALU.add).then_inc(s["added_eps"], 1)
    pool.wait_ge(s["added_eps"], n + 1)
    e = E.c(exponent)[:, 0:out.free_size()]
    if len(out.shape) == 3:
        e = e.unsqueeze(2)
    E.nc.gpsimd.tensor_tensor(out, out, e, ALU.pow).then_inc(s["power_ready"], 1)


def await_weights(E, name):
    sem, n = E.loads[name]
    E.nc.sync.wait_ge(sem, 16 * n)
    E.nc.sync.sem_clear(sem)
    E.nc.all_engine_barrier(sem_only=True)


def send_for(E, name, pairs):
    if name not in E.loads:
        E.loads[name] = (E.st.enter_context(E.nc.semaphore(f"{name}_weights")), len(pairs))
    for dst, src in pairs:
        E.nc.sync.dma_start(dst, src).then_inc(E.loads[name][0], 16)


def chunked(w):
    return w.rearrange("(c p) n -> p c n", p=P)


def fill(E, tag, pairs):
    nc = E.nc
    with ExitStack() as st:
        s, handles = signals(st, nc, tag + "_fill", "filled")
        with nc.Block(no_gpsimd_drain=True) as block:

            @block.vector
            def _(dve):
                for ap, value in pairs:
                    nc.vector.memset(ap, value).then_inc(s["filled"], 1)
                dve.wait_ge(s["filled"], len(pairs))
        end_round(nc, handles)


def joint_attention(E, tag, wq, wk, wv, wo, own_w, rows):
    nc, ps = E.nc, E.ps
    dh = 64
    M = 8 * dh // P
    F = 4 * dh
    U = GB
    KS = LK + LQ
    NCH = 4
    PW = NCH * P
    EXPS = 4
    ROUND = 2

    jobs = [("n", None, "act"), ("q", None, "dve")]
    jobs += [("k1", None, "act"), ("v1", None, "dve")]
    for j in range(GB):
        jobs += [("K", (m, j), "act") for m in range(M)]
        jobs += [("V", i, "dve") for i in range(2 * j, 2 * j + 2 + (j == GB - 1))]
    J = len(jobs)
    per = {e: sum(k[2] == e for k in jobs) for e in ("dve", "act")}

    def evacuated(n):
        e = jobs[n % J][2]
        return e, (n // J) * per[e] + sum(k[2] == e for k in jobs[:n % J + 1])

    where = {(k, a): i for i, (k, a, _) in enumerate(jobs)}

    with ExitStack() as st:
        s, handles = signals(st, nc, tag, "n_ready job_done evac_dve evac_act scores_done max_ready exp_done "
                             "transposed copied_dve copied_act pv_done heads_ready picked attn_copied y_ready x_done "
                             "ctx1 ctx0 dve_step var_ready added_eps power_ready")

        def sb(name, shape):
            return st.enter_context(nc.sbuf_tensor(f"{tag}_{name}", shape, F32))

        n_sb = sb("n", [P, D])
        stats = sb("stats", [P, 9])
        nT = sb("nT", [P, DC, P])
        qT = sb("qT", [P, M, P])
        qblk = sb("qblk", [P, M, GB, 4, LQ])
        KT = sb("KT", [P, M, GB, KS])
        V = sb("V", [P, VT, M * P])
        probs = sb("probs", [P, GB, 2, PW])
        pT = sb("pT", [P, 2, 2, NCH * P])
        negmax = sb("negmax", [P, 2, 2])
        sums = sb("sums", [P, 2, 2])
        own_sums = sb("own_sums", [P, 2, 2])
        rmask = sb("rmask", [P, 2, 4])
        heads = sb("heads", [P, 2, 2, F])
        attnT = sb("attnT", [P, M, P])
        ytmp = sb("ytmp", [P, D])
        v1 = sb("v1", [P, M * P])

        fill(E, tag, [(probs[:], 0.0)])

        with nc.Fori(0, NG // ROUND) as pair:
            g0 = pair * ROUND
            with nc.Block(no_gpsimd_drain=True) as block:

                @block.sync
                def _(sp):
                    sp.dma_start(E.ctx[:, 1], E.ctx_dram[bass.ds(g0 + 1, 1)].rearrange("a p c n -> (a p) c n")).then_inc(s["ctx1"], 16)
                    last_read = max(i for i, k in enumerate(jobs) if k[0] in ("K", "V"))
                    sp.wait_ge(s["job_done"], last_read + 1)
                    sp.dma_start(E.ctx[:, 0], E.ctx_dram[bass.ds(g0 + 2, 1)].rearrange("a p c n -> (a p) c n")).then_inc(s["ctx0"], 16)
                    sp.wait_ge(s["ctx0"], 16)

                def wait_evacuated(eng, n):
                    e, c = evacuated(n)
                    eng.wait_ge(s["evac_dve"] if e == "dve" else s["evac_act"], c)

                @block.tensor
                def _(pe):
                    mm, tr = nc.tensor.matmul, nc.tensor.transpose
                    for gi in range(ROUND):
                        cx = E.ctx[:, gi]
                        for i, (kind, arg, _e) in enumerate(jobs):
                            n = gi * J + i
                            o = ps[:, n % 4]
                            if n >= 4:
                                wait_evacuated(pe, n - 4)
                            if gi and i == 0:
                                pe.wait_ge(s["exp_done"], EXPS * gi * U)
                            if kind == "n":
                                pe.wait_ge(s["n_ready"], gi + 1)
                                for c in range(DC):
                                    last = tr(o[:, c * P:(c + 1) * P], n_sb[:, c * P:(c + 1) * P], E.c("ident"))
                            elif kind in ("q", "k1"):
                                wait_evacuated(pe, gi * J)
                                w = wq if kind == "q" else own_w[0]
                                for m in range(M):
                                    for c in range(DC):
                                        last = mm(o[:, m * P:(m + 1) * P], w[:, c, m * P:(m + 1) * P], nT[:, c], start=c == 0, stop=c == DC - 1)
                            elif kind == "v1":
                                for c in range(DC):
                                    last = mm(o[:, 0:M * P], nT[:, c], own_w[1][:, c], start=c == 0, stop=c == DC - 1)
                            elif kind == "K":
                                m, j = arg
                                if gi == 1 and (m, j) == (0, 0):
                                    pe.wait_ge(s["ctx1"], 16)
                                for c in range(DC):
                                    last = mm(o[:, 0:LK], wk[:, c, m * P:(m + 1) * P], cx[:, c, j * LK:(j + 1) * LK], start=c == 0, stop=c == DC - 1)
                            elif kind == "V":
                                w = min(P, CT - arg * P)
                                for c in range(DC):
                                    last = mm(o[0:w, 0:M * P], cx[:, c, arg * P:arg * P + w], wv[:, c], start=c == 0, stop=c == DC - 1)
                            last.then_inc(s["job_done"], 1)

                        def scores(u):
                            j = u
                            k = gi * U + u
                            if u < 2:
                                wait_evacuated(pe, gi * J + J - 1)
                                wait_evacuated(pe, gi * J + max(i for i in range(J) if jobs[i][2] == "act"))
                            else:
                                pe.wait_ge(s["exp_done"], EXPS * (k - 1))
                            for t in range(2):
                                o = ps[:, 2 * (k % 2) + t]
                                for i in range(2):
                                    c = 2 * t + i
                                    last = mm(o[:, 0:KS], qblk[:, c, j].rearrange("p a b -> p (a b)"), KT[:, c, j], start=i == 0, stop=i == 1)
                            last.then_inc(s["scores_done"], 1)

                        def transposes(u):
                            j = u
                            k = gi * U + u
                            pe.wait_ge(s["exp_done"], EXPS * (k + 1))
                            if k:
                                pe.wait_ge(s["copied_dve"], k)
                                pe.wait_ge(s["copied_act"], k)
                            for t in range(2):
                                for c in range(NCH):
                                    last = tr(ps[:, 4 + t, c * P:(c + 1) * P], probs[:, j, t, c * P:(c + 1) * P], E.c("ident"))
                            last.then_inc(s["transposed"], 1)

                        def values(u):
                            j = u
                            k = gi * U + u
                            pe.wait_ge(s["copied_dve"], k + 1)
                            pe.wait_ge(s["copied_act"], k + 1)
                            if k:
                                pe.wait_ge(s["heads_ready"], k)
                            if u == 0 and gi:
                                pe.wait_ge(s["x_done"], gi)
                            for t in range(2):
                                f = t * F
                                o = ps[:, 6, t * F:(t + 1) * F]
                                for c in range(3):
                                    w = P if c < 2 else j + 1
                                    last = mm(o, pT[0:w, k % 2, t, c * P:(c + 1) * P], V[0:w, 2 * j + c, f:f + F], start=c == 0, stop=False)
                                last = mm(o, pT[:, k % 2, t, 3 * P:4 * P], v1[:, f:f + F], start=False, stop=True)
                            last.then_inc(s["pv_done"], 1)

                        def pick(u):
                            j = u
                            k = gi * U + u
                            pe.wait_ge(s["heads_ready"], k + 1)
                            if u == 0 and gi:
                                pe.wait_ge(s["attn_copied"], gi)
                            for i in range(2 * F // P):
                                c = i
                                w = heads[:, k % 2].rearrange("p t f -> p (t f)")[:, i * P:(i + 1) * P]
                                last = mm(ps[:, 7, c * P + j * LQ:c * P + (j + 1) * LQ], w, E.c("pick"), start=True, stop=True)
                            last.then_inc(s["picked"], 1)

                        for k in range(U + 3):
                            if k < U:
                                scores(k)
                            if 0 <= k - 1 < U:
                                transposes(k - 1)
                            if 0 <= k - 2 < U:
                                values(k - 2)
                            if 0 <= k - 3 < U:
                                pick(k - 3)
                        pe.wait_ge(s["attn_copied"], gi + 1)
                        for c in range(M):
                            last = mm(ps[:, 6, 0:D], attnT[:, c], wo[:, c], start=c == 0, stop=c == M - 1)
                        last.then_inc(s["y_ready"], 1)

                @block.vector
                def _(dve):
                    v = nc.vector
                    link = chain(dve, s["dve_step"])

                    def block_diagonal(q):
                        for m in range(M):
                            mask = E.c("qmask64")[:, (m % 2) * 4:(m % 2) * 4 + 4]
                            last = v.tensor_tensor(
                                qblk[:, m], q[:, m].rearrange("p (j q) -> p j q", j=GB).unsqueeze(2).to_broadcast([P, GB, 4, LQ]),
                                mask.unsqueeze(1).unsqueeze(3).to_broadcast([P, GB, 4, LQ]), ALU.mult)
                        return last

                    for gi in range(ROUND):
                        xg = E.x[:, bass.ds(g0 + gi, 1)].rearrange("p a d -> p (a d)")
                        layer_norm(dve, link, v, s, gi, n_sb[:], xg, stats).then_inc(s["n_ready"], 1)
                        for i, (kind, arg, e) in enumerate(jobs):
                            if e != "dve":
                                continue
                            n = gi * J + i
                            o = ps[:, n % 4]
                            dve.wait_ge(s["job_done"], n + 1)
                            if kind == "q":
                                q2 = qT[:].rearrange("p m t -> p (m t)")
                                link(v.tensor_copy(q2, o[:, 0:M * P]))
                                last = block_diagonal(qT)
                            elif kind in ("V", "v1"):
                                w = min(P, CT - arg * P) if kind == "V" else P
                                dst = V[0:w, arg] if kind == "V" else v1[:]
                                last = v.tensor_copy(dst, o[0:w, 0:M * P])
                            last.then_inc(s["evac_dve"], 1)

                        def head_sums(u):
                            k = gi * U + u
                            dve.wait_ge(s["exp_done"], EXPS * (k + 1))
                            if k:
                                dve.wait_ge(s["heads_ready"], k)
                            link(v.tensor_tensor(sums[:, k % 2], sums[:, k % 2], own_sums[:, k % 2], ALU.add))
                            link(v.reciprocal(sums[:, k % 2], sums[:, k % 2]))
                            link(v.tensor_tensor(rmask[:], E.c("rowmask").unsqueeze(1).to_broadcast([P, 2, 4]),
                                                 sums[:, k % 2].unsqueeze(2).to_broadcast([P, 2, 4]), ALU.mult))
                            dve.wait_ge(s["pv_done"], k + 1)
                            if k >= 2:
                                dve.wait_ge(s["picked"], k - 1)
                            v.tensor_tensor(heads[:, k % 2].rearrange("p t (h d) -> p (t h) d", h=4),
                                            ps[:, 6, 0:2 * F].rearrange("p (a d) -> p a d", d=dh),
                                            rmask[:].rearrange("p t h -> p (t h)").unsqueeze(2).to_broadcast([P, 8, dh]), ALU.mult).then_inc(s["heads_ready"], 1)

                        for k in range(U + 2):
                            if k < U:
                                K = gi * U + k
                                dve.wait_ge(s["scores_done"], K + 1)
                                v.tensor_reduce(negmax[:, K % 2], ps[:, 2 * (K % 2):2 * (K % 2) + 2, 0:KS], AX.X, ALU.max, negate=True).then_inc(s["max_ready"], 1)
                            if 0 <= k - 1 < U:
                                K = gi * U + k - 1
                                dve.wait_ge(s["transposed"], K + 1)
                                if K >= 2:
                                    dve.wait_ge(s["pv_done"], K - 1)
                                v.tensor_copy(pT[:, K % 2, 1], ps[:, 5, 0:NCH * P]).then_inc(s["copied_dve"], 1)
                            if 0 <= k - 2 < U:
                                head_sums(k - 2)
                        dve.wait_ge(s["y_ready"], gi + 1)
                        xg = E.x[:, bass.ds(g0 + gi, 1)].rearrange("p a d -> p (a d)")
                        link(v.tensor_tensor(ytmp[:], ps[:, 6, 0:D], rows["bo"], ALU.add))
                        v.tensor_tensor(xg, ytmp[:], xg, ALU.add).then_inc(s["x_done"], 1)

                @block.gpsimd
                def _(pool):
                    for gi in range(ROUND):
                        power(E, pool, s, gi, stats[:, 8:9], stats[:, 7:8], 1e-5)

                @block.scalar
                def _(act):
                    a = nc.scalar.activation
                    for gi in range(ROUND):
                        for i, (kind, arg, e) in enumerate(jobs):
                            n = gi * J + i
                            o = ps[:, n % 4]
                            if e != "act":
                                continue
                            act.wait_ge(s["job_done"], n + 1)
                            if kind == "n":
                                last = nc.scalar.copy(nT[:].rearrange("p c t -> p (c t)"), o[:, 0:D])
                            elif kind == "k1":
                                last = nc.scalar.copy(KT[:, :, :, LK:KS], o[:, 0:M * P].rearrange("p (m j q) -> p m j q", m=M, j=GB))
                            else:
                                m, j = arg
                                last = nc.scalar.copy(KT[:, m, j, 0:LK], o[:, 0:LK])
                            last.then_inc(s["evac_act"], 1)
                        for k in range(U + 1):
                            if k < U:
                                K = gi * U + k
                                j = k % GB
                                act.wait_ge(s["max_ready"], K + 1)
                                if K >= GB:
                                    act.wait_ge(s["transposed"], K - GB + 1)
                                if K >= 2:
                                    act.wait_ge(s["heads_ready"], K - 1)
                                for t in range(2):
                                    a(probs[:, j, t, j:j + LK], ps[:, 2 * (K % 2) + t, 0:LK], ACT.Exp,
                                      bias=negmax[:, K % 2, t:t + 1], accum_out=sums[:, K % 2, t:t + 1]).then_inc(s["exp_done"], 1)
                                    a(probs[:, j, t, 3 * P + LQ * j:3 * P + LQ * (j + 1)], ps[:, 2 * (K % 2) + t, LK:KS], ACT.Exp,
                                      bias=negmax[:, K % 2, t:t + 1], accum_out=own_sums[:, K % 2, t:t + 1]).then_inc(s["exp_done"], 1)
                            if 0 <= k - 1 < U:
                                K = gi * U + k - 1
                                act.wait_ge(s["transposed"], K + 1)
                                if K >= 2:
                                    act.wait_ge(s["pv_done"], K - 1)
                                nc.scalar.copy(pT[:, K % 2, 0], ps[:, 4, 0:NCH * P]).then_inc(s["copied_act"], 1)
                        act.wait_ge(s["picked"], (gi + 1) * U)
                        nc.scalar.copy(attnT[:].rearrange("p c t -> p (c t)"), ps[:, 7, 0:M * P]).then_inc(s["attn_copied"], 1)

            end_round(nc, handles)


def context_attention(E, tag, wq, wk, wv, wo, rows, bq, bk, norm=None, deform=None, source=None, finish="residual"):
    nc, ps = E.nc, E.ps
    U = DC * GB
    ROUND = 2
    KC = 3
    PV, JOB = 4, 5
    JB = 8 - JOB
    L = 1 if deform or norm else 0
    src = E.x if source is None else source

    jobs = [("n", None, "act"), ("q", None, "dve")]
    if norm:
        jobs += [("qvar", None, "dve")]
    if deform:
        jobs += [("off", None, "dve")]
    for j in range(GB):
        jobs += [("K", (m, j), "act") for m in range(DC)]
        if norm and j:
            jobs += [("kvar", (m, j - 1), "act") for m in range(DC)]
    if norm:
        jobs += [("kvar", (m, GB - 1), "act") for m in range(DC)]
    jobs += [("V", i, "dve") for i in range(VT)]
    J = len(jobs)
    per = {e: sum(k[2] == e for k in jobs) for e in ("dve", "act")}
    where = {(k, a): i for i, (k, a, _) in enumerate(jobs)}
    starts = [min(J, u * -(-J // (U - 1))) for u in range(U + 1)]
    starts = [i + (0 < i < J and jobs[i][0] == "kvar" and jobs[i][1][0] == 1) for i in starts]

    with ExitStack() as st:
        s, handles = signals(st, nc, tag, "n_ready job_done evac_dve evac_act scores_done scores_used max_ready exp_done probs_ready "
                             "transposed copied_dve copied_act pv_done pv_used heads_ready y_ready x_done "
                             "ctx1 ctx0 dve_step act_step norm_sq soft_ready hats logs rstd_ready keys_ready var_ready added_eps power_ready zeroed")

        def sb(name, shape):
            return st.enter_context(nc.sbuf_tensor(f"{tag}_{name}", shape, F32))

        n_sb, stats, nT, qT = sb("n", [P, D]), sb("stats", [P, 9]), sb("nT", [P, DC, P]), sb("qT", [P, DC, P])
        qblk = sb("qblk", [P, 2, DC, GB, 8 * LQ])
        KT, V = sb("KT", [P, 2, DC, CT]), sb("V", [P, 2, VT, D])
        probs, pT = sb("probs", [P, GB, 2, KC * P]), sb("pT", [P, 2, KC, 2 * P])
        negmax, sums = sb("negmax", [P, 2, 2]), sb("sums", [P, 2, 2])
        own, attnT, ytmp = sb("own", [P, 8, LQ]), sb("attnT", [P, DC, P]), sb("ytmp", [P, D])
        if norm:
            qsq, qrs = sb("qsq", [P, D]), sb("qrs", [P, D])
            sq, rstd = sb("sq", [P, 2, DC, LK]), sb("rstd", [P, DC, LK])
        if deform:
            qrep, offb = sb("qrep", [P, DC, GB, 4, LQ]), sb("offb", [P, GB, 80])
            loc, t1, t2 = sb("loc", [P, GB, 4, NK]), sb("t1", [P, GB, 4, NK]), sb("t2", [P, 2, GB, 4, NK])
            S_sb = sb("S_sb", [P, 2, 2, LK])
            prod = deform["room"][2].rearrange("p (a k) -> p a k", a=2)
            hat = sb("hat", [P, 2, NK * LK])
            hat = [[r.rearrange("p (q k) -> p q k", q=NK) for r in pair] for pair in ((hat[:, 0], hat[:, 1]), deform["room"][:2])]
            sc, att = sb("sc", [P, 2, 8]), sb("att", [P, 2, 2, 8])

        def block(g0, tiles, slots):
            units = tiles * U

            def at(it):
                if not tiles:
                    k, lo, hi = 0, 0, J
                else:
                    k = it // U
                    lo, hi = starts[it % U:it % U + 2]
                if k >= len(slots):
                    return []
                return [(k * J + i, *slots[k], *jobs[i]) for i in range(lo, hi)]

            steps = units + 3 + L if tiles else 1

            def wait_evacuated(eng, n):
                e = jobs[n % J][2]
                eng.wait_ge(s["evac_" + e], (n // J) * per[e] + sum(k[2] == e for k in jobs[:n % J + 1]))

            def wait_all_evacuated(eng, k):
                for e in ("dve", "act"):
                    eng.wait_ge(s["evac_" + e], (k + 1) * per[e])

            def load(sp, half, tile, sem):
                sp.dma_start(E.ctx[:, half], E.ctx_dram[bass.ds(tile, 1)].rearrange("a p c n -> (a p) c n")).then_inc(s[sem], 16)

            with nc.Block(no_gpsimd_drain=True) as blk:

                @blk.sync
                def _(sp):
                    if not tiles:
                        load(sp, 1, 1, "ctx1")
                        sp.wait_ge(s["ctx1"], 16)
                        return
                    load(sp, 0, g0 + 2, "ctx0")
                    if len(slots) > 1:
                        sp.wait_ge(s["job_done"], J)
                        load(sp, 1, g0 + 3, "ctx1")
                        sp.wait_ge(s["ctx1"], 16)
                    sp.wait_ge(s["ctx0"], 16)

                @blk.tensor
                def _(pe):
                    mm, tr = nc.tensor.matmul, nc.tensor.transpose

                    def job(n, tile, par, kind, arg, e):
                        k = n // J
                        o = ps[:, JOB + n % JB]
                        cx = E.ctx[:, par]
                        if n >= JB:
                            wait_evacuated(pe, n - JB)
                        if kind == "n":
                            pe.wait_ge(s["n_ready"], k + 1)
                            for c in range(DC):
                                last = tr(o[:, c * P:(c + 1) * P], n_sb[:, c * P:(c + 1) * P], E.c("ident"))
                        elif kind == "q":
                            wait_evacuated(pe, k * J)
                            for m in range(DC):
                                for c in range(DC):
                                    last = mm(o[:, m * P:(m + 1) * P], wq[:, c, m * P:(m + 1) * P], nT[:, c], start=c == 0, stop=c == DC - 1)
                        elif kind == "qvar":
                            wait_evacuated(pe, k * J + where["q", None])
                            last = mm(o[:, 0:D], E.c("head_ones"), qsq[:], start=True, stop=True)
                        elif kind == "off":
                            wait_evacuated(pe, k * J + where["q", None])
                            for j in range(GB):
                                for c in range(DC):
                                    last = mm(o[:, j * 80:(j + 1) * 80], qrep[:, c, j].rearrange("p a b -> p (a b)"), E.small("Woff")[:, c], start=c == 0, stop=c == DC - 1)
                        elif kind == "K":
                            m, j = arg
                            if tiles and k == 1 and (m, j) == (0, 0):
                                pe.wait_ge(s["ctx0"], 16)
                            for c in range(DC):
                                last = mm(o[:, 0:LK], wk[:, c, m * P:(m + 1) * P], cx[:, c, j * LK:(j + 1) * LK], start=c == 0, stop=c == DC - 1)
                        elif kind == "kvar":
                            m, j = arg
                            pe.wait_ge(s["norm_sq"], (k * GB + j) * DC + m + 1)
                            last = mm(o[:, 0:LK], E.c("head_ones"), sq[:, j % 2, m], start=True, stop=True)
                        elif kind == "V":
                            w = min(P, CT - arg * P)
                            for c in range(DC):
                                last = mm(o[0:w, 0:D], cx[:, c, arg * P:arg * P + w], wv[:, c], start=c == 0, stop=c == DC - 1)
                        last.then_inc(s["job_done"], 1)

                    def scores(K):
                        gi, cc, j = K // U, K % U // GB, K % GB
                        if K % U == 0 and gi:
                            wait_all_evacuated(pe, gi - 1)
                            if norm:
                                pe.wait_ge(s["keys_ready"], gi * GB)
                        if K:
                            pe.wait_ge(*((s["scores_used"], K) if deform else (s["exp_done"], 2 * K)))
                        for t in range(2):
                            last = mm(ps[:, t, 0:LK], qblk[:, gi, cc, j, t * P:(t + 1) * P], KT[:, gi, cc, j * LK:(j + 1) * LK], start=True, stop=True)
                        last.then_inc(s["scores_done"], 1)

                    def transposes(K):
                        j = K % GB
                        pe.wait_ge(s["probs_ready"], K + 1)
                        if K:
                            pe.wait_ge(s["copied_dve"], K)
                            pe.wait_ge(s["copied_act"], K)
                        for t in range(2):
                            for c in range(KC):
                                last = tr(ps[:, 2 + t, c * P:(c + 1) * P], probs[:, j, t, c * P:(c + 1) * P], E.c("ident"))
                        last.then_inc(s["transposed"], 1)

                    def values(K):
                        gi, cc, j = K // U, K % U // GB, K % GB
                        pe.wait_ge(s["copied_dve"], K + 1)
                        pe.wait_ge(s["copied_act"], K + 1)
                        if K:
                            pe.wait_ge(s["pv_used"], K)
                        if K % U == 0 and gi:
                            pe.wait_ge(s["x_done"], gi)
                        for c in range(KC):
                            last = mm(ps[:, PV, 0:2 * P], V[:, gi, 2 * j + c, cc * P:(cc + 1) * P], pT[:, K % 2, c], start=c == 0, stop=c == KC - 1)
                        last.then_inc(s["pv_done"], 1)

                    def output(gi):
                        pe.wait_ge(s["heads_ready"], (gi + 1) * U)
                        for c in range(DC):
                            last = mm(ps[:, PV, D:2 * D], attnT[:, c], wo[:, c], start=c == 0, stop=c == DC - 1)
                        last.then_inc(s["y_ready"], 1)

                    for it in range(steps):
                        if it < units:
                            scores(it)
                        if it >= 3 + L and (it - 3 - L) % U == U - 1:
                            output((it - 3 - L) // U)
                        for a in at(it):
                            job(*a)
                        if 0 <= it - 1 - L < units:
                            transposes(it - 1 - L)
                        if 0 <= it - 2 - L < units:
                            values(it - 2 - L)

                @blk.vector
                def _(dve):
                    v = nc.vector
                    link = chain(dve, s["dve_step"])

                    def normalise(k, tile):
                        xg = src[:, bass.ds(tile, 1)].rearrange("p a d -> p (a d)")
                        if finish == "residual":
                            layer_norm(dve, link, v, s, k, n_sb[:], xg, stats).then_inc(s["n_ready"], 1)
                        else:
                            v.tensor_copy(n_sb[:], xg).then_inc(s["n_ready"], 1)

                    def block_diagonal(q, par):
                        for m in range(DC):
                            last = v.tensor_tensor(
                                qblk[:, par, m].rearrange("p j (h q) -> p j h q", h=8), q[:, m].rearrange("p (j q) -> p j q", j=GB).unsqueeze(2).to_broadcast([P, GB, 8, LQ]),
                                E.c("qmask8").unsqueeze(1).unsqueeze(3).to_broadcast([P, GB, 8, LQ]), ALU.mult)
                        return last

                    def take(n, tile, par, kind, arg, e):
                        k = n // J
                        if kind == "kvar":
                            if arg[0] == 0:
                                scale_keys()
                            else:
                                unscaled.append((k, par, arg[1]))
                        if e != "dve":
                            return
                        o = ps[:, JOB + n % JB]
                        dve.wait_ge(s["job_done"], n + 1)
                        q2 = qT[:].rearrange("p m t -> p (m t)")
                        if kind == "q":
                            for m in range(DC):
                                last = v.tensor_scalar(qT[:, m], o[:, m * P:(m + 1) * P], bq[:, m:m + 1], None, ALU.add)
                            link(last)
                            if norm:
                                last = v.tensor_tensor(qsq[:], q2, q2, ALU.mult)
                            else:
                                if deform:
                                    for m in range(DC):
                                        v.tensor_copy(qrep[:, m], qT[:, m].rearrange("p (j q) -> p j q", j=GB).unsqueeze(2).to_broadcast([P, GB, 4, LQ]))
                                last = block_diagonal(qT, par)
                        elif kind == "qvar":
                            dve.wait_ge(s["rstd_ready"], k * (1 + GB) + 1)
                            link(v.scalar_tensor_tensor(qrs[:], q2, norm[0], qrs[:], ALU.mult, ALU.mult))
                            link(v.tensor_scalar(q2, qrs[:], norm[1], None, ALU.add))
                            last = block_diagonal(qT, par)
                        elif kind == "off":
                            link(v.tensor_tensor(offb[:], o[:, 0:GB * 80].rearrange("p (j n) -> p j n", j=GB), deform["boff"].unsqueeze(1).to_broadcast([P, GB, 80]), ALU.add))
                            link(v.tensor_tensor(
                                offb[:].rearrange("p j (t h k) -> p (j t) h k", t=4, h=4), offb[:].rearrange("p j (t h k) -> p (j t) h k", t=4, h=4),
                                E.c("rowmask").unsqueeze(1).unsqueeze(3).to_broadcast([P, GB * 4, 4, NK]), ALU.mult))
                            link(v.tensor_reduce(loc[:].rearrange("p j t k -> p (j t) k"), offb[:].rearrange("p j (t h k) -> p (j t) k h", t=4, h=4), AX.X, ALU.add))
                            flat = loc[:].rearrange("p j t k -> p (j t) k")
                            link(v.tensor_tensor(flat, flat, E.c("loc_base").unsqueeze(1).to_broadcast([P, GB * 4, NK]), ALU.add))
                            flat3 = loc[:].rearrange("p j t k -> p j (t k)")
                            a3, b3 = t1[:].rearrange("p j t k -> p j (t k)"), t2[:, par].rearrange("p j t k -> p j (t k)")
                            length = deform["length"][:, bass.ds((tile) * GB, GB)].unsqueeze(2).to_broadcast([P, GB, 4 * NK])
                            inverse = deform["inverse"][:, bass.ds((tile) * GB, GB)].unsqueeze(2).to_broadcast([P, GB, 4 * NK])
                            link(v.tensor_tensor(a3, flat3, inverse, ALU.mult))
                            link(v.tensor_scalar(a3, a3, 12582912.0, None, ALU.add))
                            link(v.tensor_scalar(a3, a3, -12582912.0, None, ALU.add))
                            link(v.tensor_tensor(a3, a3, length, ALU.mult))
                            link(v.tensor_tensor(flat3, flat3, a3, ALU.subtract))
                            link(v.tensor_tensor(b3, flat3, length, ALU.mult))
                            link(v.tensor_scalar(b3, b3, 0.0, None, ALU.is_lt))
                            link(v.tensor_tensor(b3, b3, length, ALU.mult))
                            link(v.tensor_tensor(flat3, flat3, b3, ALU.add))
                            link(v.tensor_scalar(flat3, flat3, 2.0 / (LK - 1), -1.0, ALU.mult, ALU.add))
                            link(v.tensor_scalar(flat3, flat3, 1.0, float(LK), ALU.add, ALU.mult))
                            link(v.tensor_scalar(flat3, flat3, -1.0, -0.5, ALU.add, ALU.mult))
                            last = v.tensor_copy(t2[:, par], loc[:])
                        elif kind == "V":
                            w = min(P, CT - arg * P)
                            if tiles and k and arg == 0:
                                dve.wait_ge(s["pv_done"], k * U)
                            last = v.tensor_tensor(V[0:w, par, arg], o[0:w, 0:D], rows["bv"][0:w], ALU.add)
                        last.then_inc(s["evac_dve"], 1)

                    unscaled = []

                    def scale_keys():
                        for k, par, j in unscaled:
                            dve.wait_ge(s["rstd_ready"], k * (1 + GB) + 2 + j)
                            kk = [KT[:, par, m, j * LK:(j + 1) * LK] for m in range(DC)]
                            for m in range(DC):
                                last = v.scalar_tensor_tensor(kk[m], kk[m], norm[2], rstd[:, m], ALU.mult, ALU.mult)
                            link(last)
                            for m in range(DC):
                                last = v.tensor_scalar(kk[m], kk[m], norm[3], None, ALU.add)
                            last.then_inc(s["keys_ready"], 1)
                        unscaled.clear()

                    def maxima(K):
                        dve.wait_ge(s["scores_done"], K + 1)
                        v.tensor_reduce(negmax[:, K % 2], ps[:, 0:2, 0:LK], AX.X, ALU.max, negate=True).then_inc(s["max_ready"], 1)

                    def divide(K):
                        j = K % GB
                        dve.wait_ge(s["exp_done"], 2 * K + 2)
                        link(v.reciprocal(sums[:, K % 2], sums[:, K % 2]))
                        for t in range(2):
                            pr = probs[:, j, t, j:j + LK]
                            last = v.tensor_scalar(pr, pr, sums[:, K % 2, t:t + 1], None, ALU.mult)
                        last.then_inc(s["probs_ready"], 1)

                    def sampled_scores(K):
                        dve.wait_ge(s["scores_used"], K + 1)
                        for t in range(2):
                            dve.wait_ge(s["hats"], 2 * K + t + 1)
                            for q in range(NK):
                                link(v.scalar_tensor_tensor(prod[:, q % 2], hat[K % 2][t][:, q], 0.5, S_sb[:, K % 2, t], ALU.mult, ALU.mult, accum_out=sc[:, t, q:q + 1]), behind=int(q < NK - 1))
                        link(v.tensor_reduce(negmax[:, K % 2], sc[:, :, 0:NK], AX.X, ALU.max, negate=True))
                        v.tensor_tensor(att[:, K % 2, :, 0:NK], sc[:, :, 0:NK], negmax[:, K % 2].unsqueeze(2).to_broadcast([P, 2, NK]), ALU.add).then_inc(s["max_ready"], 1)
                        dve.wait_ge(s["max_ready"], K + 1)

                    def key_weights(K):
                        j = K % GB
                        w = att[:, K % 2, :, 0:NK]
                        dve.wait_ge(s["soft_ready"], K + 1)
                        link(v.tensor_reduce(sums[:, K % 2], w, AX.X, ALU.add))
                        link(v.reciprocal(sums[:, K % 2], sums[:, K % 2]))
                        link(v.tensor_scalar(sums[:, K % 2], sums[:, K % 2], 0.5, None, ALU.mult))
                        link(v.tensor_tensor(w, w, sums[:, K % 2].unsqueeze(2).to_broadcast([P, 2, NK]), ALU.mult))
                        if K >= GB:
                            dve.wait_ge(s["transposed"], K - GB + 1)
                        for q in range(NK):
                            for t in range(2):
                                pr, h = probs[:, j, t, j:j + LK], hat[K % 2][t][:, q]
                                if q == 0:
                                    last = v.tensor_scalar(pr, h, w[:, t, 0:1], None, ALU.mult)
                                else:
                                    last = v.scalar_tensor_tensor(pr, h, w[:, t, q:q + 1], pr, ALU.mult, ALU.add)
                                if (q, t) != (NK - 1, 1):
                                    link(last, behind=1)
                        last.then_inc(s["probs_ready"], 1)

                    def copy_transposed(K):
                        dve.wait_ge(s["transposed"], K + 1)
                        if K >= 2:
                            dve.wait_ge(s["pv_done"], K - 1)
                        v.tensor_copy(pT[:, K % 2, :, P:2 * P], ps[:, 3, 0:KC * P].rearrange("p (c t) -> p c t", c=KC)).then_inc(s["copied_dve"], 1)

                    def own_heads(K):
                        gi, cc, j = K // U, K % U // GB, K % GB
                        dve.wait_ge(s["pv_done"], K + 1)
                        if K:
                            dve.wait_ge(s["heads_ready"], K)
                        v.tensor_tensor(own[:], ps[:, PV, 0:2 * P].rearrange("p (h q) -> p h q", h=8),
                                        E.c("headmask").unsqueeze(2).to_broadcast([P, 8, LQ]), ALU.mult).then_inc(s["pv_used"], 1)
                        dve.wait_ge(s["pv_used"], K + 1)
                        if K % U == 0 and gi:
                            dve.wait_ge(s["y_ready"], gi)
                        v.tensor_reduce(attnT[:, cc, j * LQ:(j + 1) * LQ], own[:].rearrange("p h q -> p q h"), AX.X, ALU.add).then_inc(s["heads_ready"], 1)

                    def output(gi):
                        dve.wait_ge(s["y_ready"], gi + 1)
                        xg = src[:, bass.ds(g0 + gi, 1)].rearrange("p a d -> p (a d)")
                        link(v.tensor_tensor(ytmp[:], ps[:, PV, D:2 * D], rows["bo"], ALU.add))
                        if finish == "residual":
                            v.tensor_tensor(xg, ytmp[:], xg, ALU.add).then_inc(s["x_done"], 1)
                        else:
                            link(v.tensor_tensor(ytmp[:], ytmp[:], xg, ALU.add))
                            link(layer_norm(dve, link, v, s, gi, ytmp[:], ytmp[:], stats))
                            link(v.tensor_tensor(ytmp[:], ytmp[:], rows["g"], ALU.mult))
                            v.tensor_tensor(xg, ytmp[:], rows["b"], ALU.add).then_inc(s["x_done"], 1)
                        dve.wait_ge(s["x_done"], gi + 1)

                    if not tiles:
                        for half in range(2):
                            link(v.memset(V[:, half, VT - 1], 0.0))
                    normalise(0, slots[0][0])
                    for it in range(steps):
                        if deform and 0 <= it - 1 < units:
                            key_weights(it - 1)
                        if it < units:
                            if deform:
                                sampled_scores(it)
                            else:
                                maxima(it)
                        if it >= 3 + L and (it - 3 - L) % U == U - 1:
                            output((it - 3 - L) // U)
                        for a in at(it):
                            take(*a)
                        if it < units and not deform:
                            divide(it)
                        scale_keys()
                        if 0 <= it - 1 - L < units:
                            copy_transposed(it - 1 - L)
                        if 0 <= it - 2 - L < units:
                            own_heads(it - 2 - L)
                        if it % U == U - 1 and it // U + 1 < len(slots):
                            normalise(it // U + 1, slots[it // U + 1][0])

                @blk.gpsimd
                def _(pool):
                    if not tiles:
                        nc.gpsimd.memset(probs[:], 0.0).then_inc(s["zeroed"], 1)
                        pool.wait_ge(s["zeroed"], 1)
                    for k in range(len(slots) if finish == "residual" else tiles):
                        power(E, pool, s, k, stats[:, 8:9], stats[:, 7:8], 1e-5 if finish == "residual" else 1e-12)

                @blk.scalar
                def _(act):
                    a = nc.scalar.activation

                    def take(n, tile, par, kind, arg, e):
                        k = n // J
                        o = ps[:, JOB + n % JB]
                        if kind == "qvar":
                            act.wait_ge(s["job_done"], n + 1)
                            if k:
                                wait_evacuated(act, n - J)
                            a(qrs[:], o[:, 0:D], ACT.Ln, scale=1.0 / 16, bias=E.c("eps5")).then_inc(s["logs"], 1)
                            act.wait_ge(s["logs"], k + 1)
                            a(qrs[:], qrs[:], ACT.Exp, scale=-0.5).then_inc(s["rstd_ready"], 1)
                        if kind == "kvar":
                            m, j = arg
                            act.wait_ge(s["job_done"], n + 1)
                            if k or j:
                                act.wait_ge(s["keys_ready"], k * GB + j)
                            a(rstd[:, m], o[:, 0:LK], ACT.Ln, scale=1.0 / 16, bias=E.c("eps5")).then_inc(s["evac_act"], 1)
                            if m == DC - 1:
                                wait_evacuated(act, n)
                                a(rstd[:], rstd[:], ACT.Exp, scale=-0.5).then_inc(s["rstd_ready"], 1)
                            return
                        if e != "act":
                            return
                        act.wait_ge(s["job_done"], n + 1)
                        if kind == "n":
                            last = nc.scalar.copy(nT[:].rearrange("p c t -> p (c t)"), o[:, 0:D])
                        else:
                            m, j = arg
                            if norm:
                                if k or j >= 2:
                                    act.wait_ge(s["job_done"], (k * J + where["kvar", (m, j - 2)] if j >= 2 else (k - 1) * J + where["kvar", (m, j + 2)]) + 1)
                                a(sq[:, j % 2, m], o[:, 0:LK], ACT.Square, bias=bk[:, m:m + 1]).then_inc(s["norm_sq"], 1)
                            last = a(KT[:, par, m, j * LK:(j + 1) * LK], o[:, 0:LK], ACT.Identity, bias=bk[:, m:m + 1])
                        last.then_inc(s["evac_act"], 1)

                    def exponentials(K):
                        j = K % GB
                        act.wait_ge(s["max_ready"], K + 1)
                        if K >= GB:
                            act.wait_ge(s["transposed"], K - GB + 1)
                        if K >= 2:
                            act.wait_ge(s["probs_ready"], K - 1)
                        for t in range(2):
                            a(probs[:, j, t, j:j + LK], ps[:, t, 0:LK], ACT.Exp, bias=negmax[:, K % 2, t:t + 1], accum_out=sums[:, K % 2, t:t + 1]).then_inc(s["exp_done"], 1)

                    def hats(K, row_tiles):
                        gi, cc, j = K // U, K % U // GB, K % GB
                        if K % U == 0 and gi:
                            wait_evacuated(act, (gi - 1) * J + where["off", None])
                        if K >= 2:
                            act.wait_ge(s["probs_ready"], K - 1)
                        for t in row_tiles:
                            for q in range(NK):
                                a(hat[K % 2][t][:, q], E.c("key_index")[:, 0:LK], ACT.Abs, bias=t2[:, gi, j, 2 * cc + t, q:q + 1]).then_inc(s["act_step"], 1)
                            act.wait_ge(s["act_step"], NK * (2 * K + t + 1))
                            a(hat[K % 2][t], hat[K % 2][t], ACT.Relu, bias=E.c("one"), scale=-1.0).then_inc(s["hats"], 1)

                    def take_scores(K):
                        act.wait_ge(s["scores_done"], K + 1)
                        if K >= 2:
                            act.wait_ge(s["max_ready"], K - 1)
                        nc.scalar.copy(S_sb[:, K % 2], ps[:, 0:2, 0:LK]).then_inc(s["scores_used"], 1)

                    def soft(K):
                        act.wait_ge(s["max_ready"], K + 1)
                        w = att[:, K % 2, :, 0:NK]
                        a(w, w, ACT.Exp).then_inc(s["soft_ready"], 1)

                    if deform and tiles:
                        hats(0, (0, 1))
                    for it in range(steps):
                        if it < units:
                            if deform:
                                take_scores(it)
                            else:
                                exponentials(it)
                        for b in at(it):
                            take(*b)
                        if 0 <= it - 1 - L < units:
                            K = it - 1 - L
                            act.wait_ge(s["transposed"], K + 1)
                            if K >= 2:
                                act.wait_ge(s["pv_done"], K - 1)
                            nc.scalar.copy(pT[:, K % 2, :, 0:P], ps[:, 2, 0:KC * P].rearrange("p (c t) -> p c t", c=KC)).then_inc(s["copied_act"], 1)
                        if deform and it < units:
                            if it + 1 < units:
                                hats(it + 1, (0,))
                            soft(it)
                            if it + 1 < units:
                                hats(it + 1, (1,))

            end_round(nc, handles)

        block(0, 0, [(0, 0)])
        with nc.Fori(0, NG // ROUND - 1) as pair:
            block(pair * ROUND, ROUND, [(pair * ROUND + 1, 1), (pair * ROUND + 2, 0)])
        block(NG - ROUND, ROUND, [(NG - 1, 1)])


def self_attention(E, tag, w, rows, bq=None, bk=None, rope=None, unit_norm=False, query_scale=None, mask=False,
                   decay=None, gate_bias=None, heads_gate=None, source=None, finish="residual"):
    nc, ps = E.nc, E.ps
    ROUND = 4
    wq, wk, wv, wo = w
    src = E.x if source is None else source
    with ExitStack() as st:
        s, handles = signals(st, nc, tag, "n_ready nT_psum nT_ready qk_psum qk_sb v_psum v_ready gate_ready rot_psum squared norm_psum "
                             "qblk_ready scores_done scoresT_sb scores_rows shifted exp_done probs_ready transposed pT_ready pv_done pv_used heads_ready "
                             "attn_ready y_ready dve_step logs rstd_ready var_ready added_eps power_ready")

        def sb(name, shape):
            return st.enter_context(nc.sbuf_tensor(f"{tag}_{name}", [P, ROUND] + shape, F32))

        n_sb, stats, nT = sb("n", [D]), sb("stats", [9]), sb("nT", [DC, P])
        attnT = nT
        qk, v_sb, probs = sb("qk", [4, P]), sb("v", [D]), sb("probs", [16, LQ])
        ytmp = v_sb[:]
        tmp, big = sb("tmp", [4, P]), sb("sums", [16])
        scoresT = tmp
        gate = n_sb.rearrange("p g (c t) -> p g c t", c=DC)
        two = lambda name, shape: st.enter_context(nc.sbuf_tensor(f"{tag}_{name}", [P, 2] + shape, F32))
        qblk, pT = two("qblk", [DC, GB, 8 * LQ]), two("pT", [GB, 4 * P])
        own = st.enter_context(nc.sbuf_tensor(f"{tag}_own", [P, DC * GB, 2, LQ], F32))
        rsum = sb("rsum", [16])
        top = sb("top", [32])
        norm_cols = 512 if unit_norm else 256

        fill(E, tag, [(pT[:], 0.0)])

        with nc.Fori(0, NG // ROUND) as pair:
            g0 = pair * ROUND
            with nc.Block(no_gpsimd_drain=True) as block:

                @block.tensor
                def _(pe):
                    mm, tr = nc.tensor.matmul, nc.tensor.transpose
                    for gi in range(ROUND):
                        pe.wait_ge(s["n_ready"], gi + 1)
                        for c in range(DC):
                            last = tr(ps[:, 2 * gi, c * P:(c + 1) * P], n_sb[:, gi, c * P:(c + 1) * P], E.c("ident"))
                        last.then_inc(s["nT_psum"], 1)
                    for gi in range(ROUND):
                        pe.wait_ge(s["nT_ready"], gi + 1)
                        for i, wi in enumerate((wq, wk)):
                            for m in range(DC):
                                for c in range(DC):
                                    last = mm(ps[:, 2 * gi, (2 * i + m) * P:(2 * i + m + 1) * P], wi[:, c, m * P:(m + 1) * P], nT[:, gi, c], start=c == 0, stop=c == DC - 1)
                        last.then_inc(s["qk_psum"], 1)
                        for c in range(DC):
                            last = mm(ps[:, 2 * gi + 1, 0:D], nT[:, gi, c], wv[:, c], start=c == 0, stop=c == DC - 1)
                        if gate_bias is not None:
                            for m in range(DC):
                                for c in range(DC):
                                    last = mm(ps[:, 2 * gi + 1, D + m * P:D + (m + 1) * P], wo[:, c, m * P:(m + 1) * P], nT[:, gi, c], start=c == 0, stop=c == DC - 1)
                        last.then_inc(s["v_psum"], 1)
                    if rope:
                        for gi in range(ROUND):
                            pe.wait_ge(s["qk_sb"], gi + 1)
                            mm(ps[:, 2 * gi], E.c(rope), qk[:, gi].rearrange("p a b -> p (a b)"), start=True, stop=True).then_inc(s["rot_psum"], 1)
                    if unit_norm or query_scale:
                        for gi in range(ROUND):
                            pe.wait_ge(s["squared"], gi + 1)
                            pe.wait_ge(s["v_ready"], gi + 1)
                            mm(ps[:, 2 * gi + 1, 0:norm_cols], E.c("head_ones"), tmp[:, gi].rearrange("p a b -> p (a b)")[:, 0:norm_cols], start=True, stop=True).then_inc(s["norm_psum"], 1)
                    for gi in range(ROUND):
                        pe.wait_ge(s["qblk_ready"], gi + 1)
                        for c in range(DC):
                            for j in range(GB):
                                last = mm(ps[j * LQ:(j + 1) * LQ, 2 * gi, c * 8 * LQ:(c + 1) * 8 * LQ], qk[:, gi, 2 + c, j * LQ:(j + 1) * LQ], qblk[:, gi % 2, c, j], start=True, stop=True)
                        last.then_inc(s["scores_done"], 1)
                    for gi in range(ROUND):
                        pe.wait_ge(s["scoresT_sb"], gi + 1)
                        pe.wait_ge(s["v_ready"], gi + 1)
                        if gate_bias is not None:
                            pe.wait_ge(s["gate_ready"], gi + 1)
                        for t in range(4):
                            last = tr(ps[:, 2 * gi + 1, t * P:(t + 1) * P], scoresT[:, gi, t], E.c("ident"))
                        last.then_inc(s["scores_rows"], 1)
                    for gi in range(ROUND):
                        pe.wait_ge(s["probs_ready"], gi + 1)
                        for t in range(4):
                            last = tr(ps[:, 2 * gi, t * P:(t + 1) * P], probs[:, gi, t * GB:(t + 1) * GB].rearrange("p a b -> p (a b)"), E.c("ident"))
                        last.then_inc(s["transposed"], 1)
                    for gi in range(ROUND):
                        pe.wait_ge(s["pT_ready"], gi + 1)
                        for c in range(DC):
                            for i in range(P // 32):
                                f = slice(c * P + 32 * i, c * P + 32 * (i + 1))
                                q = slice((8 * c + 2 * i) * LQ, (8 * c + 2 * i + 2) * LQ)
                                last = mm(ps[32 * i:32 * (i + 1), 2 * gi + 1, c * D:(c + 1) * D], v_sb[:, gi, f], pT[:, gi % 2, :, q], start=True, stop=True)
                        last.then_inc(s["pv_done"], 1)
                    for gi in range(ROUND):
                        pe.wait_ge(s["heads_ready"] if gate_bias is None else s["attn_ready"], gi + 1)
                        if gate_bias is not None:
                            for c in range(DC):
                                last = tr(ps[:, 2 * gi + 1, c * P:(c + 1) * P], attnT[:, gi, c], E.c("ident"))
                        else:
                            for c in range(DC):
                                last = mm(ps[:, 2 * gi + 1, 0:D], attnT[:, gi, c], wo[:, c], start=c == 0, stop=c == DC - 1)
                            if heads_gate:
                                for c in range(DC):
                                    last = mm(ps[:, 2 * gi + 1, D:D + 17], attnT[:, gi, c], E.small("Wrs")[:, c], start=c == 0, stop=c == DC - 1)
                        last.then_inc(s["y_ready"], 1)

                @block.vector
                def _(dve):
                    v = nc.vector
                    link = chain(dve, s["dve_step"])
                    if finish == "residual":
                        for gi in range(ROUND):
                            xg = src[:, bass.ds(g0 + gi, 1)].rearrange("p a d -> p (a d)")
                            link(v.bn_stats(stats[:, gi, 0:6], xg))
                            v.bn_aggr(stats[:, gi, 6:8], stats[:, gi, 0:6]).then_inc(s["var_ready"], 1)
                    for gi in range(ROUND):
                        xg = src[:, bass.ds(g0 + gi, 1)].rearrange("p a d -> p (a d)")
                        if finish == "residual":
                            dve.wait_ge(s["power_ready"], gi + 1)
                            v.tensor_scalar(n_sb[:, gi], xg, stats[:, gi, 6:7], stats[:, gi, 8:9], ALU.subtract, ALU.mult).then_inc(s["n_ready"], 1)
                        else:
                            v.tensor_copy(n_sb[:, gi], xg).then_inc(s["n_ready"], 1)
                    for gi in range(ROUND):
                        dve.wait_ge(s["v_psum"], gi + 1)
                        if "bv" in rows:
                            v.tensor_tensor(v_sb[:, gi], ps[:, 2 * gi + 1, 0:D], rows["bv"], ALU.add).then_inc(s["v_ready"], 1)
                        else:
                            v.tensor_copy(v_sb[:, gi], ps[:, 2 * gi + 1, 0:D]).then_inc(s["v_ready"], 1)
                    if rope:
                        for gi in range(ROUND):
                            q4 = qk[:, gi].rearrange("p a (j q) -> p (a j) q", j=GB)
                            t4 = tmp[:, gi].rearrange("p a (j q) -> p (a j) q", j=GB)
                            dve.wait_ge(s["rot_psum"], gi + 1)
                            link(v.tensor_tensor(t4, ps[:, 2 * gi].rearrange("p (a q) -> p a q", q=LQ), E.c("sin").unsqueeze(1).to_broadcast([P, 16, LQ]), ALU.mult))
                            link(v.tensor_tensor(q4, q4, E.c("cos").unsqueeze(1).to_broadcast([P, 16, LQ]), ALU.mult))
                            link(v.tensor_tensor(q4, q4, t4, ALU.add))
                    if unit_norm or query_scale:
                        for gi in range(ROUND):
                            if not rope:
                                dve.wait_ge(s["qk_sb"], gi + 1)
                            q2 = qk[:, gi].rearrange("p a b -> p (a b)")[:, 0:norm_cols]
                            v.tensor_tensor(tmp[:, gi].rearrange("p a b -> p (a b)")[:, 0:norm_cols], q2, q2, ALU.mult).then_inc(s["squared"], 1)
                        for gi in range(ROUND):
                            q2 = qk[:, gi].rearrange("p a b -> p (a b)")[:, 0:norm_cols]
                            t2 = tmp[:, gi].rearrange("p a b -> p (a b)")[:, 0:norm_cols]
                            dve.wait_ge(s["norm_psum"], gi + 1)
                            dve.wait_ge(s["rstd_ready"], gi + 1)
                            link(v.tensor_tensor(q2, q2, t2, ALU.mult))
                            if query_scale:
                                for m in range(DC):
                                    link(v.tensor_scalar(qk[:, gi, m], qk[:, gi, m], query_scale[0][:, m:m + 1], query_scale[1][:, m:m + 1], ALU.add, ALU.mult))
                    for gi in range(ROUND):
                        if not (rope or unit_norm or query_scale):
                            dve.wait_ge(s["qk_sb"], gi + 1)
                        if gi >= 2:
                            dve.wait_ge(s["scores_done"], gi - 1)
                        for m in range(DC):
                            last = v.tensor_tensor(qblk[:, gi % 2, m].rearrange("p j (h q) -> p j h q", h=8), qk[:, gi, m].rearrange("p (j q) -> p j q", j=GB).unsqueeze(2).to_broadcast([P, GB, 8, LQ]),
                                                   E.c("qmask8").unsqueeze(1).unsqueeze(3).to_broadcast([P, GB, 8, LQ]), ALU.mult)
                        last.then_inc(s["qblk_ready"], 1)
                    for gi in range(ROUND):
                        dve.wait_ge(s["scores_rows"], gi + 1)
                        S = ps[:, 2 * gi + 1].rearrange("p (a k) -> p a k", k=LQ)
                        pr = probs[:, gi]
                        if decay is not None:
                            for t in range(4):
                                last = v.tensor_tensor(pr[:, t * GB:(t + 1) * GB], S[:, t * GB:(t + 1) * GB], decay[:, t].unsqueeze(1).to_broadcast([P, GB, LQ]), ALU.mult)
                            last.then_inc(s["probs_ready"], 1)
                            continue
                        if mask:
                            p4, S4 = pr.rearrange("p (t j) k -> p t (j k)", j=GB), ps[:, 2 * gi + 1].rearrange("p (t n) -> p t n", t=4)
                            at = lambda m: m[:, bass.ds((g0 + gi) * GB, GB)].rearrange("p j k -> p (j k)").unsqueeze(1).to_broadcast([P, 4, P])
                            link(v.tensor_tensor(p4, S4, at(E.keep), ALU.mult))
                            link(v.tensor_tensor(p4, p4, at(E.floor), ALU.add))
                            S = pr
                        link(v.tensor_reduce(big[:, gi], S, AX.X, ALU.max))
                        v.tensor_tensor(pr, S, big[:, gi].unsqueeze(2).to_broadcast([P, 16, LQ]), ALU.subtract).then_inc(s["shifted"], 1)
                    for gi in range(ROUND):
                        if decay is None:
                            dve.wait_ge(s["exp_done"], gi + 1)
                            link(v.tensor_reduce(rsum[:, gi], probs[:, gi], AX.X, ALU.add))
                            link(v.reciprocal(rsum[:, gi], rsum[:, gi]))
                            v.tensor_tensor(probs[:, gi], probs[:, gi], rsum[:, gi].unsqueeze(2).to_broadcast([P, 16, LQ]), ALU.mult).then_inc(s["probs_ready"], 1)
                    for gi in range(ROUND):
                        dve.wait_ge(s["pv_done"], gi + 1)
                        if gi:
                            dve.wait_ge(s["heads_ready"], gi)
                        v.tensor_tensor(own[:], ps[:, 2 * gi + 1].rearrange("p (a h q) -> p a h q", h=2, q=LQ),
                                        E.c("pairmask").unsqueeze(1).unsqueeze(3).to_broadcast([P, DC * GB, 2, LQ]), ALU.mult).then_inc(s["pv_used"], 1)
                        dve.wait_ge(s["pv_used"], gi + 1)
                        v.tensor_reduce(attnT[:, gi].rearrange("p c (j q) -> p (c j) q", q=LQ), own[:].rearrange("p a h q -> p a q h"), AX.X, ALU.add).then_inc(s["heads_ready"], 1)
                    if gate_bias is not None:
                        for gi in range(ROUND):
                            dve.wait_ge(s["heads_ready"], gi + 1)
                            v.tensor_tensor(attnT[:, gi], attnT[:, gi], gate[:, gi], ALU.mult).then_inc(s["attn_ready"], 1)
                    for gi in range(ROUND):
                        xg = src[:, bass.ds(g0 + gi, 1)].rearrange("p a d -> p (a d)")
                        y = ytmp[:, gi]
                        dve.wait_ge(s["y_ready"], gi + 1)
                        if gate_bias is not None:
                            link(v.tensor_tensor(xg, xg, ps[:, 2 * gi + 1, 0:D], ALU.add))
                            continue
                        if heads_gate:
                            tp = top[:, gi]
                            g17 = big[:, gi]
                            lg = probs[:, gi].rearrange("p a b -> p (a b)")
                            link(v.tensor_tensor(lg[:, 0:17], ps[:, 2 * gi + 1, D:D + 17], heads_gate, ALU.add))
                            for lo, hi, at in ((0, 15, 20), (15, 17, 21)):
                                link(v.tensor_reduce(tp[:, at:at + 1], lg[:, lo:hi], AX.X, ALU.max))
                                link(v.tensor_scalar(lg[:, lo:hi], lg[:, lo:hi], tp[:, at:at + 1], None, ALU.subtract))
                            v.tensor_copy(lg[:, 32:49], lg[:, 0:17]).then_inc(s["shifted"], 1)
                            dve.wait_ge(s["exp_done"], ROUND + gi + 1)
                            link(v.tensor_reduce(tp[:, 22:23], lg[:, 64:79], AX.X, ALU.add))
                            link(v.tensor_reduce(tp[:, 23:24], lg[:, 79:81], AX.X, ALU.add))
                            link(v.reciprocal(tp[:, 24:26], tp[:, 22:24]))
                            link(v.tensor_scalar(lg[:, 64:79], lg[:, 64:79], tp[:, 24:25], None, ALU.mult))
                            link(v.tensor_scalar(lg[:, 79:81], lg[:, 79:81], tp[:, 25:26], None, ALU.mult))
                            link(v.max(tp[:, 0:8], lg[:, 64:79]))
                            link(v.tensor_reduce(tp[:, 26:27], tp[:, 0:3], AX.X, ALU.add))
                            link(v.tensor_reduce(tp[:, 27:28], lg[:, 79:81], AX.X, ALU.add))
                            link(v.tensor_scalar(tp[:, 26:27], tp[:, 26:27], lg[:, 80:81], 6.0, ALU.mult, ALU.mult))
                            link(v.tensor_scalar(tp[:, 27:28], tp[:, 27:28], lg[:, 79:80], 2.0, ALU.mult, ALU.mult))
                            link(v.tensor_tensor(tp[:, 26:27], tp[:, 26:27], tp[:, 27:28], ALU.add))
                            link(v.scalar_tensor_tensor(y, ps[:, 2 * gi + 1, 0:D], tp[:, 26:27], rows["bo"], ALU.mult, ALU.add))
                        else:
                            link(v.tensor_tensor(y, ps[:, 2 * gi + 1, 0:D], rows["bo"], ALU.add))
                        if finish == "residual":
                            link(v.tensor_tensor(xg, xg, y, ALU.add))
                        else:
                            link(v.tensor_tensor(y, y, n_sb[:, gi], ALU.add))
                            link(v.bn_stats(stats[:, gi, 0:6], y))
                            v.bn_aggr(stats[:, gi, 6:8], stats[:, gi, 0:6]).then_inc(s["var_ready"], 1)
                    if finish == "norm":
                        for gi in range(ROUND):
                            dve.wait_ge(s["power_ready"], gi + 1)
                            last = v.tensor_scalar(ytmp[:, gi], ytmp[:, gi], stats[:, gi, 6:7], stats[:, gi, 8:9], ALU.subtract, ALU.mult)
                        link(last)
                        row = lambda n: rows[n].unsqueeze(1).to_broadcast([P, ROUND, D])
                        link(v.tensor_tensor(ytmp, ytmp, row("g"), ALU.mult))
                        link(v.tensor_tensor(src[:, bass.ds(g0, ROUND)], ytmp, row("b"), ALU.add))

                @block.gpsimd
                def _(pool):
                    if finish == "residual":
                        for gi in range(ROUND):
                            power(E, pool, s, gi, stats[:, gi, 8:9], stats[:, gi, 7:8], 1e-5)
                    if finish == "norm":
                        for gi in range(ROUND):
                            power(E, pool, s, gi, stats[:, gi, 8:9], stats[:, gi, 7:8], 1e-12)

                @block.scalar
                def _(act):
                    a = nc.scalar.activation
                    for gi in range(ROUND):
                        act.wait_ge(s["nT_psum"], gi + 1)
                        nc.scalar.copy(nT[:, gi].rearrange("p c t -> p (c t)"), ps[:, 2 * gi, 0:D]).then_inc(s["nT_ready"], 1)
                    for gi in range(ROUND):
                        act.wait_ge(s["qk_psum"], gi + 1)
                        if bq is None:
                            last = nc.scalar.copy(qk[:, gi].rearrange("p a b -> p (a b)"), ps[:, 2 * gi])
                        else:
                            for i in range(4):
                                b = (bq, bk)[i // 2]
                                last = a(qk[:, gi, i], ps[:, 2 * gi, i * P:(i + 1) * P], ACT.Identity, bias=b[:, i % 2:i % 2 + 1])
                        last.then_inc(s["qk_sb"], 1)
                    if gate_bias is not None:
                        for gi in range(ROUND):
                            act.wait_ge(s["v_ready"], gi + 1)
                            for m in range(DC):
                                last = a(gate[:, gi, m], ps[:, 2 * gi + 1, D + m * P:D + (m + 1) * P], ACT.Silu, bias=gate_bias[:, m:m + 1])
                            last.then_inc(s["gate_ready"], 1)
                    if unit_norm or query_scale:
                        for gi in range(ROUND):
                            act.wait_ge(s["norm_psum"], gi + 1)
                            t2 = tmp[:, gi].rearrange("p a b -> p (a b)")[:, 0:norm_cols]
                            a(t2, ps[:, 2 * gi + 1, 0:norm_cols], ACT.Ln, bias=E.c("eps6" if unit_norm else "zero")).then_inc(s["logs"], 1)
                            act.wait_ge(s["logs"], gi + 1)
                            a(t2, t2, ACT.Exp, scale=-0.5).then_inc(s["rstd_ready"], 1)
                    for gi in range(ROUND):
                        act.wait_ge(s["scores_done"], gi + 1)
                        nc.scalar.copy(scoresT[:, gi].rearrange("p a b -> p (a b)"), ps[:, 2 * gi]).then_inc(s["scoresT_sb"], 1)
                    if decay is None:
                        for gi in range(ROUND):
                            act.wait_ge(s["shifted"], gi + 1)
                            pr = probs[:, gi].rearrange("p a b -> p (a b)")
                            a(pr, pr, ACT.Exp).then_inc(s["exp_done"], 1)
                    for gi in range(ROUND):
                        act.wait_ge(s["transposed"], gi + 1)
                        if gi >= 2:
                            act.wait_ge(s["pv_done"], gi - 1)
                        for j in range(GB):
                            h = slice(j * LQ, (j + 1) * LQ)
                            last = nc.scalar.copy(pT[h, gi % 2, j], ps[h, 2 * gi])
                        last.then_inc(s["pT_ready"], 1)
                    if heads_gate:
                        for gi in range(ROUND):
                            act.wait_ge(s["shifted"], ROUND + gi + 1)
                            lg = probs[:, gi].rearrange("p a b -> p (a b)")
                            a(lg[:, 64:81], lg[:, 32:49], ACT.Exp).then_inc(s["exp_done"], 1)

            end_round(nc, handles)


def feature_major(E, tag, nT, source=None, pre=None, gating=None, extra_bias=None):
    nc, ps = E.nc, E.ps
    with ExitStack() as st:
        s, handles = signals(st, nc, tag, "n_ready nT_psum nT_ready n1T_psum n1T_ready mix_done logits_done act_in act_out comb_ready combT_psum "
                             "combT_ready b2_done dve_step var_ready added_eps power_ready")
        n_sb = st.enter_context(nc.sbuf_tensor(f"{tag}_n8", [P, NG, D], F32))
        stats = st.enter_context(nc.sbuf_tensor(f"{tag}_stats", [P, NG, 9], F32))
        if pre:
            n1T = st.enter_context(nc.sbuf_tensor(f"{tag}_n1T", [P, DC, NG * P], F32))
            g1, be1, mix, mix_b, g2, be2 = pre
        if gating:
            gw, gb, kind, comb, b2 = gating
            sc, eq, one1, t8 = (st.enter_context(nc.sbuf_tensor(f"{tag}_{n}", [P, NG, NE], F32)) for n in ("sc", "eq", "one1", "t8"))
            m1 = st.enter_context(nc.sbuf_tensor(f"{tag}_m1", [P, NG], F32))
            m2 = st.enter_context(nc.sbuf_tensor(f"{tag}_m2", [P, NG], F32))
            combT = st.enter_context(nc.sbuf_tensor(f"{tag}_combT", [NE, NG, P], F32))
        with nc.Block(no_gpsimd_drain=True) as block:

            @block.tensor
            def _(pe):
                mm, tr = nc.tensor.matmul, nc.tensor.transpose
                if pre:
                    for g in range(NG):
                        pe.wait_ge(s["n_ready"], g + 1)
                        for c in range(DC):
                            last = tr(ps[:, g, c * P:(c + 1) * P], n_sb[:, g, c * P:(c + 1) * P], E.c("ident"))
                        last.then_inc(s["n1T_psum"], 1)
                    for g in range(NG):
                        pe.wait_ge(s["n1T_ready"], g + 1)
                        for c in range(DC):
                            last = mm(ps[:, g, D:2 * D], n1T[:, c, g * P:(g + 1) * P], mix[:, c], start=c == 0, stop=c == DC - 1)
                        last.then_inc(s["mix_done"], 1)
                for g in range(NG):
                    pe.wait_ge(s["n_ready"], g + 1 + (NG if pre else 0))
                    for c in range(DC):
                        last = tr(ps[:, g, c * P:(c + 1) * P], n_sb[:, g, c * P:(c + 1) * P], E.c("ident"))
                    last.then_inc(s["nT_psum"], 1)
                if gating:
                    for g in range(NG):
                        pe.wait_ge(s["nT_ready"], g + 1)
                        for c in range(DC):
                            last = mm(ps[:, g, D:D + NE], nT[:, c, g * P:(g + 1) * P], gw[:, c], start=c == 0, stop=c == DC - 1)
                    last.then_inc(s["logits_done"], 1)
                    pe.wait_ge(s["comb_ready"], 1)
                    for g in range(NG):
                        last = tr(ps[0:NE, g, 0:P], comb[:, g], E.c("ident"))
                    last.then_inc(s["combT_psum"], 1)
                    pe.wait_ge(s["combT_ready"], 1)
                    for g in range(NG):
                        mm(ps[:, g, D:2 * D], combT[:, g], b2, start=True, stop=True).then_inc(s["b2_done"], 1)

            @block.gpsimd
            def _(pool):
                if source is not None:
                    return
                power(E, pool, s, 0, stats[:, :, 8:9], stats[:, :, 7:8], 1e-5)
                if pre:
                    power(E, pool, s, 1, stats[:, :, 8:9], stats[:, :, 7:8], 1e-5)
                    for g in range(NG):
                        power(E, pool, s, 2 + g, stats[:, g, 8:9], stats[:, g, 7:8], 1e-5)

            @block.scalar
            def _(act):
                if pre:
                    for g in range(NG):
                        act.wait_ge(s["n1T_psum"], g + 1)
                        nc.scalar.copy(n1T[:, :, g * P:(g + 1) * P], ps[:, g, 0:D].rearrange("p (c t) -> p c t", c=DC)).then_inc(s["n1T_ready"], 1)
                for g in range(NG):
                    act.wait_ge(s["nT_psum"], g + 1)
                    nc.scalar.copy(nT[:, :, g * P:(g + 1) * P], ps[:, g, 0:D].rearrange("p (c t) -> p c t", c=DC)).then_inc(s["nT_ready"], 1)
                if gating:
                    act.wait_ge(s["act_in"], 1)
                    nc.scalar.activation(sc[:], t8[:], ACT.Sigmoid if kind == "sigmoid" else ACT.Exp).then_inc(s["act_out"], 1)
                    act.wait_ge(s["combT_psum"], 1)
                    nc.scalar.copy(combT[:], ps[0:NE, :, 0:P]).then_inc(s["combT_ready"], 1)

            @block.vector
            def _(dve):
                v = nc.vector
                link = chain(dve, s["dve_step"])

                def row(r, n=NG):
                    return r.unsqueeze(1).to_broadcast([P, n, D])

                def statistics(x, n):
                    for g in range(NG):
                        last = v.bn_stats(stats[:, g, 0:6], x[:, g])
                    link(last)
                    for g in range(NG):
                        last = v.bn_aggr(stats[:, g, 6:8], stats[:, g, 0:6])
                    last.then_inc(s["var_ready"], 1)
                    dve.wait_ge(s["power_ready"], n + 1)

                if source is not None:
                    for g in range(NG):
                        v.tensor_copy(n_sb[:, g], source[:, g]).then_inc(s["n_ready"], 1)
                    return
                if pre:
                    statistics(E.x, 0)
                    for g in range(NG):
                        last = v.tensor_scalar(n_sb[:, g], E.x[:, g], stats[:, g, 6:7], stats[:, g, 8:9], ALU.subtract, ALU.mult)
                    link(last)
                    link(v.tensor_tensor(E.x[:], E.x[:], n_sb[:], ALU.add))
                    statistics(n_sb, 1)
                    link(v.tensor_copy(E.z[:], n_sb[:]))
                    for g in range(NG):
                        link(v.tensor_scalar(n_sb[:, g], n_sb[:, g], stats[:, g, 6:7], stats[:, g, 8:9], ALU.subtract, ALU.mult))
                        link(v.tensor_tensor(n_sb[:, g], n_sb[:, g], g1, ALU.mult))
                        v.tensor_tensor(n_sb[:, g], n_sb[:, g], be1, ALU.add).then_inc(s["n_ready"], 1)
                    dve.wait_ge(s["n_ready"], NG)
                    link(v.tensor_tensor(E.z[:], E.z[:], n_sb[:], ALU.add))
                    link(v.tensor_tensor(E.z[:], E.z[:], row(mix_b), ALU.add))
                    link(v.tensor_tensor(E.x[:], E.x[:], n_sb[:], ALU.add))
                    link(v.tensor_tensor(E.x[:], E.x[:], row(mix_b), ALU.add))
                    for g in range(NG):
                        dve.wait_ge(s["mix_done"], g + 1)
                        v.tensor_tensor(E.x[:, g], E.x[:, g], ps[:, g, D:2 * D], ALU.add)
                        link(v.tensor_tensor(E.z[:, g], E.z[:, g], ps[:, g, D:2 * D], ALU.add))
                        link(layer_norm(dve, link, v, s, 2 + g, n_sb[:, g], E.z[:, g], stats[:, g]))
                        link(v.tensor_tensor(n_sb[:, g], n_sb[:, g], g2, ALU.mult))
                        v.tensor_tensor(n_sb[:, g], n_sb[:, g], be2, ALU.add).then_inc(s["n_ready"], 1)
                else:
                    statistics(E.x, 0)
                    for g in range(NG):
                        v.tensor_scalar(n_sb[:, g], E.x[:, g], stats[:, g, 6:7], stats[:, g, 8:9], ALU.subtract, ALU.mult).then_inc(s["n_ready"], 1)
                if gating:
                    dve.wait_ge(s["logits_done"], 1)
                    lg = ps[:, :, D:D + NE]
                    if kind == "sigmoid":
                        v.tensor_tensor(t8[:], lg, gb.unsqueeze(1).to_broadcast([P, NG, NE]), ALU.add).then_inc(s["act_in"], 1)
                    else:
                        link(v.tensor_reduce(m1[:], lg, AX.X, ALU.max))
                        v.tensor_tensor(t8[:], lg, m1[:].unsqueeze(2).to_broadcast([P, NG, NE]), ALU.subtract).then_inc(s["act_in"], 1)
                    dve.wait_ge(s["act_out"], 1)
                    if kind != "sigmoid":
                        link(v.tensor_reduce(m1[:], sc[:], AX.X, ALU.add))
                        link(v.reciprocal(m1[:], m1[:]))
                        link(v.tensor_tensor(sc[:], sc[:], m1[:].unsqueeze(2).to_broadcast([P, NG, NE]), ALU.mult))

                    def first_of_largest(out, scores, m):
                        link(v.tensor_reduce(m, scores, AX.X, ALU.max))
                        link(v.tensor_tensor(eq[:], scores, m.unsqueeze(2).to_broadcast([P, NG, NE]), ALU.is_equal))
                        link(v.tensor_tensor(eq[:], eq[:], E.c("rank").unsqueeze(1).to_broadcast([P, NG, NE]), ALU.mult))
                        link(v.tensor_reduce(m2[:], eq[:], AX.X, ALU.max))
                        link(v.tensor_tensor(out, eq[:], m2[:].unsqueeze(2).to_broadcast([P, NG, NE]), ALU.is_equal))

                    first_of_largest(one1[:], sc[:], m1[:])
                    link(v.scalar_tensor_tensor(t8[:], one1[:], -4.0, sc[:], ALU.mult, ALU.add))
                    m3 = stats[:, :, 0]
                    first_of_largest(comb, t8[:], m3)
                    link(v.tensor_tensor(comb, comb, one1[:], ALU.add))
                    last = v.tensor_tensor(comb, comb, sc[:], ALU.mult)
                    if kind == "sigmoid":
                        link(last)
                        link(v.tensor_tensor(m1[:], m1[:], m3, ALU.add))
                        link(v.tensor_scalar(m1[:], m1[:], 1e-6, None, ALU.add))
                        link(v.reciprocal(m1[:], m1[:]))
                        last = v.tensor_tensor(comb, comb, m1[:].unsqueeze(2).to_broadcast([P, NG, NE]), ALU.mult)
                    last.then_inc(s["comb_ready"], 1)
                    dve.wait_ge(s["b2_done"], NG)
                    link(v.tensor_tensor(E.x[:], E.x[:], ps[:, :, D:2 * D], ALU.add))
                if extra_bias is not None:
                    link(v.scalar_tensor_tensor(E.x[:], row(extra_bias[0]), extra_bias[1], E.x[:], ALU.mult, ALU.add))
        end_round(nc, handles)


def mlp_block(E, s, bufs, nT, steps, chunks, func, glu=False, loads=(), norm=None):
    nc, ps = E.nc, E.ps
    hid, sil = bufs
    W = 2 if glu else 1
    HALF = NG * P // 2
    TH = NG // 2
    with nc.Block(no_gpsimd_drain=True) as block:

        @block.sync
        def _(sp):
            for need, sem, pairs in loads:
                if need:
                    sp.wait_ge(s["down_done"], need)
                for dst, src in pairs:
                    sp.dma_start(dst, src).then_inc(sem, 16)
            for need, sem, pairs in loads:
                sp.wait_ge(sem, 16 * len(pairs))

        @block.tensor
        def _(pe):
            mm = nc.tensor.matmul

            def up(i):
                step = steps[i]
                if step.get("await"):
                    pe.wait_ge(*step["await"])
                for m in range(chunks):
                    n = i * chunks + m
                    for w in range(W):
                        b = (n * W + w) % 4
                        if w == 0 and (n + 1) * W > 4:
                            pe.wait_ge(s["hid_ready"], n + 1 - 4 // W)
                        for c in range(DC):
                            last = mm(ps[:, b], step["up"][w][:, c, m * P:(m + 1) * P], nT[:, c, step["half"] * HALF:(step["half"] + 1) * HALF], start=c == 0, stop=c == DC - 1)
                    last.then_inc(s["up_done"], 1)

            def down(i):
                step = steps[i]
                pe.wait_ge(s["hid_ready"], (i + 1) * chunks)
                for t in range(TH):
                    n = i * TH + t
                    if n >= 4:
                        pe.wait_ge(s["added"], n - 3)
                    for k in range(chunks):
                        last = mm(ps[:, 4 + n % 4, 0:D], hid[:, i % 2, k, t * P:(t + 1) * P], step["down"][:, k], start=k == 0, stop=k == chunks - 1)
                    last.then_inc(s["down_done"], 1)

            up(0)
            for i in range(len(steps)):
                if i + 1 < len(steps):
                    up(i + 1)
                down(i)

        @block.scalar
        def _(act):
            for i, step in enumerate(steps):
                if i >= 2:
                    act.wait_ge(s["down_done"], (i - 1) * TH)
                for m in range(chunks):
                    n = i * chunks + m
                    act.wait_ge(s["up_done"], n + 1)
                    if glu:
                        if n >= 2:
                            act.wait_ge(s["hid_ready"], n - 1)
                        nc.scalar.activation(sil[:, n % 2], ps[:, (2 * n) % 4], ACT.Silu).then_inc(s["sil_ready"], 1)
                    else:
                        nc.scalar.activation(hid[:, i % 2, m], ps[:, n % 4], func, bias=step["b1"](m)).then_inc(s["hid_ready"], 1)

        @block.gpsimd
        def _(pool):
            if norm:
                for i, step in enumerate(steps):
                    half = norm[1][:, step["half"] * TH:(step["half"] + 1) * TH]
                    power(E, pool, s, i, half[:, :, 8:9], half[:, :, 7:8], 1e-12)

        @block.vector
        def _(dve):
            v = nc.vector
            link = chain(dve, s["dve_step"])

            def add(i):
                step = steps[i]
                if i:
                    dve.wait_ge(s["added"], i * TH)
                for t in range(TH):
                    n = i * TH + t
                    g = step["half"] * TH + t
                    dve.wait_ge(s["down_done"], n + 1)
                    dst = step["into"][:, g]
                    v.scalar_tensor_tensor(dst, ps[:, 4 + n % 4, 0:D], step["weight"](g), dst, ALU.mult, ALU.add).then_inc(s["added"], 1)
                if norm:
                    rows, stats = norm
                    tiles = range(step["half"] * TH, (step["half"] + 1) * TH)
                    h = step["into"][:, tiles[0]:tiles[-1] + 1]
                    row = lambda n: rows[n].unsqueeze(1).to_broadcast([P, TH, D])
                    dve.wait_ge(s["added"], (i + 1) * TH)
                    link(v.tensor_tensor(h, h, row("b2"), ALU.add))
                    for g in tiles:
                        last = v.bn_stats(stats[:, g, 0:6], step["into"][:, g])
                    link(last)
                    for g in tiles:
                        last = v.bn_aggr(stats[:, g, 6:8], stats[:, g, 0:6])
                    last.then_inc(s["var_ready"], 1)
                    dve.wait_ge(s["power_ready"], i + 1)
                    for g in tiles:
                        last = v.tensor_scalar(step["into"][:, g], step["into"][:, g], stats[:, g, 6:7], stats[:, g, 8:9], ALU.subtract, ALU.mult)
                    link(last)
                    link(v.tensor_tensor(h, h, row("g"), ALU.mult))
                    link(v.tensor_tensor(h, h, row("b"), ALU.add))

            for i in range(len(steps)):
                if glu:
                    if i >= 2:
                        dve.wait_ge(s["down_done"], (i - 1) * TH)
                    for m in range(chunks):
                        n = i * chunks + m
                        dve.wait_ge(s["sil_ready"], n + 1)
                        v.tensor_tensor(hid[:, i % 2, m], sil[:, n % 2], ps[:, (2 * n + 1) % 4], ALU.mult).then_inc(s["hid_ready"], 1)
                    if i:
                        add(i - 1)
                else:
                    add(i)
            if glu:
                add(len(steps) - 1)


MLP_SIGNALS = "up_done hid_ready sil_ready down_done added load_a load_b dve_step var_ready added_eps power_ready"


def expert_mixture(E, tag, w1, w2, b1_at, comb, nT, func, shared=None):
    nc = E.nc

    def views(w):
        return w[:, 0:2 * FF].rearrange("p (c n) -> p c n", c=DC), w[:, 2 * FF:4 * FF].rearrange("p (c n) -> p c n", c=FC)

    def load(w, e):
        up, down = views(w)
        return [(up, w1[bass.ds(e, 1)].rearrange("a (c p) n -> (a p) c n", p=P)), (down, w2[bass.ds(e, 1)].rearrange("a (c p) n -> (a p) c n", p=P))]

    with ExitStack() as st:
        s, handles = signals(st, nc, tag, MLP_SIGNALS)
        hid = st.enter_context(nc.sbuf_tensor(f"{tag}_hid", [P, 2, FC, NG * P // 2], F32))
        with nc.Fori(0, NE // 2) as pair:
            e0 = pair * 2
            steps = []
            for k, w in enumerate((E.wA, E.wB)):
                up, down = views(w)
                for half in range(2):
                    steps.append({"up": [up], "down": down, "half": half, "into": E.x,
                                  "b1": lambda m, k=k: E.cols[:, bass.ds((e0 + k) * FC + (b1_at + m), 1)],
                                  "weight": lambda g, k=k: comb[:, g, bass.ds(e0 + k, 1)]})
            steps[2]["await"] = (s["load_b"], 32)
            mlp_block(E, s, (hid, None), nT, steps, FC, func,
                      loads=[(0, s["load_b"], load(E.wB, e0 + 1)), (NG, s["load_a"], load(E.wA, e0 + 2))])
            end_round(nc, handles)
        if shared is not None:
            up, down = views(E.wA)
            steps = [{"up": [up], "down": down, "half": half, "into": E.x, "b1": lambda m: E.cols[:, b1_at + NE * FC + m:b1_at + NE * FC + m + 1],
                      "weight": lambda g: shared} for half in range(2)]
            mlp_block(E, s, (hid, None), nT, steps, FC, func)
            end_round(nc, handles)


def decoder_mlp(E, tag, w1, w2, b1, rows):
    nc, h = E.nc, E.h
    with ExitStack() as st:
        nT = st.enter_context(nc.sbuf_tensor(f"{tag}_nT", [P, DC, NG * P], F32))
        feature_major(E, tag + "t", nT, source=h)
        hid = st.enter_context(nc.sbuf_tensor(f"{tag}_hid", [P, 2, FC, NG * P // 2], F32))
        s, handles = signals(st, nc, tag, MLP_SIGNALS)
        steps = [{"up": [w1], "down": w2, "half": half, "into": h, "b1": b1, "weight": lambda g: 1.0} for half in range(2)]
        stats = st.enter_context(nc.sbuf_tensor(f"{tag}_stats", [P, NG, 9], F32))
        mlp_block(E, s, (hid, None), nT, steps, FC, ACT.Relu, norm=(rows, stats))
        end_round(nc, handles)


def decoder(E, A):
    nc = E.nc
    with ExitStack() as st:
        s, handles = signals(st, nc, "dec", "ints dve_step var_ready added_eps power_ready")
        ints = st.enter_context(nc.sbuf_tensor("mask_ints", [P, NB, LQ], I32))
        E.keep = st.enter_context(nc.sbuf_tensor("mask_keep", [P, NB, LQ], F32))
        E.floor = st.enter_context(nc.sbuf_tensor("mask_floor", [P, NB, LQ], F32))
        stats = st.enter_context(nc.sbuf_tensor("dec_stats", [P, NG, 9], F32))
        with nc.Block(no_gpsimd_drain=True) as block:

            @block.sync
            def _(sp):
                for i in range(4):
                    sp.dma_start(ints[LQ * i:LQ * (i + 1)], A["mask_BxSxS_ik0"].rearrange("b q k -> q b k")).then_inc(s["ints"], 16)

            @block.vector
            def _(dve):
                v = nc.vector
                link = chain(dve, s["dve_step"])
                dve.wait_ge(s["ints"], 64)
                link(v.tensor_scalar(E.keep[:], ints[:], 0.0, None, ALU.not_equal))
                link(v.tensor_scalar(E.floor[:], E.keep[:], -1.0, 10000.0, ALU.add, ALU.mult))
                for g in range(NG):
                    link(layer_norm(dve, link, v, s, g, E.h[:, g], E.x[:, g], stats[:, g]))

            @block.gpsimd
            def _(pool):
                for g in range(NG):
                    power(E, pool, s, g, stats[:, g, 8:9], stats[:, g, 7:8], 1e-5)
        end_round(nc, handles)

        four = lambda w: [w[:, i * 512:(i + 1) * 512].rearrange("p (c n) -> p c n", c=DC) for i in range(4)]

        def attention_load(key, W, R, layer):
            return [(W[:, 0:2048].rearrange("p (a c n) -> p a c n", a=4, c=DC), A[f"{key}_w"][bass.ds(layer, 1)].rearrange("l a (c p) n -> (l p) a c n", p=P)),
                    (R[:, 0:4], A[f"{key}_rows"][bass.ds(layer, 1)].rearrange("l r d -> l (r d)").partition_broadcast(P).rearrange("p l (r d) -> p (l r) d", r=4))]

        def mlp_load(layer):
            return [(E.wB[:, 0:2 * FF].rearrange("p (c n) -> p c n", c=DC), A["L1_xattn_w1"][bass.ds(layer, 1)].rearrange("a (c p) n -> (a p) c n", p=P)),
                    (E.wB[:, 2 * FF:4 * FF].rearrange("p (c n) -> p c n", c=FC), A["L1_xattn_w2"][bass.ds(layer, 1)].rearrange("a (c p) n -> (a p) c n", p=P)),
                    (E.rB[:, 0:3], A["mlp_rows"][bass.ds(layer, 1)].rearrange("l r d -> l (r d)").partition_broadcast(P).rearrange("p l (r d) -> p (l r) d", r=3))]

        def rows(R):
            return {"bv": R[:, 0], "bo": R[:, 1], "g": R[:, 2], "b": R[:, 3]}

        send_for(E, "sa", attention_load("sa", E.wC, E.rC, 0))
        bias = st.enter_context(nc.sbuf_tensor("layer_bias", [P, 24], F32))
        with nc.Fori(0, NL) as layer:
            await_weights(E, "sa")
            send_for(E, "ca", attention_load("ca", E.wA, E.rA, layer))
            send_for(E, "mlp", mlp_load(layer))
            b, bh = signals(st, nc, "bias", "moved")
            with nc.Block(no_gpsimd_drain=True) as block:

                @block.vector
                def _(dve):
                    for i, name in enumerate(("sa_b0", "ca_b0", "L1_b1_0")):
                        nc.vector.tensor_copy(bias[:, 8 * i:8 * i + 8], E.cols[:, bass.ds(layer * 8 + COL_AT[name][0], 8)]).then_inc(b["moved"], 1)
                    dve.wait_ge(b["moved"], 3)
            end_round(nc, bh)
            w = four(E.wC)
            self_attention(E, "sa", w, rows(E.rC), bq=bias[:, 0:2], bk=bias[:, 2:4], mask=True, source=E.h, finish="norm")
            await_weights(E, "ca")
            send_for(E, "sa", attention_load("sa", E.wC, E.rC, layer + 1))
            w = four(E.wA)
            context_attention(E, "ca", *w, rows(E.rA), bq=bias[:, 8:10], bk=bias[:, 10:12], source=E.h, finish="norm")
            await_weights(E, "mlp")
            decoder_mlp(E, "dm", E.wB[:, 0:2 * FF].rearrange("p (c n) -> p c n", c=DC), E.wB[:, 2 * FF:4 * FF].rearrange("p (c n) -> p c n", c=FC),
                        lambda m: bias[:, 16 + m:17 + m], {"b2": E.rB[:, 0], "g": E.rB[:, 1], "b": E.rB[:, 2]})
        await_weights(E, "sa")
        t, th = signals(st, nc, "dec_end", "added")
        with nc.Block(no_gpsimd_drain=True) as block:

            @block.vector
            def _(dve):
                nc.vector.tensor_tensor(E.x[:], E.x[:], E.h[:], ALU.add).then_inc(t["added"], 1)
                dve.wait_ge(t["added"], 1)
        end_round(nc, th)


def prepare_decay(E, gamma_sb, decay):
    nc = E.nc
    with ExitStack() as st:
        s, handles = signals(st, nc, "decay", "sig act_step neg")
        with nc.Block(no_gpsimd_drain=True) as block:

            @block.scalar
            def _(act):
                nc.scalar.activation(gamma_sb[:], gamma_sb[:], ACT.Sigmoid).then_inc(s["sig"], 1)
                act.wait_ge(s["neg"], 1)
                for t in range(4):
                    nc.scalar.activation(decay[:, t], E.c("lag"), ACT.Exp, scale=gamma_sb[:, t:t + 1])

            @block.vector
            def _(dve):
                dve.wait_ge(s["sig"], 1)
                nc.vector.tensor_scalar(gamma_sb[:], gamma_sb[:], -1.0, None, ALU.mult).then_inc(s["neg"], 1)
        end_round(nc, handles)


def prepare_lengths(E, mask_ints, length, inverse):
    nc, ps = E.nc, E.ps
    with ExitStack() as st:
        s, handles = signals(st, nc, "len", "dve_step diag summed")
        m = st.enter_context(nc.sbuf_tensor("len_m", [NB, LK], F32))
        n = st.enter_context(nc.sbuf_tensor("len_n", [NB, 1], F32))
        diag = st.enter_context(nc.sbuf_tensor("len_diag", [NB, NB], F32))
        ones = st.enter_context(nc.sbuf_tensor("len_ones", [NB, P], F32))
        with nc.Block(no_gpsimd_drain=True) as block:

            @block.vector
            def _(dve):
                v = nc.vector
                link = chain(dve, s["dve_step"])
                link(v.memset(ones[:], 1.0))
                link(v.tensor_scalar(m[:], mask_ints[:], -1.0, 1.0, ALU.mult, ALU.add))
                link(v.tensor_reduce(n[:], m[:], AX.X, ALU.add))
                link(v.tensor_scalar(n[:], n[:], -1.0, None, ALU.add))
                v.tensor_scalar(diag[:], E.c("ident")[0:NB, 0:NB], n[:, 0:1], None, ALU.mult).then_inc(s["diag"], 1)
                dve.wait_ge(s["summed"], 1)
                link(v.tensor_copy(length[:], ps[:, 0, 0:NB]))
                link(v.reciprocal(inverse[:], length[:]))

            @block.tensor
            def _(pe):
                pe.wait_ge(s["diag"], 1)
                nc.tensor.matmul(ps[:, 0, 0:NB], ones[:], diag[:], start=True, stop=True).then_inc(s["summed"], 1)
        end_round(nc, handles)


def prepare_centred(E, raw, centred, bias_in, bias_out):
    nc, ps = E.nc, E.ps
    with ExitStack() as st:
        s, handles = signals(st, nc, "cent", "done copied")
        with nc.Block(no_gpsimd_drain=True) as block:

            @block.tensor
            def _(pe):
                for i, w in enumerate(raw):
                    for c in range(DC):
                        for m in range(DC):
                            last = nc.tensor.matmul(ps[:, 2 * i + c, m * P:(m + 1) * P], w[:, m, c * P:(c + 1) * P], E.c("centre"), start=True, stop=True)
                for i, b in enumerate(bias_in):
                    last = nc.tensor.matmul(ps[:, 4, 2 * i:2 * i + 2], E.c("centre"), b, start=True, stop=True)
                last.then_inc(s["done"], 1)

            @block.vector
            def _(dve):
                dve.wait_ge(s["done"], 1)
                for i, w in enumerate(centred):
                    nc.vector.tensor_copy(w[:], ps[:, 2 * i:2 * i + 2, 0:D])
                nc.vector.tensor_copy(bias_out[:], ps[:, 4, 0:4]).then_inc(s["copied"], 1)
                dve.wait_ge(s["copied"], 1)
        end_round(nc, handles)


def fourier_attention(E, w, rows, bq, bk, proj):
    nc, ps = E.nc, E.ps
    wq, wk, wv, wo = w
    NCHK = 4
    ROUND = 2
    CH = ROUND * NCHK
    MAGIC = 12582912.0
    TURN = 6.283185
    with ExitStack() as st:
        s, handles = signals(st, nc, "four", "n_ready nT_psum nT_ready qk_psum qk_ready v_psum v_ready p_done turns_ready rounded frac_ready sin_ready abs_ready cos_ready "
                             "scores_done masked o_done o_ready oT_psum oT_ready y_ready x_done dve_step var_ready added_eps power_ready")

        def sb(name, shape):
            return st.enter_context(nc.sbuf_tensor(f"four_{name}", [P] + shape, F32))

        n_sb, stats, nT = sb("n", [ROUND, D]), sb("stats", [ROUND, 9]), sb("nT", [DC, P])
        qk, v_sb = sb("qk", [ROUND, 4, P]), sb("v", [ROUND, D])
        turns, frac, rnd = sb("turns", [2, 1024]), sb("frac", [2, 1024]), sb("rnd", [1024])
        sin, cos, sc, o_sb, oT, ytmp = sb("sin", [2, 1024]), sb("cos", [2, 1024]), sb("sc", [2, 4, P]), sb("o", [D]), sb("oT", [DC, P]), sb("ytmp", [D])
        half_pi = sb("half_pi", [1])
        fill(E, "four", [(half_pi[:], float(np.pi / 2))])
        with nc.Fori(0, NG // ROUND) as pair:
            g0 = pair * ROUND
            with nc.Block(no_gpsimd_drain=True) as block:

                @block.tensor
                def _(pe):
                    mm, tr = nc.tensor.matmul, nc.tensor.transpose
                    for gi in range(ROUND):
                        pe.wait_ge(s["n_ready"], gi + 1)
                        if gi:
                            pe.wait_ge(s["v_ready"], gi)
                            pe.wait_ge(s["qk_ready"], gi)
                        for c in range(DC):
                            last = tr(ps[:, 7, c * P:(c + 1) * P], n_sb[:, gi, c * P:(c + 1) * P], E.c("ident"))
                        last.then_inc(s["nT_psum"], 1)
                        pe.wait_ge(s["nT_ready"], gi + 1)
                        for i, wi in enumerate((wq, wk)):
                            for m in range(DC):
                                for c in range(DC):
                                    last = mm(ps[:, 6, (2 * i + m) * P:(2 * i + m + 1) * P], wi[:, c, m * P:(m + 1) * P], nT[:, c], start=c == 0, stop=c == DC - 1)
                        last.then_inc(s["qk_psum"], 1)
                        for c in range(DC):
                            last = mm(ps[:, 7, 0:D], nT[:, c], wv[:, c], start=c == 0, stop=c == DC - 1)
                        last.then_inc(s["v_psum"], 1)
                    pe.wait_ge(s["qk_ready"], ROUND)

                    def project(hc):
                        if hc >= 2:
                            pe.wait_ge(s["turns_ready"], hc - 1)
                        for i in range(2):
                            for a in range(4):
                                h = 4 * (hc % NCHK) + a
                                last = mm(ps[:, 2 * (hc % 2) + i, a * P:(a + 1) * P], proj[:, h % 8], qk[:, hc // NCHK, 2 * i + h // 8], start=True, stop=True)
                        last.then_inc(s["p_done"], 1)

                    def scores(hc):
                        pe.wait_ge(s["sin_ready"], hc + 1)
                        pe.wait_ge(s["cos_ready"], hc + 1)
                        if hc >= 2:
                            pe.wait_ge(s["masked"], hc - 1)
                        for a in range(4):
                            for i, f in enumerate((cos, sin)):
                                last = mm(ps[:, 4 + hc % 2, a * P:(a + 1) * P], f[:, hc % 2, 512 + a * P:512 + (a + 1) * P], f[:, hc % 2, a * P:(a + 1) * P], start=i == 0, stop=i == 1)
                        last.then_inc(s["scores_done"], 1)

                    def values(hc):
                        pe.wait_ge(s["masked"], hc + 1)
                        gi = hc // NCHK
                        if hc == 0:
                            pe.wait_ge(s["v_ready"], ROUND)
                        if hc == NCHK:
                            pe.wait_ge(s["o_ready"], 1)
                        for a in range(4):
                            h = 4 * (hc % NCHK) + a
                            last = mm(ps[:, 6, gi * D + h * 16:gi * D + h * 16 + 16], sc[:, hc % 2, a], v_sb[:, gi, h * 16:h * 16 + 16], start=True, stop=True)
                        last.then_inc(s["o_done"], 1)

                    def transpose_o(gi):
                        pe.wait_ge(s["o_ready"], gi + 1)
                        if gi:
                            pe.wait_ge(s["x_done"], gi)
                        for c in range(DC):
                            last = tr(ps[:, 7, c * P:(c + 1) * P], o_sb[:, c * P:(c + 1) * P], E.c("ident"))
                        last.then_inc(s["oT_psum"], 1)

                    def output(gi):
                        pe.wait_ge(s["oT_ready"], gi + 1)
                        for c in range(DC):
                            last = mm(ps[:, 7, D:2 * D], oT[:, c], wo[:, c], start=c == 0, stop=c == DC - 1)
                        last.then_inc(s["y_ready"], 1)

                    project(0)
                    project(1)
                    for k in range(CH + 1):
                        if k + 2 < CH:
                            project(k + 2)
                        if k < CH:
                            scores(k)
                        if k:
                            values(k - 1)
                        if k == NCHK + 2:
                            transpose_o(0)
                        if k == NCHK + 3:
                            output(0)
                    transpose_o(1)
                    output(1)

                @block.vector
                def _(dve):
                    v = nc.vector
                    link = chain(dve, s["dve_step"])
                    xg = [E.x[:, bass.ds(g0 + gi, 1)].rearrange("p a d -> p (a d)") for gi in range(ROUND)]
                    for gi in range(ROUND):
                        layer_norm(dve, link, v, s, gi, n_sb[:, gi], xg[gi], stats[:, gi]).then_inc(s["n_ready"], 1)
                    for gi in range(ROUND):
                        dve.wait_ge(s["v_psum"], gi + 1)
                        v.tensor_tensor(v_sb[:, gi], ps[:, 7, 0:D], rows["bv"], ALU.add).then_inc(s["v_ready"], 1)

                    def reduce_angles(hc):
                        u, f = turns[:, hc % 2], frac[:, hc % 2]
                        dve.wait_ge(s["turns_ready"], hc + 1)
                        link(v.tensor_scalar(rnd[:], u, MAGIC, -MAGIC, ALU.add, ALU.add))
                        if hc >= 2:
                            dve.wait_ge(s["cos_ready"], hc - 1)
                        v.tensor_tensor(f, u, rnd[:], ALU.subtract).then_inc(s["frac_ready"], 1)
                        dve.wait_ge(s["frac_ready"], hc + 1)
                        v.scalar_tensor_tensor(u, f, -1.0, f, ALU.mult, ALU.max).then_inc(s["abs_ready"], 1)

                    def mask(hc):
                        dve.wait_ge(s["scores_done"], hc + 1)
                        if hc >= 2:
                            dve.wait_ge(s["o_done"], hc - 1)
                        v.scalar_tensor_tensor(sc[:, hc % 2], ps[:, 4 + hc % 2].rearrange("p (a q) -> p a q", a=4), 1.0 / 128,
                                               E.c("same_seq").unsqueeze(1).to_broadcast([P, 4, P]), ALU.mult, ALU.mult).then_inc(s["masked"], 1)

                    def output(gi):
                        dve.wait_ge(s["y_ready"], gi + 1)
                        link(v.tensor_tensor(ytmp[:], ps[:, 7, D:2 * D], rows["bo"], ALU.add))
                        v.tensor_tensor(xg[gi], xg[gi], ytmp[:], ALU.add).then_inc(s["x_done"], 1)
                        dve.wait_ge(s["x_done"], gi + 1)

                    reduce_angles(0)
                    for k in range(CH):
                        if k + 1 < CH:
                            reduce_angles(k + 1)
                        mask(k)
                    output(0)
                    output(1)

                @block.gpsimd
                def _(pool):
                    for gi in range(ROUND):
                        power(E, pool, s, gi, stats[:, gi, 8:9], stats[:, gi, 7:8], 1e-5)

                @block.scalar
                def _(act):
                    a = nc.scalar.activation
                    for gi in range(ROUND):
                        act.wait_ge(s["nT_psum"], gi + 1)
                        nc.scalar.copy(nT[:].rearrange("p c t -> p (c t)"), ps[:, 7, 0:D]).then_inc(s["nT_ready"], 1)
                        act.wait_ge(s["qk_psum"], gi + 1)
                        for i in range(4):
                            b = (bq, bk)[i // 2]
                            last = a(qk[:, gi, i], ps[:, 6, i * P:(i + 1) * P], ACT.Identity, bias=b[:, i % 2:i % 2 + 1])
                        last.then_inc(s["qk_ready"], 1)

                    def to_turns(hc):
                        act.wait_ge(s["p_done"], hc + 1)
                        if hc >= 2:
                            act.wait_ge(s["cos_ready"], hc - 1)
                        nc.scalar.mul(turns[:, hc % 2], ps[:, 2 * (hc % 2):2 * (hc % 2) + 2].rearrange("p a b -> p (a b)"), float(0.25 / (2 * np.pi))).then_inc(s["turns_ready"], 1)

                    def take_o(gi):
                        act.wait_ge(s["o_done"], (gi + 1) * NCHK)
                        nc.scalar.copy(o_sb[:], ps[:, 6, gi * D:(gi + 1) * D]).then_inc(s["o_ready"], 1)

                    def take_oT(gi):
                        act.wait_ge(s["oT_psum"], gi + 1)
                        nc.scalar.copy(oT[:].rearrange("p c t -> p (c t)"), ps[:, 7, 0:D]).then_inc(s["oT_ready"], 1)

                    to_turns(0)
                    to_turns(1)
                    for k in range(CH):
                        act.wait_ge(s["frac_ready"], k + 1)
                        if k >= 2:
                            act.wait_ge(s["scores_done"], k - 1)
                        a(sin[:, k % 2], frac[:, k % 2], ACT.Sin, scale=TURN).then_inc(s["sin_ready"], 1)
                        act.wait_ge(s["abs_ready"], k + 1)
                        a(cos[:, k % 2], turns[:, k % 2], ACT.Sin, scale=-TURN, bias=half_pi[:]).then_inc(s["cos_ready"], 1)
                        if k == NCHK:
                            take_o(0)
                        if k + 2 < CH:
                            to_turns(k + 2)
                        if k == NCHK + 2:
                            take_oT(0)
                    take_o(1)
                    take_oT(1)

            end_round(nc, handles)


def gated_mlp(E, w_ints, up, down):
    nc = E.nc
    HC = HID // P
    with ExitStack() as st:
        s, handles = signals(st, nc, "glu", MLP_SIGNALS)
        t, pre = signals(st, nc, "deq", "scaled")
        nT = st.enter_context(nc.sbuf_tensor("glu_nT", [P, DC, NG * P], F32))
        hid = st.enter_context(nc.sbuf_tensor("glu_hid", [P, 2, HC, NG * P // 2], F32))
        sil = st.enter_context(nc.sbuf_tensor("glu_sil", [P, 2, NG * P // 2], F32))
        with nc.Block(no_gpsimd_drain=True) as block:

            @block.vector
            def _(dve):
                for i, (dst, src) in enumerate(w_ints):
                    nc.vector.tensor_scalar(dst, src, float(np.float32(1.0 / 127.0)), None, ALU.mult).then_inc(t["scaled"], 1)
                dve.wait_ge(t["scaled"], len(w_ints))
        end_round(nc, pre)
        feature_major(E, "glut", nT)
        steps = [{"up": up, "down": down, "half": half, "into": E.x, "weight": lambda g: 1.0} for half in range(2)]
        mlp_block(E, s, (hid, sil), nT, steps, HC, None, glu=True)
        end_round(nc, handles)


def gated_recurrence(E, w, rows):
    nc, ps = E.nc, E.ps
    w_dx, w_x, w_gx, w_ga, w_o, pe_dx, pe_x = w
    HALF = NG * P // 2
    col = E.col
    with ExitStack() as st:
        def sb(name, shape):
            return st.enter_context(nc.sbuf_tensor(f"rec_{name}", [P] + shape, F32))

        nT = sb("nT", [DC, NG * P])
        feature_major(E, "rect", nT)
        s, handles = signals(st, nc, "rec", "expit rest_ready root_ready xh_psum xh_ready gates_psum gates_ready scan_done y_ready x_done dve_step var_ready added_eps power_ready")
        expit, keep = sb("expit", [DC]), sb("keep", [DC])
        xh, gx, ga = sb("xh", [DC, HALF]), sb("gx", [DC, HALF]), sb("ga", [DC, HALF])
        co, hh, ytmp = sb("co", [DC, HALF]), sb("hh", [2, DC, HALF]), sb("ytmp", [2, D])
        with nc.Block(no_gpsimd_drain=True) as block:

            @block.tensor
            def _(pe):
                mm = nc.tensor.matmul
                for half in range(2):
                    if half:
                        pe.wait_ge(s["xh_ready"], half)
                    for m in range(DC):
                        for c in range(DC):
                            mm(ps[:, m], w_x[:, c, m * P:(m + 1) * P], nT[:, c, half * HALF:(half + 1) * HALF], start=c == 0, stop=False)
                        last = mm(ps[:, m], pe_x[:, m * P:(m + 1) * P], E.c("pe")[0:16].unsqueeze(1).to_broadcast([16, HALF // P, P]), start=False, stop=True)
                    last.then_inc(s["xh_psum"], 1)
                    pe.wait_ge(s["xh_ready"], half + 1)
                    if half:
                        pe.wait_ge(s["gates_ready"], half)
                    for i, wg in enumerate((w_gx, w_ga)):
                        for m in range(DC):
                            for c in range(DC):
                                last = mm(ps[:, 2 + 2 * i + m], wg[:, c, m * P:(m + 1) * P], xh[:, c], start=c == 0, stop=c == DC - 1)
                    last.then_inc(s["gates_psum"], 1)
                for half in range(2):
                    pe.wait_ge(s["scan_done"], half + 1)
                    for t in range(HALF // P):
                        n = half * (HALF // P) + t
                        if n >= 2:
                            pe.wait_ge(s["x_done"], n - 1)
                        g = n
                        o = ps[:, 6 + n % 2, 0:D]
                        for c in range(DC):
                            mm(o, nT[:, c, g * P:(g + 1) * P], w_dx[:, c], start=c == 0, stop=False)
                        mm(o, E.c("pe")[0:16], pe_dx, start=False, stop=False)
                        for c in range(DC):
                            last = mm(o, hh[:, half, c, t * P:(t + 1) * P], w_o[:, c], start=False, stop=c == DC - 1)
                        last.then_inc(s["y_ready"], 1)

            @block.gpsimd
            def _(pool):
                power(E, pool, s, 0, keep[:], keep[:], 0.0, "half")

            @block.scalar
            def _(act):
                a = nc.scalar.activation
                a(expit[:], col("L3_attn_a_logit"), ACT.Sigmoid).then_inc(s["expit"], 1)
                for half in range(2):
                    act.wait_ge(s["gates_psum"], half + 1)
                    if half:
                        act.wait_ge(s["scan_done"], half)
                    for i, (dst, b) in enumerate(((gx, "L3_attn_b_gx"), (ga, "L3_attn_b_ga"))):
                        for m in range(DC):
                            last = a(dst[:, m], ps[:, 2 + 2 * i + m], ACT.Sigmoid, bias=col(b)[:, m:m + 1])
                    last.then_inc(s["gates_ready"], 1)
                    act.wait_ge(s["rest_ready"], half + 1)
                    a(co[:], co[:], ACT.Sqrt).then_inc(s["root_ready"], 1)

            @block.vector
            def _(dve):
                v = nc.vector
                link = chain(dve, s["dve_step"])
                dve.wait_ge(s["expit"], 1)
                link(v.tensor_tensor(keep[:], expit[:], expit[:], ALU.mult))
                v.tensor_scalar(keep[:], keep[:], -1.0, 1.0, ALU.mult, ALU.add).then_inc(s["var_ready"], 1)
                dve.wait_ge(s["power_ready"], 1)
                for half in range(2):
                    dve.wait_ge(s["xh_psum"], half + 1)
                    for m in range(DC):
                        last = v.tensor_scalar(xh[:, m], ps[:, m], col("L3_attn_b_x")[:, m:m + 1], keep[:, m:m + 1], ALU.add, ALU.mult)
                    last.then_inc(s["xh_ready"], 1)
                    dve.wait_ge(s["gates_ready"], half + 1)
                    for m in range(DC):
                        last = v.tensor_scalar(ga[:, m], ga[:, m], expit[:, m:m + 1], None, ALU.mult)
                    link(last)
                    link(v.tensor_tensor(co[:], ga[:], ga[:], ALU.mult))
                    v.tensor_scalar(co[:], co[:], -1.0, 1.0, ALU.mult, ALU.add).then_inc(s["rest_ready"], 1)
                    link(v.tensor_tensor(gx[:], gx[:], xh[:], ALU.mult))
                    dve.wait_ge(s["root_ready"], half + 1)
                    link(v.tensor_tensor(co[:], co[:], gx[:], ALU.mult))
                    for m in range(DC):
                        last = v.memset(ga[:, m].rearrange("p (b t) -> p b t", t=LQ)[:, :, 0:1], 0.0)
                    link(last)
                    for m in range(DC):
                        last = v.tensor_tensor_scan(hh[:, half, m], ga[:, m], co[:, m], 0.0, ALU.mult, ALU.add)
                    last.then_inc(s["scan_done"], 1)
                for n in range(NG):
                    dve.wait_ge(s["y_ready"], n + 1)
                    y = ytmp[:, n % 2]
                    link(v.tensor_tensor(y, ps[:, 6 + n % 2, 0:D], rows["b_dx"], ALU.add))
                    link(v.tensor_tensor(y, y, rows["b_o"], ALU.add))
                    v.scalar_tensor_tensor(E.x[:, n], y, 0.5, E.x[:, n], ALU.mult, ALU.add).then_inc(s["x_done"], 1)
                dve.wait_ge(s["x_done"], NG)
        end_round(nc, handles)


def prepare_softplus(E, out):
    nc = E.nc
    with ExitStack() as st:
        s, handles = signals(st, nc, "sp", "abs exp ln dve_step")
        a = st.enter_context(nc.sbuf_tensor("sp_a", [P, DC], F32))
        with nc.Block(no_gpsimd_drain=True) as block:

            @block.vector
            def _(dve):
                v = nc.vector
                link = chain(dve, s["dve_step"])
                v.scalar_tensor_tensor(a[:], E.col("temperature"), -1.0, E.col("temperature"), ALU.mult, ALU.max).then_inc(s["abs"], 1)
                link(v.tensor_scalar(out[:], E.col("temperature"), 0.0, None, ALU.max))
                dve.wait_ge(s["ln"], 1)
                link(v.tensor_tensor(out[:], out[:], a[:], ALU.add))

            @block.scalar
            def _(act):
                act.wait_ge(s["abs"], 1)
                nc.scalar.activation(a[:], a[:], ACT.Exp, scale=-1.0).then_inc(s["exp"], 1)
                act.wait_ge(s["exp"], 1)
                nc.scalar.activation(a[:], a[:], ACT.Ln, bias=E.c("one")).then_inc(s["ln"], 1)
        end_round(nc, handles)


def build(nc, A, only=None):
    with ExitStack() as st:
        def sb(name, shape, dt=F32):
            return st.enter_context(nc.sbuf_tensor(name, shape, dt))

        E = Core()
        E.nc, E.st, E.loads = nc, st, {}
        E.ps = st.enter_context(nc.psum_tensor("banks", [P, 8, 512], F32))
        E.x, E.h = sb("x_state", [P, NG, D]), sb("h_state", [P, NG, D])
        E.z = E.h
        E.ctx = sb("ctx_tiles", [P, 2, DC, CT])
        E.ctx_dram = A["ctx"]
        E.wA, E.wB, E.wC = sb("weights_a", [P, WA]), sb("weights_b", [P, WB]), sb("weights_c", [P, WC])
        E.rA, E.rB, E.rC = (sb(f"rows_{k}", [P, ROW, D]) for k in "abc")
        const, cols, small, short = sb("const", [P, CONST_W]), sb("cols", [P, COL_W]), sb("small", [P, SMALL_W]), sb("short", [P, SHORT_W])
        b2 = sb("expert_b2", [NE, 2, D])
        gamma_sb, decay = sb("gamma", [P, 4]), sb("decay", [P, 4, LQ])
        comb = sb("comb", [P, NG, NE])
        proj = sb("proj", [P, 8, P])
        E.cols = cols
        E.c = lambda n: const[:, CONST_AT[n][0]:sum(CONST_AT[n])]
        E.col = lambda n: cols[:, COL_AT[n][0]:sum(COL_AT[n])]
        E.small = lambda n: small[:, SMALL_AT[n][0]:sum(SMALL_AT[n])].rearrange("p (c n) -> p c n", c=DC)
        E.short = lambda n: short[:, SHORT_AT[n][0]:sum(SHORT_AT[n])]

        def cut(w, at, names, out=D):
            return [(w[:, at + i * DC * out:at + (i + 1) * DC * out].rearrange("p (c n) -> p c n", c=DC), chunked(A[n])) for i, n in enumerate(names)]

        def rows(r, at, names):
            i = ROWS.index(names[0])
            return [(r[:, at:at + len(names)], A["rows"][i:i + len(names)].rearrange("r d -> (r d)").partition_broadcast(P).rearrange("p (r d) -> p r d", d=D))]

        def expert0(w1, w2):
            return [(E.wA[:, 0:2 * FF].rearrange("p (c n) -> p c n", c=DC), chunked(A[w1][0])),
                    (E.wA[:, 2 * FF:4 * FF].rearrange("p (c n) -> p c n", c=FC), chunked(A[w2][0]))]

        L0x = cut(E.wA, 0, ["L0_xattn_Wk2", "L0_xattn_Wv2", "L0_xattn_Wq1", "L0_xattn_Wk1", "L0_xattn_Wv1"], 512)
        L0x_wo = E.wA[:, 5120:6144].rearrange("p (c n) -> p c n", c=4)
        L0a = cut(E.wC, 0, ["L0_attn_Wq", "L0_attn_Wk", "L0_attn_Wv", "L0_attn_Wg"])
        L1a = cut(E.wA, 4096, ["L1_attn_Wq", "L1_attn_Wk", "L1_attn_Wv", "L1_attn_Wo"])
        L1f = cut(E.wC, 0, ["L1_ffn_mix_w"])
        L2x = cut(E.wA, 4096, ["L2_xattn_Wq", "L2_xattn_Wk", "L2_xattn_Wv", "L2_xattn_Wo"])
        L2a = cut(E.wC, 0, ["L2_attn_Wq", "L2_attn_Wk", "L2_attn_Wv", "L2_attn_Wo"])
        L3x = cut(E.wB, 2048, ["L3_xattn_Wq", "L3_xattn_Wk", "L3_xattn_Wv", "L3_xattn_Wproj"])
        L3a = cut(E.wA, 3072, ["L3_attn_W_dx", "L3_attn_W_x", "L3_attn_W_gx", "L3_attn_W_ga", "L3_attn_W_o"])
        L3a_pe = [(E.wA[0:16, 5632 + i * D:5632 + (i + 1) * D], A[n]) for i, n in enumerate(("L3_attn_W_dx_pe", "L3_attn_W_x_pe"))]
        L3f = cut(E.wC, 0, ["L3_ffn_Wq", "L3_ffn_Wk", "L3_ffn_Wv", "L3_ffn_Wp"])
        ints = [(E.wA[:, i * 2 * HID:(i + 1) * 2 * HID].bitcast(I32).rearrange("p (c n) -> p c n", c=DC), chunked(A[n])) for i, n in enumerate(("w_gate", "w_up"))]
        ints.append((E.wB[:, 0:2 * HID].bitcast(I32).rearrange("p (c n) -> p c n", c=HID // P), chunked(A["w_down"])))

        def at(pairs):
            return [p[0] for p in pairs]

        fill(E, "proj", [(proj[:], 0.0)])
        first = [(const[:], A["const"]), (E.x[:], A["x"].rearrange("(g p) d -> p g d", p=P)), (cols[:], A["cols"]), (small[:], A["small"]),
                 (short[:], A["short"].partition_broadcast(P)), (E.ctx[:, 0], A["ctx"][0]), (b2[:], A["expert_b2"])]
        first += [(gamma_sb[LQ * i:LQ * (i + 1)], A["gamma"][i].partition_broadcast(LQ)) for i in range(4)]
        first += [(proj[16 * h:16 * h + 16, h], A["L2_attn_proj_mat"]) for h in range(8)]
        send_for(E, "first", first)
        send_for(E, "L0x", L0x + [(L0x_wo, chunked(A["L0_xattn_Wo"]))] + rows(E.rA, 0, ["L0_xattn_bo"]))
        send_for(E, "L0a", L0a + rows(E.rC, 0, ["L0_attn_bv"]))
        await_weights(E, "first")
        run = lambda n: only is None or n in only

        await_weights(E, "L0x")
        if run(0):
            wk2, wv2, wq1, wk1, wv1 = at(L0x)
            joint_attention(E, "l0x", wq1, wk2, wv2, L0x_wo, (wk1, wv1), {"bo": E.rA[:, 0]})
        await_weights(E, "L0a")
        send_for(E, "L0f", expert0("L0_w1", "L0_w2") + rows(E.rB, 0, ["L0_ffn_sb2"]))
        if run(1):
            prepare_decay(E, gamma_sb, decay)
            self_attention(E, "l0a", at(L0a), {"bv": E.rC[:, 0]}, bq=E.col("L0_attn_bq"), bk=E.col("L0_attn_bk"), rope="rot_pairs", decay=decay, gate_bias=E.col("L0_attn_bg"))
        await_weights(E, "L0f")
        if run(2):
            with nc.sbuf_tensor("l0f_nT", [P, DC, NG * P], F32) as nT:
                feature_major(E, "l0ft", nT, gating=(E.small("L0_gate"), E.short("gate_b"), "sigmoid", comb[:], b2[:, 0]), extra_bias=(E.rB[:, 0], 0.1))
                expert_mixture(E, "l0f", A["L0_w1"], A["L0_w2"], COL_AT["L0_ffn_b1_0"][0], comb, nT, ACT.Gelu, shared=0.1)
        send_for(E, "L1a", L1a + rows(E.rA, 4, ["L1_attn_bo"]))
        if run(3):
            decoder(E, A)
        await_weights(E, "L1a")
        send_for(E, "L1f", L1f + expert0("L1_w1", "L1_w2") + rows(E.rC, 0, ["L1_ffn_g1", "L1_ffn_be1", "L1_ffn_mix_b", "L1_ffn_g2", "L1_ffn_be2"]))
        if run(4):
            self_attention(E, "l1a", at(L1a), {"bo": E.rA[:, 4]}, rope="rot_halves", unit_norm=True)
        await_weights(E, "L1f")
        send_for(E, "L2x", L2x + rows(E.rA, 0, ["L2_xattn_bv", "L2_xattn_bo"]))
        if run(5):
            with nc.sbuf_tensor("l1f_nT", [P, DC, NG * P], F32) as nT:
                feature_major(E, "l1ft", nT, pre=(E.rC[:, 0], E.rC[:, 1], at(L1f)[0], E.rC[:, 2], E.rC[:, 3], E.rC[:, 4]),
                              gating=(E.small("L1_router"), None, "softmax", comb[:], b2[:, 1]))
                expert_mixture(E, "l1f", A["L1_w1"], A["L1_w2"], COL_AT["L1_ffn_b1_0"][0], comb, nT, ACT.Silu)
        await_weights(E, "L2x")
        send_for(E, "L2a", L2a + rows(E.rC, 0, ["L2_attn_bv", "L2_attn_bo"]))
        send_for(E, "L2f", ints)
        if run(6):
            with nc.sbuf_tensor("length", [P, NB], F32) as length, nc.sbuf_tensor("inverse", [P, NB], F32) as inverse, nc.sbuf_tensor("mask_s2", [NB, LK], I32) as m:
                send_for(E, "mask", [(m[:], A["mask_BxS2_if0"])])
                await_weights(E, "mask")
                prepare_lengths(E, m, length, inverse)
                context_attention(E, "l2x", *at(L2x), {"bv": E.rA[:, 0], "bo": E.rA[:, 1]}, bq=E.col("L2_xattn_bq"), bk=E.col("L2_xattn_bk"),
                                deform={"boff": E.short("boff"), "length": length, "inverse": inverse,
                                        "room": (E.h.rearrange("p g d -> p (g d)")[:, 0:NK * LK], E.wB[:, 2048:2048 + NK * LK], E.wB[:, 2048 + NK * LK:2048 + (NK + 2) * LK])})
        await_weights(E, "L2a")
        send_for(E, "L3x", L3x + rows(E.rB, 0, ["L3_xattn_bv", "L3_xattn_bproj"]))
        if run(7):
            fourier_attention(E, at(L2a), {"bv": E.rC[:, 0], "bo": E.rC[:, 1]}, E.col("L2_attn_bq"), E.col("L2_attn_bk"), proj)
        await_weights(E, "L2f")
        send_for(E, "L3f", L3f + rows(E.rC, 0, ["L3_ffn_bv", "L3_ffn_bp"]))
        send_for(E, "L3a", L3a + L3a_pe + rows(E.rA, 0, ["L3_attn_b_dx", "L3_attn_b_o"]))
        if run(8):
            gate, up, down = [i[0].bitcast(F32) for i in ints]
            gated_mlp(E, list(zip((gate, up, down), at(ints))), [gate, up], down)
        await_weights(E, "L3x")
        if run(9):
            with ExitStack() as own:
                cw = [own.enter_context(nc.sbuf_tensor(f"centred{i}", [P, DC, D], F32)) for i in range(2)]
                cb = own.enter_context(nc.sbuf_tensor("centred_bias", [P, 4], F32))
                wq, wk, wv, wp = at(L3x)
                prepare_centred(E, (wq, wk), cw, (E.col("L3_xattn_bq"), E.col("L3_xattn_bkv")[:, 0:2]), cb)
                context_attention(E, "l3x", cw[0][:], cw[1][:], wv, wp, {"bv": E.rB[:, 0], "bo": E.rB[:, 1]}, bq=cb[:, 0:2], bk=cb[:, 2:4],
                                norm=[E.col(n) for n in ("q_gamma", "q_beta", "k_gamma", "k_beta")])
        await_weights(E, "L3a")
        if run(10):
            gated_recurrence(E, at(L3a) + at(L3a_pe), {"b_dx": E.rA[:, 0], "b_o": E.rA[:, 1]})
        await_weights(E, "L3f")
        if run(11):
            with nc.sbuf_tensor("softplus", [P, DC], F32) as sp:
                prepare_softplus(E, sp)
                self_attention(E, "l3f", at(L3f), {"bv": E.rC[:, 0], "bo": E.rC[:, 1]}, bq=E.col("L3_ffn_bq"), bk=E.col("L3_ffn_bk"),
                               query_scale=(E.col("L3_ffn_query_embedding"), sp), heads_gate=E.short("brs"))
        send_for(E, "out", [(A["out"].rearrange("(g p) d -> p g d", p=P), E.x[:])])
        await_weights(E, "out")


def arrays_of(inputs):
    a = {k: np.asarray(v) for k, v in inputs.items()}
    f = lambda x: np.ascontiguousarray(x)

    def columns(v):
        return np.asarray(v).reshape(-1, P).T

    a.update(sa={}, ca={})
    vec = {n: a[n] for n in COL_NAMES_DIRECT}
    for layer in range(NL):
        vec[f"sa_b{layer}"], vec[f"ca_b{layer}"], vec[f"L1_b1_{layer}"] = a["L1_xattn_sa_b"][layer], a["L1_xattn_ca_b"][layer], a["L1_xattn_b1"][layer]
    for e in range(NE):
        vec[f"L0_ffn_b1_{e}"], vec[f"L1_ffn_b1_{e}"] = a["L0_ffn_b1"][e], a["L1_ffn_b1"][e]
    vec["temperature"] = np.repeat(a["L3_ffn_temperature"].reshape(-1), 16)
    for n in ("q_gamma", "q_beta", "k_gamma", "k_beta"):
        vec[n] = np.tile(a[f"L3_xattn_{n}"], 8)
    small = {"L0_gate": a["L0_ffn_gate_w"].T, "L1_router": a["L1_ffn_router_w"], "Woff": a["L2_xattn_Woff"].T,
             "Wrs": np.concatenate([a["L3_ffn_Wr"], a["L3_ffn_Ws"]]).T}
    row = dict(a, L3_xattn_bv=a["L3_xattn_bkv"][D:])
    again = lambda w: np.concatenate([w, w[:1]])
    g, b = a["L1_xattn_ln_g"], a["L1_xattn_ln_b"]
    out = {
        "x": a["x"].reshape(NB * LQ, D),
        "ctx": again(a["ctx_1024"].reshape(NG, CT, DC, P).transpose(0, 3, 2, 1)),
        "const": np.concatenate(list(CONST.values()), 1),
        "cols": np.concatenate([columns(vec[n]) for n, _ in COLS], 1),
        "small": np.concatenate([small[n].reshape(DC, P, -1).transpose(1, 0, 2).reshape(P, -1) for n, _ in SMALL], 1),
        "short": np.concatenate([a["L2_xattn_boff"], a["L0_ffn_gate_b"], a["L3_ffn_br"], a["L3_ffn_bs"]]),
        "rows": np.stack([row[n] for n in ROWS]),
        "gamma": a["L0_attn_gamma"].reshape(4, 4).T,
        "expert_b2": np.stack([a["L0_ffn_b2"], a["L1_ffn_b2"]], 1),
        "L0_w1": np.concatenate([a["L0_ffn_w1"], a["L0_ffn_sw1"][None]]),
        "L0_w2": np.concatenate([a["L0_ffn_w2"], a["L0_ffn_sw2"][None]]),
        "L1_w1": again(a["L1_ffn_w1"]),
        "L1_w2": again(a["L1_ffn_w2"]),
        "sa_w": again(a["L1_xattn_sa_w"]),
        "ca_w": a["L1_xattn_ca_w"],
        "sa_rows": again(np.stack([a["L1_xattn_sa_b"][:, 2], a["L1_xattn_sa_b"][:, 3], g[:, 0], b[:, 0]], 1)),
        "ca_rows": np.stack([a["L1_xattn_ca_b"][:, 2], a["L1_xattn_ca_b"][:, 3], g[:, 1], b[:, 1]], 1),
        "mlp_rows": np.stack([a["L1_xattn_b2"], g[:, 2], b[:, 2]], 1),
        "w_gate": a["L2_ffn_w_gate"].T, "w_up": a["L2_ffn_w_up"].T, "w_down": a["L2_ffn_w_down"].T,
        "L3_attn_W_dx": a["L3_attn_W_dx"][:D], "L3_attn_W_x": a["L3_attn_W_x"][:D],
        "L3_attn_W_dx_pe": a["L3_attn_W_dx"][D:], "L3_attn_W_x_pe": a["L3_attn_W_x"][D:],
        "L3_xattn_Wq": a["L3_xattn_Wq"], "L3_xattn_Wk": a["L3_xattn_Wkv"][:D],
        "L3_xattn_Wv": a["L3_xattn_Wkv"][D:].T, "L3_xattn_Wproj": a["L3_xattn_Wproj"].T,
    }
    for i, n in enumerate(("Wq", "Wk", "Wv")):
        out[f"L1_attn_{n}"] = a["L1_attn_Wqkv"][:, i * D:(i + 1) * D]
    for n in ("mask_BxSxS_ik0", "mask_BxS2_if0", "L0_xattn_Wq1", "L0_xattn_Wk1", "L0_xattn_Wv1", "L0_xattn_Wk2", "L0_xattn_Wv2", "L0_xattn_Wo",
              "L1_xattn_w1", "L1_xattn_w2", "L1_attn_Wo", "L1_ffn_mix_w", "L2_attn_proj_mat", "L3_attn_W_gx", "L3_attn_W_ga", "L3_attn_W_o"):
        out[n] = a[n]
    for block, names in (("L0_attn", "Wq Wk Wv Wg"), ("L2_xattn", "Wq Wk Wv Wo"), ("L2_attn", "Wq Wk Wv Wo"), ("L3_ffn", "Wq Wk Wv Wp")):
        for n in names.split():
            out[f"{block}_{n}"] = a[f"{block}_{n}"].T
    return {k: f(v) for k, v in out.items()}


COL_NAMES_DIRECT = [n for n, _ in COLS if n[:2] in ("L0", "L2", "L3") and "_b1_" not in n]


def kernel(**inputs):
    import concourse.bacc as bacc
    from concourse.bass_utils import run_bass_kernel_spmd

    arrays = arrays_of(inputs)
    nc = bacc.Bacc("TRN2", target_bir_lowering=False, num_devices=1)
    A = {k: nc.dram_tensor(f"in_{k}", v.shape, mybir.dt.from_np(v.dtype), kind="ExternalInput").ap() for k, v in arrays.items()}
    A["out"] = nc.dram_tensor("out", (NB * LQ, D), F32, kind="ExternalOutput").ap()
    build(nc, A)
    r = run_bass_kernel_spmd(nc, [{f"in_{k}": v for k, v in arrays.items()}], core_ids=[0])
    return r.results[0]["out"].reshape(NB, LQ, D)
```
